# Optimizing a Trainium2 kernel written in Bass

```python
import numpy as np
import jax
import jax.numpy as jnp

def _softmax(x, axis=-1):
    return jax.nn.softmax(x, axis=axis)

def _gelu(x):
    return jax.nn.gelu(x, approximate=True)

def _silu(x):
    return jax.nn.silu(x)

def _sigmoid(x):
    return jax.nn.sigmoid(x)

def _layernorm(x, axis=-1, eps=1e-05):
    m = jnp.mean(x, axis=axis, keepdims=True)
    v = jnp.var(x, axis=axis, keepdims=True)
    return (x - m) / jnp.sqrt(v + eps)

def _scatter_add(tgt, idx, src, axis=0):
    return tgt.at[idx].add(src)

def _segment_sum(src, seg, n):
    return jax.ops.segment_sum(src, seg, n)
kernel_name = 'mk_audio_tower_d2_tok_aud1d256_r4_918fa2'

def setup_inputs(seed: int=0):
    np.random.seed(seed)
    _w = jnp.asarray

    def _rec_inputs():
        import jax
        import jax.numpy as jnp
        _rk = jax.random.key(seed)
        x = -0.000292821 + 1.00034 * jax.random.normal(jax.random.fold_in(_rk, 1), (128, 8192), jnp.float32)
        return x
    x = _rec_inputs()

    def _L0_tok_setup():
        import jax, jax.numpy as jnp
        import numpy as np
        EPS = 1e-05

        def _conv1d(x, W, b, stride, pad):
            y = jax.lax.conv_general_dilated(x, W, (stride,), [(pad, pad)], dimension_numbers=('NCH', 'OIH', 'NCH'))
            return y + b[None, :, None]

        def _bn(x, g, b, m, v):
            return (x - m[None, :, None]) * (g * jax.lax.rsqrt(v + EPS))[None, :, None] + b[None, :, None]

        def _maxpool(x, k):
            B, C, L = x.shape
            return x.reshape(B, C, L // k, k).max(axis=-1)

        def _self_attn(x, Wq, bq, Wk, bk, Wv, bv, gamma):
            q = jnp.einsum('oc,bcl->bol', Wq, x) + bq[None, :, None]
            k = jnp.einsum('oc,bcl->bol', Wk, x) + bk[None, :, None]
            v = jnp.einsum('oc,bcl->bol', Wv, x) + bv[None, :, None]
            energy = jnp.einsum('bci,bcj->bij', q, k)
            attn = jax.nn.softmax(energy, axis=-1)
            out = jnp.einsum('bcj,bij->bci', v, attn)
            return gamma * out + x
        key = jax.random.key(seed)
        ks = jax.random.split(key, 32)
        B, D = (128, 8192)
        r = lambda i, shape, s=0.1: jax.random.normal(ks[i], shape, jnp.float32) * s
        return {'x': jax.random.normal(ks[0], (B, D), jnp.float32), 'w1': r(1, (16, 2, 3)), 'b1': r(2, (16,)), 'g1': 1.0 + r(3, (16,)), 'be1': r(4, (16,)), 'm1': r(5, (16,)), 'v1': 0.5 + jax.random.uniform(ks[6], (16,), jnp.float32), 'w2': r(7, (64, 16, 3)), 'b2': r(8, (64,)), 'g2': 1.0 + r(9, (64,)), 'be2': r(10, (64,)), 'm2': r(11, (64,)), 'v2': 0.5 + jax.random.uniform(ks[12], (64,), jnp.float32), 'wq': r(13, (8, 64)), 'bq': r(14, (8,)), 'wk': r(15, (8, 64)), 'bk': r(16, (8,)), 'wv': r(17, (64, 64)), 'bv': r(18, (64,)), 'gamma': jnp.float32(0.7), 'w3': r(19, (128, 64, 4)), 'b3': r(20, (128,)), 'g3': 1.0 + r(21, (128,)), 'be3': r(22, (128,)), 'm3': r(23, (128,)), 'v3': 0.5 + jax.random.uniform(ks[24], (128,), jnp.float32)}
    _L0_tok_all = _L0_tok_setup()
    _L0_tok_in = {k: v for k, v in _L0_tok_all.items() if k in ('w1', 'b1', 'g1', 'be1', 'm1', 'v1', 'w2', 'b2', 'g2', 'be2', 'm2', 'v2', 'wq', 'bq', 'wk', 'bk', 'wv', 'bv', 'gamma', 'w3', 'b3', 'g3', 'be3', 'm3', 'v3')}
    del _L0_tok_all

    def _L0_attn_setup():
        import jax, jax.numpy as jnp
        import numpy as np
        D_MODEL = 64
        N_HEAD = 8

        def _l1_scores(q, k):
            scale = 1.0 / np.sqrt(q.shape[-1]).astype(np.float32)
            q_sbhw = q.transpose(1, 0, 2, 3)

            def one_query(qs):
                return -jnp.sum(jnp.abs(qs[:, None, :, :] - k), axis=-1) * scale
            s = jax.lax.map(one_query, q_sbhw)
            return s.transpose(1, 0, 2, 3)
        key = jax.random.key(seed)
        ks = jax.random.split(key, 3)
        b, t = (4, 250)
        x = jax.random.normal(ks[0], (b, t, D_MODEL), jnp.float32)
        wqv_w = 0.005 * jax.random.normal(ks[1], (3 * N_HEAD * D_MODEL, D_MODEL), jnp.float32)
        wqv_b = jnp.zeros((3 * N_HEAD * D_MODEL,), jnp.float32)
        wk = 0.005 * jnp.ones((N_HEAD, D_MODEL), jnp.float32)
        fanin_w = 0.005 * jax.random.normal(ks[2], (D_MODEL, D_MODEL), jnp.float32)
        fanin_b = jnp.zeros((D_MODEL,), jnp.float32)
        return dict(x=x, wqv_w=wqv_w, wqv_b=wqv_b, wk=wk, fanin_w=fanin_w, fanin_b=fanin_b)
    _L0_attn_all = _L0_attn_setup()
    _L0_attn_in = {k: v for k, v in _L0_attn_all.items() if k in ('wqv_w', 'wqv_b', 'wk', 'fanin_w', 'fanin_b')}
    del _L0_attn_all

    def _L0_ffn_setup():
        import jax, jax.numpy as jnp
        import numpy as np
        B, T, IN_DIM = (64, 64, 64)
        HID, OUT_DIM = (128, 64)
        N_LAYERS, N_EXPERTS, N_SHARED = (2, 16, 1)
        key = jax.random.key(seed)
        ks = jax.random.split(key, 10)
        s = 0.02
        x = jax.random.normal(ks[0], (B, T, IN_DIM), dtype=jnp.float32)
        route_id = jax.random.randint(ks[1], (B,), 0, N_EXPERTS)
        Wi = jax.random.normal(ks[2], (HID, IN_DIM), dtype=jnp.float32) * s
        bi = jnp.zeros((HID,), dtype=jnp.float32)
        Wr = jax.random.normal(ks[3], (N_LAYERS, N_EXPERTS, HID, HID), dtype=jnp.float32) * s
        br = jax.random.normal(ks[4], (N_LAYERS, N_EXPERTS, HID), dtype=jnp.float32) * s
        Ws = jax.random.normal(ks[5], (N_LAYERS, N_SHARED, HID, HID), dtype=jnp.float32) * s
        bs = jax.random.normal(ks[6], (N_LAYERS, N_SHARED, HID), dtype=jnp.float32) * s
        Wo = jax.random.normal(ks[7], (OUT_DIM, HID), dtype=jnp.float32) * s
        bo = jnp.zeros((OUT_DIM,), dtype=jnp.float32)
        return {'x': x, 'route_id': route_id, 'Wi': Wi, 'bi': bi, 'Wr': Wr, 'br': br, 'Ws': Ws, 'bs': bs, 'Wo': Wo, 'bo': bo}
    _L0_ffn_all = _L0_ffn_setup()
    _L0_ffn_in = {k: v for k, v in _L0_ffn_all.items() if k in ('route_id', 'Wi', 'bi', 'Wr', 'br', 'Ws', 'bs', 'Wo', 'bo')}
    del _L0_ffn_all

    def _L1_attn_setup():
        import jax, jax.numpy as jnp
        import numpy as np
        key = jax.random.key(seed)
        ks = jax.random.split(key, 5)
        b, t, e, h = (8, 256, 64, 8)
        w = lambda k, shape: jax.random.normal(k, shape, dtype=jnp.float32) * 0.02
        return {'x': jax.random.normal(ks[0], (b, t, e), dtype=jnp.float32), 'Wq': w(ks[1], (e, e * h)), 'bq': jnp.zeros((e * h,), jnp.float32), 'Wk': w(ks[2], (e, e * h)), 'bk': jnp.zeros((e * h,), jnp.float32), 'Wv': w(ks[3], (e, e * h)), 'bv': jnp.zeros((e * h,), jnp.float32), 'Wu': w(ks[4], (e * h, e)), 'bu': jnp.zeros((e,), jnp.float32)}
    _L1_attn_all = _L1_attn_setup()
    _L1_attn_in = {k: v for k, v in _L1_attn_all.items() if k in ('Wq', 'bq', 'Wk', 'bk', 'Wv', 'bv', 'Wu', 'bu')}
    del _L1_attn_all

    def _L1_ffn_setup():
        import jax, jax.numpy as jnp
        import numpy as np
        NUM_EXPERTS = 8
        TOP_K = 2
        B, S, D = (8, 2048, 64)

        def _moe(tokens, router_w, w1, b1, w2, b2):
            N = tokens.shape[0]
            E = router_w.shape[0]
            logits = tokens.astype(jnp.float32) @ router_w.astype(jnp.float32).T
            probs = jax.nn.softmax(logits, axis=-1)
            rw, re = jax.lax.top_k(probs, TOP_K)
            if TOP_K > 1:
                rw = rw / jnp.maximum(rw.sum(-1, keepdims=True), 1e-12)
            rw = rw.astype(tokens.dtype)
            combine = jnp.zeros((N, E), tokens.dtype).at[jnp.arange(N)[:, None], re].set(rw)
            out = tokens
            for e in range(E):
                h = jax.nn.gelu(tokens @ w1[e] + b1[e], approximate=False)
                y = h @ w2[e] + b2[e]
                out = out + combine[:, e:e + 1] * y
            return out
        key = jax.random.key(seed)
        ks = jax.random.split(key, 4)
        scale = 1.0 / np.sqrt(D).astype(np.float32)
        return {'input_embeddings': jax.random.normal(ks[0], (B, S, D), jnp.float32), 'router_w': jax.random.normal(ks[1], (NUM_EXPERTS, D), jnp.float32) * scale, 'w1': jax.random.normal(ks[2], (NUM_EXPERTS, D, D), jnp.float32) * scale, 'b1': jnp.zeros((NUM_EXPERTS, D), jnp.float32), 'w2': jax.random.normal(ks[3], (NUM_EXPERTS, D, D), jnp.float32) * scale, 'b2': jnp.zeros((NUM_EXPERTS, D), jnp.float32)}
    _L1_ffn_all = _L1_ffn_setup()
    _L1_ffn_in = {k: v for k, v in _L1_ffn_all.items() if k in ('router_w', 'w1', 'b1', 'w2', 'b2')}
    del _L1_ffn_all
    return {'x': x, 'L0_tok_w1': _L0_tok_in['w1'], 'L0_tok_b1': _L0_tok_in['b1'], 'L0_tok_g1': _L0_tok_in['g1'], 'L0_tok_be1': _L0_tok_in['be1'], 'L0_tok_m1': _L0_tok_in['m1'], 'L0_tok_v1': _L0_tok_in['v1'], 'L0_tok_w2': _L0_tok_in['w2'], 'L0_tok_b2': _L0_tok_in['b2'], 'L0_tok_g2': _L0_tok_in['g2'], 'L0_tok_be2': _L0_tok_in['be2'], 'L0_tok_m2': _L0_tok_in['m2'], 'L0_tok_v2': _L0_tok_in['v2'], 'L0_tok_wq': _L0_tok_in['wq'], 'L0_tok_bq': _L0_tok_in['bq'], 'L0_tok_wk': _L0_tok_in['wk'], 'L0_tok_bk': _L0_tok_in['bk'], 'L0_tok_wv': _L0_tok_in['wv'], 'L0_tok_bv': _L0_tok_in['bv'], 'L0_tok_gamma': _L0_tok_in['gamma'], 'L0_tok_w3': _L0_tok_in['w3'], 'L0_tok_b3': _L0_tok_in['b3'], 'L0_tok_g3': _L0_tok_in['g3'], 'L0_tok_be3': _L0_tok_in['be3'], 'L0_tok_m3': _L0_tok_in['m3'], 'L0_tok_v3': _L0_tok_in['v3'], 'L0_attn_wqv_w': _L0_attn_in['wqv_w'], 'L0_attn_wqv_b': _L0_attn_in['wqv_b'], 'L0_attn_wk': _L0_attn_in['wk'], 'L0_attn_fanin_w': _L0_attn_in['fanin_w'], 'L0_attn_fanin_b': _L0_attn_in['fanin_b'], 'L0_ffn_route_id': _L0_ffn_in['route_id'], 'L0_ffn_Wi': _L0_ffn_in['Wi'], 'L0_ffn_bi': _L0_ffn_in['bi'], 'L0_ffn_Wr': _L0_ffn_in['Wr'], 'L0_ffn_br': _L0_ffn_in['br'], 'L0_ffn_Ws': _L0_ffn_in['Ws'], 'L0_ffn_bs': _L0_ffn_in['bs'], 'L0_ffn_Wo': _L0_ffn_in['Wo'], 'L0_ffn_bo': _L0_ffn_in['bo'], 'L1_attn_Wq': _L1_attn_in['Wq'], 'L1_attn_bq': _L1_attn_in['bq'], 'L1_attn_Wk': _L1_attn_in['Wk'], 'L1_attn_bk': _L1_attn_in['bk'], 'L1_attn_Wv': _L1_attn_in['Wv'], 'L1_attn_bv': _L1_attn_in['bv'], 'L1_attn_Wu': _L1_attn_in['Wu'], 'L1_attn_bu': _L1_attn_in['bu'], 'L1_ffn_router_w': _L1_ffn_in['router_w'], 'L1_ffn_w1': _L1_ffn_in['w1'], 'L1_ffn_b1': _L1_ffn_in['b1'], 'L1_ffn_w2': _L1_ffn_in['w2'], 'L1_ffn_b2': _L1_ffn_in['b2']}

def reference(x, L0_tok_w1, L0_tok_b1, L0_tok_g1, L0_tok_be1, L0_tok_m1, L0_tok_v1, L0_tok_w2, L0_tok_b2, L0_tok_g2, L0_tok_be2, L0_tok_m2, L0_tok_v2, L0_tok_wq, L0_tok_bq, L0_tok_wk, L0_tok_bk, L0_tok_wv, L0_tok_bv, L0_tok_gamma, L0_tok_w3, L0_tok_b3, L0_tok_g3, L0_tok_be3, L0_tok_m3, L0_tok_v3, L0_attn_wqv_w, L0_attn_wqv_b, L0_attn_wk, L0_attn_fanin_w, L0_attn_fanin_b, L0_ffn_route_id, L0_ffn_Wi, L0_ffn_bi, L0_ffn_Wr, L0_ffn_br, L0_ffn_Ws, L0_ffn_bs, L0_ffn_Wo, L0_ffn_bo, L1_attn_Wq, L1_attn_bq, L1_attn_Wk, L1_attn_bk, L1_attn_Wv, L1_attn_bv, L1_attn_Wu, L1_attn_bu, L1_ffn_router_w, L1_ffn_w1, L1_ffn_b1, L1_ffn_w2, L1_ffn_b2):
    import jax
    import jax.numpy as jnp

    def _L0_tok_ref(x, w1, b1, g1, be1, m1, v1, w2, b2, g2, be2, m2, v2, wq, bq, wk, bk, wv, bv, gamma, w3, b3, g3, be3, m3, v3):
        import jax, jax.numpy as jnp
        import numpy as np
        EPS = 1e-05

        def _conv1d(x, W, b, stride, pad):
            y = jax.lax.conv_general_dilated(x, W, (stride,), [(pad, pad)], dimension_numbers=('NCH', 'OIH', 'NCH'))
            return y + b[None, :, None]

        def _bn(x, g, b, m, v):
            return (x - m[None, :, None]) * (g * jax.lax.rsqrt(v + EPS))[None, :, None] + b[None, :, None]

        def _maxpool(x, k):
            B, C, L = x.shape
            return x.reshape(B, C, L // k, k).max(axis=-1)

        def _self_attn(x, Wq, bq, Wk, bk, Wv, bv, gamma):
            q = jnp.einsum('oc,bcl->bol', Wq, x) + bq[None, :, None]
            k = jnp.einsum('oc,bcl->bol', Wk, x) + bk[None, :, None]
            v = jnp.einsum('oc,bcl->bol', Wv, x) + bv[None, :, None]
            energy = jnp.einsum('bci,bcj->bij', q, k)
            attn = jax.nn.softmax(energy, axis=-1)
            out = jnp.einsum('bcj,bij->bci', v, attn)
            return gamma * out + x
        B, D = x.shape
        emb_sample, emb_task = (x[:, :D // 2], x[:, D // 2:])
        h = jnp.stack([emb_sample, emb_task], axis=1)
        h = _maxpool(jax.nn.relu(_bn(_conv1d(h, w1, b1, 1, 1), g1, be1, m1, v1)), 8)
        h = _maxpool(jax.nn.relu(_bn(_conv1d(h, w2, b2, 1, 1), g2, be2, m2, v2)), 4)
        h = _self_attn(h, wq, bq, wk, bk, wv, bv, gamma)
        h = _bn(_conv1d(h, w3, b3, 2, 1), g3, be3, m3, v3)
        return h

    def _L0_attn_ref(x, wqv_w, wqv_b, wk, fanin_w, fanin_b):
        import jax, jax.numpy as jnp
        import numpy as np
        D_MODEL = 64
        N_HEAD = 8

        def _l1_scores(q, k):
            scale = 1.0 / np.sqrt(q.shape[-1]).astype(np.float32)
            q_sbhw = q.transpose(1, 0, 2, 3)

            def one_query(qs):
                return -jnp.sum(jnp.abs(qs[:, None, :, :] - k), axis=-1) * scale
            s = jax.lax.map(one_query, q_sbhw)
            return s.transpose(1, 0, 2, 3)
        b, t, d = x.shape
        h = N_HEAD
        v = (x @ wqv_w.T + wqv_b).reshape(b, t, 3 * h, d)
        q, vf, vb = (v[:, :, :h], v[:, :, h:2 * h], v[:, :, 2 * h:])
        k = x[:, :, None, :] * wk[None, None]
        a = _l1_scores(q, k)
        a = jnp.concatenate([a, jnp.zeros((b, 1, t, h), a.dtype)], axis=1)
        a = jax.nn.softmax(a, axis=1)[:, :t]
        bf = jnp.einsum('bsdh,bshw->bdhw', a, vf)
        bb = jnp.einsum('bdsh,bshw->bdhw', a, vb)
        o = (bf + bb).sum(axis=2).reshape(b, t, d)
        y = o * jax.nn.sigmoid(1.702 * o)
        y = y @ fanin_w.T + fanin_b
        return x + y

    def _L0_ffn_ref(x, route_id, Wi, bi, Wr, br, Ws, bs, Wo, bo):
        import jax, jax.numpy as jnp
        import numpy as np
        B, T, IN_DIM = (64, 64, 64)
        HID, OUT_DIM = (128, 64)
        N_LAYERS, N_EXPERTS, N_SHARED = (2, 16, 1)
        flat = x.reshape(-1, x.shape[-1])
        n_tok = flat.shape[0]
        route = jnp.repeat(route_id, n_tok // route_id.shape[0])
        h = jax.nn.relu(flat @ Wi.T + bi)
        n_layers, n_experts = (Wr.shape[0], Wr.shape[1])
        for l in range(n_layers):
            shared = (jnp.einsum('nd,shd->snh', h, Ws[l]) + bs[l][:, None, :]).mean(axis=0)
            routed = jnp.zeros_like(h)
            for e in range(n_experts):
                ye = h @ Wr[l, e].T + br[l, e]
                routed = routed + jnp.where((route == e)[:, None], ye, 0.0)
            h = jax.nn.relu(shared + routed + h)
        out = h @ Wo.T + bo
        return out.reshape(*x.shape[:-1], out.shape[-1])

    def _L1_attn_ref(x, Wq, bq, Wk, bk, Wv, bv, Wu, bu):
        import jax, jax.numpy as jnp
        import numpy as np
        b, t, e = x.shape
        h = Wq.shape[1] // e
        q = (x @ Wq + bq).reshape(b, t, h, e)
        k = (x @ Wk + bk).reshape(b, t, h, e)
        v = (x @ Wv + bv).reshape(b, t, h, e)
        scores = jnp.einsum('bihe,bjhe->bhij', q, k) / jnp.sqrt(jnp.asarray(e, jnp.float32))
        i = jnp.arange(t)[:, None]
        j = jnp.arange(t)[None, :]
        scores = jnp.where(j >= i, -jnp.inf, scores)
        scores = jnp.where(i == 0, 0.0, scores)
        att = jax.nn.softmax(scores, axis=-1)
        att = jnp.where(i == 0, 0.0, att)
        out = jnp.einsum('bhij,bjhe->bihe', att, v).reshape(b, t, h * e)
        return out @ Wu + bu

    def _L1_ffn_ref(input_embeddings, router_w, w1, b1, w2, b2):
        import jax, jax.numpy as jnp
        import numpy as np
        NUM_EXPERTS = 8
        TOP_K = 2
        B, S, D = (8, 2048, 64)

        def _moe(tokens, router_w, w1, b1, w2, b2):
            N = tokens.shape[0]
            E = router_w.shape[0]
            logits = tokens.astype(jnp.float32) @ router_w.astype(jnp.float32).T
            probs = jax.nn.softmax(logits, axis=-1)
            rw, re = jax.lax.top_k(probs, TOP_K)
            if TOP_K > 1:
                rw = rw / jnp.maximum(rw.sum(-1, keepdims=True), 1e-12)
            rw = rw.astype(tokens.dtype)
            combine = jnp.zeros((N, E), tokens.dtype).at[jnp.arange(N)[:, None], re].set(rw)
            out = tokens
            for e in range(E):
                h = jax.nn.gelu(tokens @ w1[e] + b1[e], approximate=False)
                y = h @ w2[e] + b2[e]
                out = out + combine[:, e:e + 1] * y
            return out
        b, s, d = input_embeddings.shape
        tokens = input_embeddings.reshape(b * s, d)
        return _moe(tokens, router_w, w1, b1, w2, b2).reshape(b, s, d)
    h = _L0_tok_ref(x, L0_tok_w1, L0_tok_b1, L0_tok_g1, L0_tok_be1, L0_tok_m1, L0_tok_v1, L0_tok_w2, L0_tok_b2, L0_tok_g2, L0_tok_be2, L0_tok_m2, L0_tok_v2, L0_tok_wq, L0_tok_bq, L0_tok_wk, L0_tok_bk, L0_tok_wv, L0_tok_bv, L0_tok_gamma, L0_tok_w3, L0_tok_b3, L0_tok_g3, L0_tok_be3, L0_tok_m3, L0_tok_v3)
    h = h + _L0_attn_ref(_layernorm(h, axis=-1), L0_attn_wqv_w, L0_attn_wqv_b, L0_attn_wk, L0_attn_fanin_w, L0_attn_fanin_b)
    h = h + _L0_ffn_ref(_layernorm(h, axis=-1), L0_ffn_route_id, L0_ffn_Wi, L0_ffn_bi, L0_ffn_Wr, L0_ffn_br, L0_ffn_Ws, L0_ffn_bs, L0_ffn_Wo, L0_ffn_bo)
    h = h + _L1_attn_ref(_layernorm(h, axis=-1), L1_attn_Wq, L1_attn_bq, L1_attn_Wk, L1_attn_bk, L1_attn_Wv, L1_attn_bv, L1_attn_Wu, L1_attn_bu)
    h = h + _L1_ffn_ref(_layernorm(h, axis=-1), L1_ffn_router_w, L1_ffn_w1, L1_ffn_b1, L1_ffn_w2, L1_ffn_b2)
    return h

_drawn_inputs = setup_inputs


def setup_inputs(seed=0):
    import zlib

    import numpy as np

    out = dict(_drawn_inputs(seed))
    spreads = {'L0_attn_wqv_b': (0.0, 0.751),
     'L0_attn_wk': (0.004999999888241291, 0.6),
     'L0_attn_fanin_b': (0.0, 0.1),
     'L0_ffn_bi': (0.0, 0.322),
     'L0_ffn_bo': (0.0, 0.1),
     'L1_attn_bq': (0.0, 0.8),
     'L1_attn_bk': (0.0, 0.8),
     'L1_attn_bv': (0.0, 0.1),
     'L1_attn_bu': (0.0, 0.1),
     'L1_ffn_b1': (0.0, 0.377),
     'L1_ffn_b2': (0.0, 0.1)}
    factors = {'L0_tok_wq': 8.0,
     'L0_tok_bq': 8.0,
     'L0_tok_wk': 8.0,
     'L0_tok_bk': 8.0,
     'L0_attn_wqv_w': 8.0,
     'L0_attn_fanin_w': 4.936,
     'L0_ffn_Wr': 4.262,
     'L0_ffn_br': 5.478,
     'L0_ffn_Ws': 4.115,
     'L0_ffn_bs': 5.036,
     'L1_attn_Wq': 8.0,
     'L1_attn_Wk': 8.0}
    for name, (base, spread) in spreads.items():
        noise = np.random.default_rng([zlib.crc32(name.encode()), seed]).standard_normal(out[name].shape)
        drawn = base * np.exp(spread * noise) if base else spread * noise
        out[name] = jnp.asarray(drawn.astype(out[name].dtype))
    for name, factor in factors.items():
        out[name] = (out[name] * factor).astype(out[name].dtype)
    return out
```

```python
from collections import namedtuple
from contextlib import ExitStack

import concourse.bass as bass
from concourse import mybir

F32 = mybir.dt.float32
I32 = mybir.dt.int32
ALU = mybir.AluOpType
ACT = mybir.ActivationFunctionType
AX = mybir.AxisListType

P = 128
SAMPLES = 128
PAIRS = SAMPLES // 2
TOK = 128
D = 64
HEADS = 8
HID = 128
LAYERS = 2
ROUTES = 16
EXPERTS = 8
GROUP = 8
GROUPS = SAMPLES // GROUP
GP = GROUP // 2
LEN = 4096
POOL1 = 8
POOL2 = 4
L1_LEN = LEN // POOL1
L2_LEN = L1_LEN // POOL2
EPS = 1e-5


def named(**things):
    return namedtuple("Named", list(things))(**things)


class Part:

    def __init__(self, nc, ctx, name):
        self.nc, self.ctx, self.name, self.mine = nc, ctx, name, []

    def sb(self, name, shape, dt=F32):
        return self.ctx.enter_context(self.nc.sbuf_tensor(f"{self.name}_{name}", shape, dt))

    def sem(self, name):
        s = self.ctx.enter_context(self.nc.semaphore(f"{self.name}_{name}"))
        self.mine.append(s)
        return s

    def sems(self, names):
        return named(**{n: self.sem(n) for n in names.split()})

    def end(self):
        with self.nc.Block() as block:
            @block.sync
            def _(sp):
                for s in self.mine:
                    sp.sem_clear(s)


def spread(ap, axis, size):
    a = ap.unsqueeze(axis)
    shape = list(a.shape)
    shape[axis] = size
    return a.broadcast_to(shape)


def layer_norm_start(dve, nc, n, src, b, s):
    nc.vector.tensor_reduce(b.sum[:], src, AX.X, ALU.add).then_inc(s.ln_sum, 1)
    dve.wait_ge(s.ln_sum, n + 1)
    nc.vector.scalar_tensor_tensor(out=b.xc[:], in0=spread(b.sum[:], 2, D), scalar=-1.0 / D, in1=src,
                                   op0=ALU.mult, op1=ALU.add).then_inc(s.ln_centred, 1)
    dve.wait_ge(s.ln_centred, n + 1)
    nc.vector.tensor_tensor(b.sq[:], b.xc[:], b.xc[:], ALU.mult).then_inc(s.ln_squared, 1)
    dve.wait_ge(s.ln_squared, n + 1)
    nc.vector.tensor_reduce(b.var[:], b.sq[:], AX.X, ALU.add).then_inc(s.ln_sumsq, 1)
    dve.wait_ge(s.ln_sumsq, n + 1)
    nc.vector.tensor_scalar(b.var[:], b.var[:], 1.0 / D, EPS, ALU.mult, ALU.add).then_inc(s.ln_var, 1)


def layer_norm_end(dve, nc, n, b, s):
    dve.wait_ge(s.ln_root, n + 1)
    nc.vector.tensor_tensor(b.xn[:], b.xc[:], spread(b.rstd[:], 2, D), ALU.mult).then_inc(s.ln_done, 1)


def layer_norm_root(pool, nc, n, b, s):
    pool.wait_ge(s.ln_var, n + 1)
    nc.gpsimd.tensor_tensor(b.rstd[:], b.var[:], b.minus_half[:], ALU.pow).then_inc(s.ln_root, 1)


LN_SEMS = "ln_sum ln_centred ln_squared ln_sumsq ln_var ln_root ln_done half_set "


def layer_norm_buffers(part, ns):
    return named(sum=part.sb("ln_sum", [P, ns]), var=part.sb("ln_var", [P, ns]),
                           rstd=part.sb("ln_rstd", [P, ns]), minus_half=part.sb("ln_minus_half", [P, ns]),
                           xc=part.sb("ln_xc", [P, ns, D]), sq=part.sb("ln_sq", [P, ns, D]),
                           xn=part.sb("ln_xn", [P, ns, D]))


def tokenise(nc, A, h, PS):
    with ExitStack() as ctx:
        p = Part(nc, ctx, "tok")
        w1 = p.sb("w1", [48, P])
        w2 = p.sb("w2", [P, 3 * GP, P])
        w3 = p.sb("w3", [P, 4, P])
        wq = p.sb("wq", [P, 40])
        wk = p.sb("wk", [P, 40])
        wv = p.sb("wv", [P, P])
        bqk = p.sb("bqk", [40, 2])
        bv = p.sb("bv", [P, P])
        gamma = p.sb("gamma", [P, 1])
        ident = p.sb("ident", [P, P])
        cols = p.sb("cols", [P, 5, 3])
        scale = p.sb("scale", [P, 3])
        veps = p.sb("veps", [P, 3])
        root = p.sb("root", [P, 3])
        half3 = p.sb("half3", [P, 3])
        shift = p.sb("shift", [P, 3])
        warm = p.sb("warm", [P, 1])
        xin = p.sb("xin", [48, 2, LEN])
        h1raw = p.sb("h1raw", [P, L1_LEN])
        h1 = p.sb("h1", [P, L1_LEN + 2])
        h2raw = p.sb("h2raw", [P, GP, L2_LEN])
        h2 = p.sb("h2", [P, GP, L2_LEN])
        q = p.sb("q", [40, GP, L2_LEN])
        k = p.sb("k", [40, GP, L2_LEN])
        vT = p.sb("vT", [P, GP, P])
        prob = p.sb("prob", [P, 2 * GP, L2_LEN])
        probT = p.sb("probT", [P, 2 * GP, L2_LEN])
        nmax = p.sb("nmax", [P, 2 * GP])
        total = p.sb("total", [P, 2 * GP])
        h3 = p.sb("h3", [P, GP, L2_LEN + 2])
        s = p.sems("weights half_set veps root scale rows folded shift0 shift edges_a edges_b warm "
                   "h1 h2 qk_psum q k e v_psum v nmax shifted exp total recip norm pT probT out h3 c3 done c1_used")
        x_in = [p.sem(f"x_in{j}") for j in range(2)]
        x_used = [p.sem(f"x_used{j}") for j in range(2)]
        conv1 = [p.sem(f"conv1_{j}") for j in range(2)]
        pool1 = [p.sem(f"pool1_{j}") for j in range(2)]
        conv2 = [p.sem(f"conv2_{j}") for j in range(2)]
        pool2 = [p.sem(f"pool2_{j}") for j in range(2)]
        loads = [(w1[:], A.c1_w), (w2[:], A.c2_w), (w3[:], A.c3_w), (wq[:], A.tok_wq), (wk[:], A.tok_wk),
                 (wv[:], A.tok_wv), (bqk[:], A.tok_bqk), (bv[:], A.tok_bv), (gamma[:], A.gamma),
                 (ident[:], A.ident), (cols[:], A.norm_cols)]
        TURNS = GROUPS // 2
        CH = LEN // 512

        with nc.Block() as block:
            @block.sync
            def _(sp):
                for dst, src in loads:
                    sp.dma_start(dst, src).then_inc(s.weights, 16)
                sp.wait_ge(s.edges_a, 1)
                with sp.Fori(0, TURNS) as i:
                    for j in range(2):
                        n = 2 * i + j
                        sp.wait_ge(x_used[j], i)
                        rows = A.x_rows[bass.ds(n * 16, 16), :]
                        sp.dma_start(xin[0:16, j, 1:LEN], rows[:, 0:LEN - 1]).then_inc(x_in[j], 16)
                        sp.dma_start(xin[16:32, j, :], rows).then_inc(x_in[j], 16)
                        sp.dma_start(xin[32:48, j, 0:LEN - 1], rows[:, 1:LEN]).then_inc(x_in[j], 16)

            @block.gpsimd
            def _(pool):
                nc.gpsimd.memset(half3[:], -0.5).then_inc(s.half_set, 1)
                nc.gpsimd.memset(h1[:], 0.0).then_inc(s.edges_b, 1)
                nc.gpsimd.memset(h3[:], 0.0).then_inc(s.edges_b, 1)
                pool.wait_ge(s.half_set, 1)
                pool.wait_ge(s.veps, 1)
                nc.gpsimd.tensor_tensor(root[:], veps[:], half3[:], ALU.pow).then_inc(s.root, 1)

            @block.vector
            def _(dve):
                nc.vector.memset(xin[:, :, 0:1], 0.0)
                nc.vector.memset(xin[:, :, LEN - 1:LEN], 0.0).then_inc(s.edges_a, 1)
                dve.wait_ge(s.weights, 16 * len(loads))
                nc.vector.tensor_scalar(veps[:], cols[:, 4, :], EPS, None, ALU.add).then_inc(s.veps, 1)
                dve.wait_ge(s.root, 1)
                nc.vector.tensor_tensor(scale[:], cols[:, 1, :], root[:], ALU.mult).then_inc(s.scale, 1)
                dve.wait_ge(s.scale, 1)
                nc.vector.tensor_tensor(shift[:], cols[:, 0, :], cols[:, 3, :], ALU.subtract).then_inc(s.shift0, 1)
                dve.wait_ge(s.shift0, 1)
                nc.vector.tensor_tensor(shift[:], shift[:], scale[:], ALU.mult).then_inc(s.shift0, 1)
                dve.wait_ge(s.shift0, 2)
                nc.vector.tensor_tensor(shift[:], shift[:], cols[:, 2, :], ALU.add).then_inc(s.shift, 1)
                dve.wait_ge(s.rows, 1)
                nc.vector.tensor_tensor(w1[:], w1[:], PS[0:48, 0, 0:P], ALU.mult).then_inc(s.folded, 1)
                nc.vector.tensor_tensor(w2[:], w2[:], spread(PS[:, 1, 0:P], 1, 3 * GP), ALU.mult).then_inc(s.folded, 1)
                nc.vector.tensor_tensor(w3[:], w3[:], spread(PS[:, 2, 0:P], 1, 4), ALU.mult).then_inc(s.folded, 1)
                with dve.Fori(0, TURNS) as i:
                    for j in range(2):
                        n = 2 * i + j
                        for c in range(CH):
                            dve.wait_ge(conv1[c % 2], n * (CH // 2) + c // 2 + 1)
                            if c == 0:
                                dve.wait_ge(s.h1, n)
                            nc.vector.tensor_reduce(
                                h1raw[:, c * 64:(c + 1) * 64], PS[:, c % 2, :].rearrange("p (a b) -> p a b", b=POOL1),
                                AX.X, ALU.max).then_inc(pool1[c % 2], 1)
                        for g in range(GP):
                            dve.wait_ge(conv2[g % 2], n * (GP // 2) + g // 2 + 1)
                            if g == 0:
                                dve.wait_ge(s.h2, n)
                            nc.vector.tensor_reduce(
                                h2raw[:, g, :], PS[:, 2 + g % 2, :].rearrange("p (a b) -> p a b", b=POOL2),
                                AX.X, ALU.max).then_inc(pool2[g % 2], 1)
                        dve.wait_ge(s.qk_psum, n + 1)
                        nc.vector.tensor_scalar(k[:].rearrange("p a b -> p (a b)"), PS[0:40, 5, :], bqk[:, 1:2], None,
                                                ALU.add).then_inc(s.k, 1)
                        dve.wait_ge(s.v_psum, n + 1)
                        nc.vector.tensor_tensor(vT[:], PS[:, 4, :].rearrange("p (a b) -> p a b", a=GP),
                                                spread(bv[:], 1, GP), ALU.add).then_inc(s.v, 1)
                        dve.wait_ge(s.e, n + 1)
                        energy = PS[:, 6:8, :].rearrange("p a (b c) -> p (a b) c", b=GP)
                        nc.vector.tensor_reduce(nmax[:], energy, AX.X, ALU.max, negate=True).then_inc(s.nmax, 1)
                        dve.wait_ge(s.nmax, n + 1)
                        nc.vector.tensor_tensor(prob[:], energy, spread(nmax[:], 2, L2_LEN), ALU.add)\
                            .then_inc(s.shifted, 1)
                        dve.wait_ge(s.exp, n + 1)
                        nc.vector.tensor_reduce(total[:], prob[:], AX.X, ALU.add).then_inc(s.total, 1)
                        dve.wait_ge(s.total, n + 1)
                        nc.vector.reciprocal(total[:], total[:]).then_inc(s.recip, 1)
                        dve.wait_ge(s.recip, n + 1)
                        nc.vector.tensor_tensor(prob[:], prob[:], spread(total[:], 2, L2_LEN), ALU.mult)\
                            .then_inc(s.norm, 1)
                        dve.wait_ge(s.out, n + 1)
                        nc.vector.scalar_tensor_tensor(
                            out=h3[:, :, 1:L2_LEN + 1], in0=PS[:, 5, :].rearrange("p (a b) -> p a b", a=GP),
                            scalar=gamma[:, 0:1], in1=h2[:], op0=ALU.mult, op1=ALU.add).then_inc(s.h3, 1)

            @block.scalar
            def _(act):
                act.wait_ge(s.edges_b, 2)
                nc.scalar.activation(warm[:], h1[:, 0:1], ACT.Exp).then_inc(s.warm, 1)
                act.wait_ge(s.shift, 1)
                with act.Fori(0, TURNS) as i:
                    for j in range(2):
                        n = 2 * i + j
                        act.wait_ge(pool1[0], (n + 1) * (CH // 2))
                        act.wait_ge(pool1[1], (n + 1) * (CH // 2))
                        act.wait_ge(s.qk_psum, n)
                        nc.scalar.activation(h1[:, 1:L1_LEN + 1], h1raw[:], ACT.Relu, bias=shift[:, 0:1])\
                            .then_inc(s.h1, 1)
                        act.wait_ge(pool2[0], (n + 1) * (GP // 2))
                        act.wait_ge(pool2[1], (n + 1) * (GP // 2))
                        act.wait_ge(s.h3, n)
                        nc.scalar.activation(h2[:], h2raw[:], ACT.Relu, bias=shift[:, 1:2]).then_inc(s.h2, 1)
                        act.wait_ge(s.qk_psum, n + 1)
                        nc.scalar.activation(q[:].rearrange("p a b -> p (a b)"), PS[0:40, 4, :], ACT.Identity,
                                             bias=bqk[:, 0:1]).then_inc(s.q, 1)
                        act.wait_ge(s.shifted, n + 1)
                        nc.scalar.activation(prob[:], prob[:], ACT.Exp).then_inc(s.exp, 1)
                        act.wait_ge(s.pT, n + 1)
                        nc.scalar.activation(probT[:], PS[:, 6:8, :].rearrange("p a (b c) -> p (a b) c", b=GP),
                                             ACT.Copy).then_inc(s.probT, 1)
                        act.wait_ge(s.c3, n + 1)
                        hv = h[:, bass.ds(n * GROUP, GROUP), :].rearrange("p (g b) d -> p b g d", b=2)
                        nc.scalar.activation(hv, PS[:, 4:6, 0:256].rearrange("p b (g d) -> p b g d", g=GP),
                                             ACT.Identity, bias=shift[:, 2:3]).then_inc(s.done, 1)

            @block.tensor
            def _(pe):
                pe.wait_ge(s.weights, 16 * len(loads))
                pe.wait_ge(s.scale, 1)
                for m in range(3):
                    mm = nc.tensor.matmul(PS[:, m, 0:P], scale[:, m:m + 1].broadcast_to([P, P]), ident[:],
                                          start=True, stop=True)
                mm.then_inc(s.rows, 1)
                pe.wait_ge(s.folded, 3)
                pe.wait_ge(s.edges_b, 2)
                with pe.Fori(0, TURNS) as i:
                    for j in range(2):
                        n = 2 * i + j
                        pe.wait_ge(x_in[j], 48 * i + 48)
                        for c in range(CH):
                            pe.wait_ge(pool1[c % 2], n * (CH // 2) + c // 2)
                            mm = nc.tensor.matmul(PS[:, c % 2, :], w1[:], xin[:, j, c * 512:(c + 1) * 512],
                                                  start=True, stop=True)
                            mm.then_inc(conv1[c % 2], 1)
                        pe.wait_ge(pool1[(CH - 1) % 2], (n + 1) * (CH // 2))
                        pe.sem_inc(x_used[j], 1)
                        pe.wait_ge(s.h1, n + 1)
                        for g in range(GP):
                            pe.wait_ge(pool2[g % 2], n * (GP // 2) + g // 2)
                            for tap in range(3):
                                mm = nc.tensor.matmul(PS[:, 2 + g % 2, :], w2[:, tap * GP + g, :],
                                                      h1[:, tap:tap + L1_LEN], start=(tap == 0), stop=(tap == 2))
                            mm.then_inc(conv2[g % 2], 1)
                        pe.wait_ge(s.h2, n + 1)
                        pe.wait_ge(s.done, n)
                        h2f = h2[:].rearrange("p a b -> p (a b)")
                        nc.tensor.matmul(PS[0:40, 4, :], wq[:], h2f, start=True, stop=True)
                        nc.tensor.matmul(PS[0:40, 5, :], wk[:], h2f, start=True, stop=True).then_inc(s.qk_psum, 1)
                        pe.wait_ge(s.q, n + 1)
                        for g in range(GP):
                            mm = nc.tensor.matmul(PS[:, 4, g * P:(g + 1) * P], h2[:, g, :], wv[:], start=True, stop=True)
                        mm.then_inc(s.v_psum, 1)
                        pe.wait_ge(s.k, n + 1)
                        pe.wait_ge(s.probT, n)
                        for b in range(2):
                            for g in range(GP):
                                mm = nc.tensor.matmul(PS[:, 6 + b, g * P:(g + 1) * P], q[32 * b:32 * b + 8, g, :],
                                                      k[32 * b:32 * b + 8, g, :], start=True, stop=True)
                        mm.then_inc(s.e, 1)
                        pe.wait_ge(s.norm, n + 1)
                        for m in range(2 * GP):
                            mm = nc.tensor.transpose(PS[:, 6 + m // GP, (m % GP) * P:(m % GP + 1) * P], prob[:, m, :],
                                                     ident[:])
                        mm.then_inc(s.pT, 1)
                        pe.wait_ge(s.probT, n + 1)
                        pe.wait_ge(s.v, n + 1)
                        for g in range(GP):
                            for b in range(2):
                                mm = nc.tensor.matmul(PS[64 * b:64 * b + 64, 5, g * P:(g + 1) * P],
                                                      vT[:, g, 64 * b:64 * b + 64], probT[:, b * GP + g, :],
                                                      start=True, stop=True)
                        mm.then_inc(s.out, 1)
                        pe.wait_ge(s.h3, n + 1)
                        for tap in range(4):
                            for b in range(2):
                                mm = nc.tensor.matmul(
                                    PS[:, 4 + b, 0:256], w3[64 * b:64 * b + 64, tap, :],
                                    h3[64 * b:64 * b + 64, :, tap:tap + L2_LEN - 1:2],
                                    start=(tap == 0), stop=(tap == 3))
                        mm.then_inc(s.c3, 1)
        p.end()


QUADS = 4
KEYS = 16
KGROUPS = TOK // KEYS
HG = 2
HH = HEADS // HG
ROWS = HH * 2
TINY = 1e-30


def on_scalar(u):
    return u in (3, 6, 7, 10, 11, 14, 15)


SCALAR_TILES = [u for u in range(KEYS) if on_scalar(u)]
VECTOR_TILES = [u for u in range(KEYS) if not on_scalar(u)]


def heads_diagonal(bank):
    a = bank[:, 0:HH * TOK]
    (pstep, pn), _ = a.ap[0], a.ap[1]
    return bass.AP(tensor=a.tensor, offset=a.offset, ap=[[pstep, pn], [TOK + 2, HH], [ROWS, KEYS], [1, 2]])


def l1_attention(nc, A, h, PS):
    with ExitStack() as ctx:
        p = Part(nc, ctx, "l1")
        wq = p.sb("wq", [P, HEADS, P])
        wv = p.sb("wv", [P, 2 * HEADS * D])
        bv = p.sb("bv", [P, 2 * HEADS * D])
        fan = p.sb("fan", [P, P])
        fan_b = p.sb("fan_b", [P, P])
        ident = p.sb("ident", [P, P])
        own_key = p.sb("own_key", [P, KEYS])
        wk_rows = p.sb("wk_rows", [P, HEADS * D])
        wk_cols = p.sb("wk_cols", [P, HEADS])
        bq = p.sb("bq", [P, HEADS])
        g1 = p.sb("g1", [P, HEADS * D])
        g2 = p.sb("g2", [P, HEADS * D])
        wsum = p.sb("wsum", [P, HG, 3 * ROWS + ROWS + 3 * ROWS])
        wall = p.sb("wall", [P, HG, KEYS * ROWS])
        warm = p.sb("warm", [P, 1])
        ln = layer_norm_buffers(p, 2)
        xT = p.sb("xT", [P, 2, TOK])
        nxT = p.sb("nxT", [P, 2, TOK])
        xpad = p.sb("xpad", [P, 2, 2, TOK])
        qs = p.sb("qs", [P, 2, HEADS * TOK])
        tiles = p.sb("tiles", [P, KEYS, HEADS * TOK])
        qterm = p.sb("qterm", [P, 2, HG * HH * TOK])
        xprod = p.sb("xprod", [P, HG * KGROUPS, KEYS])
        xterm = p.sb("xterm", [P, 2, HG * KGROUPS])
        v = p.sb("v", [P, 2, 2, 2 * HEADS * D])
        logit = p.sb("logit", [P, 2, HG, HH * TOK])
        e = p.sb("e", [P, 2, 2, HEADS, TOK])
        eT = p.sb("eT", [P, 2, HEADS, TOK])
        den = p.sb("den", [P, 2, HEADS])
        sig = p.sb("sig", [P, TOK])
        yT = p.sb("yT", [P, TOK])
        z = p.sb("z", [P, 2 * D])
        s = p.sems(LN_SEMS + "weights guard folded zeroed warm xres "
                   "tile_vector tile_scalar x_psum x q_psum q qterm_psum qterm xterm_psum xprod xterm "
                   "v_psum v eT_psum den0 den1 den eT a_psum a oT_psum sig_exp sig1 sig yT z_psum z added")
        used = [p.sem(f"quad_used{m}") for m in range(QUADS)]
        logit_done = [p.sem(f"logit_done{m}") for m in range(2)]
        lT_psum = [[p.sem(f"lT_psum{m}{g}") for g in range(HG)] for m in range(2)]
        e_done = [p.sem(f"e_done{m}") for m in range(HG)]
        o_psum = [p.sem(f"o_psum{m}") for m in range(2)]
        loads = [(wq[:], A.l1_wq), (wv[:], A.l1_wv), (bv[:], A.l1_bv), (fan[:], A.fan_w), (fan_b[:], A.fan_b),
                 (ident[:], A.ident), (own_key[:], A.own_key), (wk_rows[:], A.wk_rows), (wk_cols[:], A.wk_cols),
                 (bq[:], A.l1_bq)]
        T = TOK

        def body(step):
            def pair_steps(prev, this, nxt):
                for at in range(KGROUPS * QUADS):
                    step(at, prev, this, nxt)
            return pair_steps

        def run(eng, steps):
            steps(None, (0, 0, 0), (1, 1, 0))
            with eng.Fori(0, PAIRS // 2 - 1) as i:
                steps((2 * i, 0, i), (2 * i + 1, 1, i), (2 * i + 2, 0, i + 1))
                steps((2 * i + 1, 1, i), (2 * i + 2, 0, i + 1), (2 * i + 3, 1, i + 1))
            k = PAIRS // 2 - 1
            steps((2 * k, 0, k), (2 * k + 1, 1, k), None)
            steps((2 * k + 1, 1, k), None, None)

        with nc.Block() as block:
            @block.sync
            def _(sp):
                for dst, src in loads:
                    sp.dma_start(dst, src).then_inc(s.weights, 16)

            @block.gpsimd
            def _(pool):
                nc.gpsimd.memset(ln.minus_half[:], -0.5).then_inc(s.half_set, 1)
                nc.gpsimd.memset(wsum[:], 0.0).then_inc(s.zeroed, 1)
                nc.gpsimd.memset(wall[:], 0.0).then_inc(s.zeroed, 1)
                nc.gpsimd.memset(xpad[:], 0.0).then_inc(s.zeroed, 1)
                pool.wait_ge(s.half_set, 1)
                with pool.Fori(0, PAIRS) as n:
                    layer_norm_root(pool, nc, n, ln, s)

            @block.vector
            def _(dve):
                dve.wait_ge(s.weights, 16 * len(loads))
                dve.wait_ge(s.zeroed, 3)
                step = 0
                for w, width in ((wk_rows, HEADS * D), (wk_cols, HEADS)):
                    a, b = g1[:, 0:width], g2[:, 0:width]
                    nc.vector.tensor_scalar(a, w[:], -1.0, None, ALU.mult).then_inc(s.guard, 1)
                    dve.wait_ge(s.guard, step + 1)
                    nc.vector.tensor_tensor(a, a, w[:], ALU.max).then_inc(s.guard, 1)
                    dve.wait_ge(s.guard, step + 2)
                    nc.vector.tensor_scalar(b, a, TINY, None, ALU.is_ge).then_inc(s.guard, 1)
                    dve.wait_ge(s.guard, step + 3)
                    nc.vector.tensor_tensor(w[:], w[:], b, ALU.mult).then_inc(s.guard, 1)
                    dve.wait_ge(s.guard, step + 4)
                    nc.vector.tensor_scalar(b, a, TINY, TINY, ALU.is_lt, ALU.mult).then_inc(s.guard, 1)
                    dve.wait_ge(s.guard, step + 5)
                    nc.vector.tensor_tensor(w[:], w[:], b, ALU.add).then_inc(s.guard, 1)
                    dve.wait_ge(s.guard, step + 6)
                    nc.vector.tensor_tensor(a, a, b, ALU.max).then_inc(s.guard, 1)
                    nc.vector.reciprocal(w[:], w[:]).then_inc(s.guard, 1)
                    dve.wait_ge(s.guard, step + 8)
                    step += 8
                nc.vector.tensor_tensor(wq[:].rearrange("p h (b w) -> p h b w", b=2),
                                        wq[:].rearrange("p h (b w) -> p h b w", b=2),
                                        spread(wk_rows[:].rearrange("p (h w) -> p h w", h=HEADS), 2, 2),
                                        ALU.mult).then_inc(s.folded, 1)
                nc.vector.tensor_tensor(bq[:], bq[:], wk_cols[:], ALU.mult).then_inc(s.folded, 1)
                absk = g1[:, 0:HEADS].rearrange("p (g h) -> p g h", g=HG)
                for b in range(2):
                    rows = slice(64 * b, 64 * b + 64)
                    nc.vector.tensor_scalar(wsum[rows, :, 3 * ROWS + b:4 * ROWS:2], absk[rows], -0.25, None,
                                            ALU.mult).then_inc(s.folded, 1)
                    dst = wall[rows].rearrange("p g (v h b) -> p g v h b", v=KEYS, b=2)[:, :, :, :, b]
                    for g in range(HG):
                        nc.vector.tensor_scalar(dst[:, g], spread(absk[rows, g], 1, KEYS), 0.125, None,
                                                ALU.mult).then_inc(s.folded, 1)
                dve.wait_ge(s.folded, 8)

                def normalise_1(n):
                    hp = h[:, bass.ds(n * 2, 2), :]
                    layer_norm_start(dve, nc, n, hp, ln, s)

                def normalise_2(n):
                    dve.wait_ge(s.x_psum, n)
                    layer_norm_end(dve, nc, n, ln, s)
                    dve.wait_ge(s.ln_done, n + 1)
                    hp = h[:, bass.ds(n * 2, 2), :]
                    nc.vector.tensor_tensor(hp, hp, ln.xn[:], ALU.add).then_inc(s.xres, 1)

                def take_x(n, j):
                    dve.wait_ge(s.x_psum, n + 1)
                    nc.vector.tensor_copy(xT[:, j, :], PS[:, 7, 0:T])
                    nc.vector.tensor_scalar(nxT[:, j, :], PS[:, 7, 0:T], -1.0, None, ALU.mult)
                    nc.vector.tensor_copy(xpad[0:64, j, 0, :], PS[0:64, 7, 0:T])
                    nc.vector.tensor_copy(xpad[64:128, j, 1, :], PS[64:128, 7, 0:T]).then_inc(s.x, 1)

                def take_q(n, j):
                    dve.wait_ge(s.q_psum, n + 1)
                    nc.vector.tensor_tensor(
                        qs[:, j, :].rearrange("p (h t) -> p h t", h=HEADS),
                        PS[:, 6:8, :].rearrange("p a (h t) -> p (a h) t", t=T), spread(bq[:], 2, T), ALU.add)\
                        .then_inc(s.q, 1)

                def take_xterm(n, j):
                    dve.wait_ge(s.xterm_psum, n + 1)
                    nc.vector.tensor_tensor(xprod[:], PS[:, 6, 0:HG * T].rearrange("p (a v) -> p a v", v=KEYS),
                                            spread(own_key[:], 1, HG * KGROUPS), ALU.mult).then_inc(s.xprod, 1)
                    dve.wait_ge(s.xprod, n + 1)
                    nc.vector.tensor_reduce(xterm[:, j, :], xprod[:], AX.X, ALU.add).then_inc(s.xterm, 1)

                def take_v(n, j, b):
                    dve.wait_ge(s.v_psum, 2 * n + b + 1)
                    nc.vector.tensor_tensor(v[:, j, b, :], PS[:, 6:8, :].rearrange("p a c -> p (a c)"), bv[:], ALU.add)\
                        .then_inc(s.v, 1)

                def take_logits(n, j, k, g):
                    gs = g % 2
                    dve.wait_ge(used[QUADS - 1], n * KGROUPS + g + 1)
                    dve.wait_ge(s.qterm, n + 1)
                    dve.wait_ge(s.xterm, n + 1)
                    for hg in range(HG):
                        dve.wait_ge(lT_psum[gs][hg], n * (KGROUPS // 2) + g // 2)
                        nc.vector.scalar_tensor_tensor(
                            out=logit[:, gs, hg, :], in0=PS[:, 2 * gs + hg, :],
                            scalar=xterm[:, j, hg * KGROUPS + g:hg * KGROUPS + g + 1],
                            in1=qterm[:, j, hg * HH * T:(hg + 1) * HH * T],
                            op0=ALU.subtract, op1=ALU.add).then_inc(logit_done[gs], 1)

                def take_eT(n, b):
                    dve.wait_ge(s.eT_psum, 2 * n + b + 1)
                    et = PS[:, 6:8, :].rearrange("p a (h t) -> p (a h) t", t=T)
                    nc.vector.tensor_reduce(den[:, b, :], et, AX.X, ALU.add).then_inc(s.den0, 1)
                    dve.wait_ge(s.den0, 2 * n + b + 1)
                    nc.vector.tensor_scalar(den[:, b, :], den[:, b, :], 1.0, None, ALU.add).then_inc(s.den1, 1)
                    dve.wait_ge(s.den1, 2 * n + b + 1)
                    nc.vector.reciprocal(den[:, b, :], den[:, b, :]).then_inc(s.den, 1)
                    dve.wait_ge(s.den, 2 * n + b + 1)
                    nc.vector.tensor_tensor(eT[:, b], et, spread(den[:, b, :], 2, T), ALU.mult).then_inc(s.eT, 1)

                def gate(n, j, k):
                    dve.wait_ge(s.sig_exp, n + 1)
                    nc.vector.tensor_scalar(sig[:], sig[:], 1.0, None, ALU.add).then_inc(s.sig1, 1)
                    dve.wait_ge(s.sig1, n + 1)
                    nc.vector.reciprocal(sig[:], sig[:]).then_inc(s.sig, 1)
                    dve.wait_ge(s.sig, n + 1)
                    nc.vector.tensor_tensor(yT[:], PS[:, 6, 0:T], sig[:], ALU.mult).then_inc(s.yT, 1)

                def add_up(n):
                    dve.wait_ge(s.z_psum, n + 1)
                    nc.vector.tensor_tensor(z[:], PS[:, 6, 0:2 * D], fan_b[:], ALU.add).then_inc(s.z, 1)
                    dve.wait_ge(s.z, n + 1)
                    hp = h[:, bass.ds(n * 2, 2), :]
                    nc.vector.tensor_tensor(hp, hp, z[:].rearrange("p (b w) -> p b w", b=2), ALU.add)\
                        .then_inc(s.added, 1)

                def step(at, prev, this, nxt):
                    g, m = at // QUADS, at % QUADS
                    if prev and at == 1:
                        take_logits(*prev, KGROUPS - 2)
                    if prev and at == 5:
                        take_logits(*prev, KGROUPS - 1)
                    if this and at >= 9 and m == 1:
                        take_logits(*this, g - 2)
                    if this and at == 1:
                        take_xterm(this[0], this[1])
                    if this and at == 3:
                        take_v(this[0], this[1], 0)
                    if this and at == 6:
                        take_v(this[0], this[1], 1)
                    if nxt and at == 4:
                        normalise_1(nxt[0])
                    if nxt and at == 8:
                        normalise_2(nxt[0])
                    if prev and at == 11:
                        take_eT(prev[0], 0)
                    if prev and at == 16:
                        take_eT(prev[0], 1)
                    if prev and at == 22:
                        gate(*prev)
                    if prev and at == 25:
                        add_up(prev[0])
                    if nxt and at == 27:
                        take_x(nxt[0], nxt[1])
                    if nxt and at == 29:
                        take_q(nxt[0], nxt[1])
                    if this:
                        n, j, _ = this
                        mine = [c for c in range(4) if 4 * m + c in VECTOR_TILES]
                        dve.wait_ge(used[m], n * KGROUPS + g)
                        for c in mine:
                            key = g * KEYS + 4 * c + m
                            nc.vector.tensor_scalar(tiles[:, 4 * m + c, :], qs[:, j, :], xT[:, j, key:key + 1], 0.0,
                                                    ALU.subtract, ALU.max).then_inc(s.tile_vector, 1)

                normalise_1(0)
                normalise_2(0)
                take_x(0, 0)
                take_q(0, 0)
                dve.wait_ge(s.x, 1)
                dve.wait_ge(s.q, 1)
                run(dve, body(step))

            @block.scalar
            def _(act):
                act.wait_ge(s.zeroed, 3)
                nc.scalar.activation(warm[:], wsum[:, 0, 0:1], ACT.Exp).then_inc(s.warm, 1)

                def take_qterm(n, j):
                    act.wait_ge(s.qterm_psum, n + 1)
                    nc.scalar.activation(qterm[:, j, :], PS[:, 6:8, :].rearrange("p a c -> p (a c)"), ACT.Copy)\
                        .then_inc(s.qterm, 1)

                def exponentials(n, j, k, g):
                    if g == 0:
                        act.wait_ge(o_psum[j], k)
                    for hg in range(HG):
                        act.wait_ge(lT_psum[g % 2][hg], n * (KGROUPS // 2) + g // 2 + 1)
                        dst = e[:, j, :, hg * HH:(hg + 1) * HH, g * KEYS:(g + 1) * KEYS]
                        nc.scalar.activation(dst.rearrange("p b h t -> p h t b"), heads_diagonal(PS[:, 4 + hg, :]),
                                             ACT.Exp).then_inc(e_done[hg], 1)

                def take_a(n, j, b):
                    act.wait_ge(s.a_psum, 2 * n + b + 1)
                    nc.scalar.activation(e[:, j, b], PS[:, 6:8, :].rearrange("p a (h t) -> p (a h) t", t=T), ACT.Copy)\
                        .then_inc(s.a, 1)

                def gate_exp(n, j, k):
                    act.wait_ge(o_psum[j], k + 1)
                    nc.scalar.activation(sig[:], PS[:, 6, 0:T], ACT.Exp, scale=-1.702).then_inc(s.sig_exp, 1)

                def step(at, prev, this, nxt):
                    g, m = at // QUADS, at % QUADS
                    if prev and at in (0, 4, 8):
                        exponentials(*prev, KGROUPS - 3 + g)
                    if this and at >= 12 and m == 0:
                        exponentials(*this, g - 3)
                    if prev and at in (14, 19):
                        take_a(prev[0], prev[1], (at - 14) // 5)
                    if prev and at == 21:
                        gate_exp(*prev)
                    if nxt and at == 31:
                        take_qterm(nxt[0], nxt[1])
                    if this:
                        n, j, _ = this
                        if at == 0:
                            act.wait_ge(s.x, n + 1)
                            act.wait_ge(s.q, n + 1)
                        mine = [c for c in range(4) if 4 * m + c in SCALAR_TILES]
                        act.wait_ge(used[m], n * KGROUPS + g)
                        for c in mine:
                            key = g * KEYS + 4 * c + m
                            nc.scalar.activation(tiles[:, 4 * m + c, :], qs[:, j, :], ACT.Relu,
                                                 bias=nxT[:, j, key:key + 1]).then_inc(s.tile_scalar, 1)

                take_qterm(0, 0)
                run(act, body(step))

            @block.tensor
            def _(pe):
                pe.wait_ge(s.weights, 16 * len(loads))
                pe.wait_ge(s.folded, 8)

                def quad(n, g, m):
                    vdone = sum(u < 4 * m + 4 for u in VECTOR_TILES)
                    sdone = sum(u < 4 * m + 4 for u in SCALAR_TILES)
                    pe.wait_ge(s.tile_vector, (n * KGROUPS + g) * len(VECTOR_TILES) + vdone)
                    pe.wait_ge(s.tile_scalar, (n * KGROUPS + g) * len(SCALAR_TILES) + sdone)
                    gs = g % 2
                    if m == 0:
                        pe.wait_ge(logit_done[gs], (n * (KGROUPS // 2) + g // 2) * HG)
                    for hg in range(HG):
                        for c in range(4):
                            mm = nc.tensor.matmul(
                                PS[32 * c:32 * c + 32, 2 * gs + hg, :],
                                wsum[:, hg, (3 - m) * ROWS:(7 - m) * ROWS],
                                tiles[:, 4 * m + c, hg * HH * T:(hg + 1) * HH * T], start=(m == 0), stop=(m == QUADS - 1))
                    mm.then_inc(used[m], 1)

                def transpose_logits(n, j, k, g):
                    gs = g % 2
                    for hg in range(HG):
                        pe.wait_ge(logit_done[gs], (n * (KGROUPS // 2) + g // 2) * HG + hg + 1)
                        pe.wait_ge(e_done[hg], n * KGROUPS + g)
                        for hh in range(HH):
                            mm = nc.tensor.transpose(PS[:, 4 + hg, hh * T:(hh + 1) * T],
                                                     logit[:, gs, hg, hh * T:(hh + 1) * T], ident[:])
                        mm.then_inc(lT_psum[gs][hg], 1)

                def make_x(n):
                    pe.wait_ge(s.ln_done, n + 1)
                    nc.tensor.transpose(PS[:, 7, 0:T], ln.xn[:].rearrange("p b w -> p (b w)"), ident[:])\
                        .then_inc(s.x_psum, 1)

                def make_q(n, j):
                    pe.wait_ge(s.x, n + 1)
                    for hh in range(HEADS):
                        mm = nc.tensor.matmul(PS[:, 6 + hh // 4, (hh % 4) * T:(hh % 4 + 1) * T], wq[:, hh, :],
                                              xT[:, j, :], start=True, stop=True)
                    mm.then_inc(s.q_psum, 1)

                def make_qterm(n, j):
                    pe.wait_ge(s.q, n + 1)
                    for hg in range(HG):
                        mm = nc.tensor.matmul(PS[:, 6 + hg, :], wall[:, hg, :], qs[:, j, hg * HH * T:(hg + 1) * HH * T],
                                              start=True, stop=True)
                    mm.then_inc(s.qterm_psum, 1)

                def make_xterm(n, j):
                    pe.wait_ge(s.qterm, n + 1)
                    for hg in range(HG):
                        mm = nc.tensor.matmul(PS[:, 6, hg * T:(hg + 1) * T], wall[:, hg, :], xT[:, j, :],
                                              start=True, stop=True)
                    mm.then_inc(s.xterm_psum, 1)

                def make_v(n, j, b):
                    if b == 0:
                        pe.wait_ge(s.xprod, n + 1)
                    else:
                        pe.wait_ge(s.v, 2 * n + 1)
                    for c in range(2):
                        mm = nc.tensor.matmul(PS[:, 6 + c, :], xpad[:, j, b, :],
                                              wv[:, c * HEADS * D:(c + 1) * HEADS * D],
                                              start=True, stop=True)
                    mm.then_inc(s.v_psum, 1)

                def transpose_e(n, j, b):
                    if b == 0:
                        for hg in range(HG):
                            pe.wait_ge(e_done[hg], (n + 1) * KGROUPS)
                        pe.wait_ge(s.v, 2 * n + 4 if not is_last(n) else 2 * n + 2)
                    else:
                        pe.wait_ge(s.a, 2 * n + 1)
                    for hh in range(HEADS):
                        mm = nc.tensor.transpose(PS[:, 6 + hh // 4, (hh % 4) * T:(hh % 4 + 1) * T], e[:, j, b, hh, :],
                                                 ident[:])
                    mm.then_inc(s.eT_psum, 1)

                def is_last(n):
                    return isinstance(n, int) and n == PAIRS - 1

                def transpose_back(n, b):
                    pe.wait_ge(s.eT, 2 * n + b + 1)
                    for hh in range(HEADS):
                        mm = nc.tensor.transpose(PS[:, 6 + hh // 4, (hh % 4) * T:(hh % 4 + 1) * T], eT[:, b, hh, :],
                                                 ident[:])
                    mm.then_inc(s.a_psum, 1)

                def attend(n, j):
                    pe.wait_ge(s.a, 2 * n + 2)
                    pe.wait_ge(s.v, 2 * n + 2)
                    for hh in range(HEADS):
                        for b in range(2):
                            nc.tensor.matmul(PS[64 * b:64 * b + 64, 6, 0:T], v[:, j, b, hh * D:(hh + 1) * D],
                                             e[:, j, b, hh, :], start=(hh == 0), stop=False)
                    for hh in range(HEADS):
                        for b in range(2):
                            mm = nc.tensor.matmul(PS[64 * b:64 * b + 64, 6, 0:T],
                                                  v[:, j, b, (HEADS + hh) * D:(HEADS + hh + 1) * D],
                                                  eT[:, b, hh, :], start=False, stop=(hh == HEADS - 1))
                    mm.then_inc(o_psum[j], 1)

                def fan_in(n):
                    pe.wait_ge(s.yT, n + 1)
                    nc.tensor.matmul(PS[:, 6, 0:2 * D], yT[:], fan[:], start=True, stop=True).then_inc(s.z_psum, 1)

                def step(at, prev, this, nxt):
                    g, m = at // QUADS, at % QUADS
                    if prev and at == 3:
                        transpose_logits(*prev, KGROUPS - 1)
                    if this and at >= 7 and m == 3:
                        transpose_logits(*this, g - 1)
                    if this and at == 1:
                        make_v(this[0], this[1], 1)
                    if prev and at in (6, 11):
                        transpose_e(prev[0], prev[1], (at - 6) // 5)
                    if prev and at in (9, 14):
                        transpose_back(prev[0], (at - 9) // 5)
                    if prev and at == 16:
                        attend(prev[0], prev[1])
                    if prev and at == 20:
                        fan_in(prev[0])
                    if nxt and at == 22:
                        if not prev:
                            pe.wait_ge(s.v, 2 * this[0] + 2)
                        make_x(nxt[0])
                    if nxt and at == 24:
                        if prev:
                            pe.wait_ge(s.z, prev[0] + 1)
                        make_q(nxt[0], nxt[1])
                    if nxt and at == 26:
                        make_qterm(nxt[0], nxt[1])
                    if nxt and at == 28:
                        make_xterm(nxt[0], nxt[1])
                    if nxt and at == 30:
                        make_v(nxt[0], nxt[1], 0)
                    if this:
                        quad(this[0], g, m)

                make_x(0)
                make_q(0, 0)
                make_qterm(0, 0)
                make_xterm(0, 0)
                make_v(0, 0, 0)
                run(pe, body(step))
        p.end()


def routed_layers(nc, A, h, PS):
    with ExitStack() as ctx:
        p = Part(nc, ctx, "rt")
        wi = p.sb("wi", [P, HID])
        wr = p.sb("wr", [P, LAYERS, ROUTES + 1, HID + 1])
        ws = p.sb("ws", [P, LAYERS, HID + 1])
        wo = p.sb("wo", [P, D])
        bi = p.sb("bi", [P, 1])
        bo = p.sb("bo", [P, D])
        ident = p.sb("ident", [P, P])
        ids = p.sb("ids", [1, PAIRS], I32)
        idf = p.sb("idf", [1, PAIRS])
        m1 = p.sb("m1", [1, PAIRS])
        m2 = p.sb("m2", [1, PAIRS])
        route = p.sb("route", [1, PAIRS], I32)
        warm = p.sb("warm", [P, 1])
        ln = layer_norm_buffers(p, GROUP)
        xT = p.sb("xT", [P, GP, TOK])
        hid = p.sb("hid", [P, LAYERS + 1, GP, 2, TOK])
        own = p.sb("own", [P, LAYERS, GP, HID + 1])
        res = p.sb("res", [P, GROUP, D])
        s = p.sems(LN_SEMS + "weights ids ones shared residual route_steps route warm xT_psum xT h0_psum "
                   "h0 own o_psum o added")
        hl_psum = [p.sem(f"layer_psum{m}") for m in range(LAYERS)]
        hl = [p.sem(f"layer{m}") for m in range(LAYERS)]
        loads = [(wi[:], A.rt_wi), (wr[:, :, 0:ROUTES, :], A.rt_wr), (ws[:], A.rt_ws), (wo[:], A.rt_wo),
                 (bi[:], A.rt_bi), (bo[:], A.rt_bo), (ident[:], A.ident), (ids[:], A.route_id)]
        with nc.Block() as block:
            @block.sync
            def _(sp):
                for dst, src in loads:
                    sp.dma_start(dst, src).then_inc(s.weights, 16)

            @block.gpsimd
            def _(pool):
                nc.gpsimd.memset(ln.minus_half[:], -0.5).then_inc(s.half_set, 1)
                pool.wait_ge(s.half_set, 1)
                pool.wait_ge(s.residual, 1)
                pool.wait_ge(s.route, 1)
                with pool.Fori(0, GROUPS) as n:
                    layer_norm_root(pool, nc, n, ln, s)
                    for l in range(LAYERS):
                        pool.wait_ge(hl[l], GP * n)
                    for g in range(GP):
                        r = pool.value_load(route[0:1, bass.ds(n * GP + g, 1)], min_val=0, max_val=ROUTES)
                        last = nc.gpsimd.tensor_copy(own[:, :, g, :], wr[:, :, bass.ds(r, 1), :].rearrange(
                            "p l o c -> p (l o) c"))
                        last.then_inc(s.own, 1)

            @block.vector
            def _(dve):
                dve.wait_ge(s.weights, 16 * len(loads))
                nc.vector.tensor_tensor(ws[:, :, 0:HID], ws[:, :, 0:HID], spread(ident[:], 1, LAYERS), ALU.add)\
                    .then_inc(s.shared, 1)
                dve.wait_ge(s.shared, 1)
                nc.vector.tensor_copy(wr[:, :, ROUTES, :], ws[:])
                nc.vector.tensor_tensor(wr[:, :, 0:ROUTES, :], wr[:, :, 0:ROUTES, :], spread(ws[:], 2, ROUTES),
                                        ALU.add).then_inc(s.residual, 1)
                nc.vector.tensor_copy(idf[:], ids[:]).then_inc(s.route_steps, 1)
                dve.wait_ge(s.route_steps, 1)
                nc.vector.tensor_scalar(m1[:], idf[:], 0.0, None, ALU.is_ge).then_inc(s.route_steps, 1)
                nc.vector.tensor_scalar(m2[:], idf[:], float(ROUTES - 1), None, ALU.is_le).then_inc(s.route_steps, 1)
                dve.wait_ge(s.route_steps, 3)
                nc.vector.tensor_tensor(m1[:], m1[:], m2[:], ALU.mult).then_inc(s.route_steps, 1)
                nc.vector.tensor_scalar(idf[:], idf[:], -float(ROUTES), None, ALU.add).then_inc(s.route_steps, 1)
                dve.wait_ge(s.route_steps, 5)
                nc.vector.tensor_tensor(idf[:], idf[:], m1[:], ALU.mult).then_inc(s.route_steps, 1)
                dve.wait_ge(s.route_steps, 6)
                nc.vector.tensor_scalar(route[:], idf[:], float(ROUTES), None, ALU.add).then_inc(s.route, 1)
                with dve.Fori(0, GROUPS) as n:
                    hg = h[:, bass.ds(n * GROUP, GROUP), :]
                    layer_norm_start(dve, nc, n, hg, ln, s)
                    layer_norm_end(dve, nc, n, ln, s)
                    dve.wait_ge(s.xT_psum, n + 1)
                    nc.vector.tensor_copy(xT[:].rearrange("p a b -> p (a b)"), PS[:, 0, :]).then_inc(s.xT, 1)
                    dve.wait_ge(s.o_psum, n + 1)
                    nc.vector.tensor_tensor(res[:], PS[:, 7, :].rearrange("p (a b) -> p a b", a=GROUP),
                                            spread(bo[:], 1, GROUP), ALU.add).then_inc(s.o, 1)
                    dve.wait_ge(s.o, n + 1)
                    nc.vector.tensor_tensor(hg, hg, res[:], ALU.add).then_inc(s.added, 1)

            @block.scalar
            def _(act):
                act.wait_ge(s.weights, 16 * len(loads))
                nc.scalar.activation(warm[:], bi[:], ACT.Relu).then_inc(s.warm, 1)
                with act.Fori(0, GROUPS) as n:
                    act.wait_ge(s.h0_psum, n + 1)
                    for b in range(2):
                        nc.scalar.activation(hid[:, 0, :, b, :], PS[:, 1 + b, :].rearrange("p (g t) -> p g t", g=GP),
                                             ACT.Relu, bias=bi[:]).then_inc(s.h0, 1)
                    for l in range(LAYERS):
                        for g in range(GP):
                            act.wait_ge(hl_psum[l], GP * n + g // 2 * 2 + 2)
                            nc.scalar.activation(hid[:, l + 1, g], PS[:, 3 + 2 * l + g // 2, (g % 2) * 256:(g % 2) * 256 + 256]
                                                 .rearrange("p (b t) -> p b t", b=2), ACT.Relu,
                                                 bias=own[:, l, g, HID:HID + 1]).then_inc(hl[l], 1)

            @block.tensor
            def _(pe):
                pe.wait_ge(s.weights, 16 * len(loads))
                with pe.Fori(0, GROUPS) as n:
                    pe.wait_ge(s.ln_done, n + 1)
                    for g in range(GP):
                        mm = nc.tensor.transpose(PS[:, 0, g * P:(g + 1) * P],
                                                 ln.xn[:, 2 * g:2 * g + 2, :].rearrange("p b w -> p (b w)"), ident[:])
                    mm.then_inc(s.xT_psum, 1)
                    pe.wait_ge(s.xT, n + 1)
                    for b in range(2):
                        mm = nc.tensor.matmul(PS[:, 1 + b, :], wi[64 * b:64 * b + 64, :],
                                              xT[64 * b:64 * b + 64].rearrange("p a b -> p (a b)"), start=True, stop=True)
                    mm.then_inc(s.h0_psum, 1)
                    pe.wait_ge(s.own, GP * n + GP)
                    for l in range(LAYERS):
                        for g in range(GP):
                            if l == 0:
                                pe.wait_ge(s.h0, 2 * n + 2)
                            else:
                                pe.wait_ge(hl[l - 1], GP * n + g + 1)
                            nc.tensor.matmul(PS[:, 3 + 2 * l + g // 2, (g % 2) * 256:(g % 2) * 256 + 256],
                                             own[:, l, g, 0:HID], hid[:, l, g].rearrange("p b t -> p (b t)"),
                                             start=True, stop=True).then_inc(hl_psum[l], 1)
                    for g in range(GP):
                        pe.wait_ge(hl[LAYERS - 1], GP * n + g + 1)
                        for b in range(2):
                            mm = nc.tensor.matmul(PS[:, 7, (2 * g + b) * D:(2 * g + b + 1) * D], hid[:, LAYERS, g, b, :],
                                                  wo[:], start=True, stop=True)
                    mm.then_inc(s.o_psum, 1)
        p.end()


MASKED = -1e30


def causal_attention(nc, A, h, PS):
    with ExitStack() as ctx:
        p = Part(nc, ctx, "ca")
        HPAIRS = HEADS // 2
        wqk = p.sb("wqk", [P, 2, HEADS * D])
        wv = p.sb("wv", [P, HEADS * D])
        wu = p.sb("wu", [P, HPAIRS, D])
        bqk = p.sb("bqk", [P, 2, HPAIRS])
        bv = p.sb("bv", [P, HEADS * D])
        bu = p.sb("bu", [P, D])
        ident = p.sb("ident", [P, P])
        mask = p.sb("mask", [P, TOK])
        later = p.sb("later", [P, 1])
        warm = p.sb("warm", [P, 1])
        ln = layer_norm_buffers(p, GROUP)
        xT = p.sb("xT", [P, GP, TOK])
        qk = p.sb("qk", [P, 2, HPAIRS, 2, GP * TOK])
        v = p.sb("v", [P, GROUP, HEADS * D])
        sc = p.sb("sc", [P, 2, HEADS, TOK])
        nmax = p.sb("nmax", [P, HEADS])
        pr = p.sb("pr", [P, 2, HEADS, TOK])
        tot = p.sb("tot", [P, HEADS])
        prT = p.sb("prT", [P, 2, HEADS, TOK])
        out = p.sb("out", [P, 2, HEADS * D])
        outT = p.sb("outT", [P, 2, HPAIRS, TOK])
        res = p.sb("res", [P, GROUP, D])
        s = p.sems(LN_SEMS + "weights warm xT_psum xT q k v scores masked nmax shifted exp tot recip rinv "
                   "prT_psum prT o_psum out outT_psum outT u_psum u added")
        proj = [p.sem(f"proj{m}") for m in range(4)]
        proj_used = [p.sem(f"proj_used{m}") for m in range(4)]
        NPROJ = 2 * HPAIRS * 2 + GROUP
        loads = [(wqk[:], A.ca_wqk), (wv[:], A.ca_wv), (wu[:], A.ca_wu), (bqk[:], A.ca_bqk), (bv[:], A.ca_bv),
                 (bu[:], A.ca_bu), (ident[:], A.ident), (mask[:], A.mask), (later[:], A.later)]
        with nc.Block() as block:
            @block.sync
            def _(sp):
                for dst, src in loads:
                    sp.dma_start(dst, src).then_inc(s.weights, 16)

            @block.gpsimd
            def _(pool):
                nc.gpsimd.memset(ln.minus_half[:], -0.5).then_inc(s.half_set, 1)
                pool.wait_ge(s.half_set, 1)
                with pool.Fori(0, GROUPS) as n:
                    layer_norm_root(pool, nc, n, ln, s)

            @block.vector
            def _(dve):
                dve.wait_ge(s.weights, 16 * len(loads))
                with dve.Fori(0, GROUPS) as n:
                    hg = h[:, bass.ds(n * GROUP, GROUP), :]
                    layer_norm_start(dve, nc, n, hg, ln, s)
                    layer_norm_end(dve, nc, n, ln, s)
                    dve.wait_ge(s.xT_psum, n + 1)
                    nc.vector.tensor_copy(xT[:].rearrange("p a b -> p (a b)"), PS[:, 4, :]).then_inc(s.xT, 1)
                    for c in range(2 * HPAIRS, NPROJ):
                        r = c % 4
                        dve.wait_ge(proj[r], n * (NPROJ // 4) + c // 4 + 1)
                        if c < 4 * HPAIRS:
                            hp, b = (c - 2 * HPAIRS) // 2, c % 2
                            nc.vector.tensor_scalar(qk[:, 1, hp, b, :], PS[:, r, :], bqk[:, 1, hp:hp + 1], None, ALU.add)\
                                .then_inc(proj_used[r], 1)
                        else:
                            nc.vector.tensor_tensor(v[:, c - 4 * HPAIRS, :], PS[:, r, :], bv[:], ALU.add)\
                                .then_inc(proj_used[r], 1)

                    def softmax_in(b):
                        m = n * GROUP + b
                        dve.wait_ge(s.scores, m + 1)
                        nc.vector.scalar_tensor_tensor(
                            out=sc[:, b % 2], in0=PS[:, 2 * (b % 2):2 * (b % 2) + 2, :].rearrange("p a (h t) -> p (a h) t", t=TOK),
                            scalar=D ** -0.5, in1=spread(mask[:], 1, HEADS), op0=ALU.mult, op1=ALU.add)\
                            .then_inc(s.masked, 1)
                        dve.wait_ge(s.masked, m + 1)
                        nc.vector.tensor_reduce(nmax[:], sc[:, b % 2], AX.X, ALU.max, negate=True).then_inc(s.nmax, 1)
                        dve.wait_ge(s.nmax, m + 1)
                        nc.vector.tensor_tensor(sc[:, b % 2], sc[:, b % 2], spread(nmax[:], 2, TOK), ALU.add)\
                            .then_inc(s.shifted, 1)

                    softmax_in(0)
                    for b in range(GROUP):
                        m = n * GROUP + b
                        if b + 1 < GROUP:
                            softmax_in(b + 1)
                        dve.wait_ge(s.exp, m + 1)
                        nc.vector.tensor_reduce(tot[:], pr[:, b % 2], AX.X, ALU.add).then_inc(s.tot, 1)
                        dve.wait_ge(s.tot, m + 1)
                        nc.vector.reciprocal(tot[:], tot[:]).then_inc(s.recip, 1)
                        dve.wait_ge(s.recip, m + 1)
                        nc.vector.tensor_scalar(tot[:], tot[:], later[:], None, ALU.mult).then_inc(s.rinv, 1)
                        dve.wait_ge(s.rinv, m + 1)
                        dve.wait_ge(s.o_psum, m + 1)
                        nc.vector.tensor_tensor(
                            out[:, b % 2].rearrange("p (h a w) -> p h a w", a=2, w=D),
                            PS[:, 6, :].rearrange("p (h a w) -> p h a w", a=2, w=D),
                            spread(tot[:].rearrange("p (a h) -> p h a", a=2), 3, D), ALU.mult).then_inc(s.out, 1)
                        dve.wait_ge(s.u_psum, m + 1)
                        nc.vector.tensor_tensor(res[:, b, :], PS[:, 7, 0:D], bu[:], ALU.add).then_inc(s.u, 1)
                    dve.wait_ge(s.u, n * GROUP + GROUP)
                    nc.vector.tensor_tensor(hg, hg, res[:], ALU.add).then_inc(s.added, 1)

            @block.scalar
            def _(act):
                act.wait_ge(s.weights, 16 * len(loads))
                nc.scalar.activation(warm[:], later[:], ACT.Exp).then_inc(s.warm, 1)
                with act.Fori(0, GROUPS) as n:
                    for c in range(2 * HPAIRS):
                        r, hp, b = c % 4, c // 2, c % 2
                        act.wait_ge(proj[r], n * (NPROJ // 4) + c // 4 + 1)
                        nc.scalar.activation(qk[:, 0, hp, b, :], PS[:, r, :], ACT.Identity, bias=bqk[:, 0, hp:hp + 1])\
                            .then_inc(proj_used[r], 1)
                    for b in range(GROUP):
                        m = n * GROUP + b
                        act.wait_ge(s.shifted, m + 1)
                        nc.scalar.activation(pr[:, b % 2], sc[:, b % 2], ACT.Exp).then_inc(s.exp, 1)
                        act.wait_ge(s.prT_psum, m + 1)
                        nc.scalar.activation(prT[:, b % 2], PS[:, 4:6, :].rearrange("p a (h t) -> p (a h) t", t=TOK),
                                             ACT.Copy).then_inc(s.prT, 1)
                        act.wait_ge(s.outT_psum, m + 1)
                        nc.scalar.activation(outT[:, b % 2].rearrange("p a b -> p (a b)"), PS[:, 7, :], ACT.Copy)\
                            .then_inc(s.outT, 1)

            @block.tensor
            def _(pe):
                pe.wait_ge(s.weights, 16 * len(loads))
                with pe.Fori(0, GROUPS) as n:
                    pe.wait_ge(s.ln_done, n + 1)
                    for g in range(GP):
                        mm = nc.tensor.transpose(PS[:, 4, g * P:(g + 1) * P],
                                                 ln.xn[:, 2 * g:2 * g + 2, :].rearrange("p b w -> p (b w)"), ident[:])
                    mm.then_inc(s.xT_psum, 1)
                    pe.wait_ge(s.xT, n + 1)
                    pe.wait_ge(s.masked, n * GROUP)
                    for c in range(NPROJ):
                        r, b = c % 4, c % 2
                        pe.wait_ge(proj_used[r], n * (NPROJ // 4) + c // 4)
                        rows = slice(64 * b, 64 * b + 64)
                        if c < 4 * HPAIRS:
                            i, hp = c // (2 * HPAIRS), (c // 2) % HPAIRS
                            mm = nc.tensor.matmul(PS[:, r, :], wqk[rows, i, hp * P:(hp + 1) * P],
                                                  xT[rows].rearrange("p a b -> p (a b)"), start=True, stop=True)
                        else:
                            mm = nc.tensor.matmul(PS[:, r, :], xT[rows, (c - 4 * HPAIRS) // 2, :], wv[rows, :],
                                                  start=True, stop=True)
                        mm.then_inc(proj[r], 1)
                    for r in range(4):
                        pe.wait_ge(proj_used[r], (n + 1) * (NPROJ // 4))

                    def scores(b):
                        if b >= 2:
                            pe.wait_ge(s.masked, n * GROUP + b - 1)
                        for hp in range(HPAIRS):
                            for a in range(2):
                                rows = slice(64 * a, 64 * a + 64)
                                cols = slice((b // 2) * TOK, (b // 2 + 1) * TOK)
                                mm = nc.tensor.matmul(PS[:, 2 * (b % 2) + a, hp * TOK:(hp + 1) * TOK],
                                                      qk[rows, 0, hp, b % 2, cols], qk[rows, 1, hp, b % 2, cols],
                                                      start=True, stop=True)
                        mm.then_inc(s.scores, 1)

                    scores(0)
                    for b in range(GROUP):
                        m = n * GROUP + b
                        if b + 1 < GROUP:
                            scores(b + 1)
                        pe.wait_ge(s.exp, m + 1)
                        pe.wait_ge(s.prT, m)
                        for c in range(HEADS):
                            mm = nc.tensor.transpose(PS[:, 4 + c // 4, (c % 4) * TOK:(c % 4 + 1) * TOK], pr[:, b % 2, c, :],
                                                     ident[:])
                        mm.then_inc(s.prT_psum, 1)
                        pe.wait_ge(s.prT, m + 1)
                        pe.wait_ge(s.out, m)
                        for c in range(HEADS):
                            head = 2 * (c % HPAIRS) + c // HPAIRS
                            mm = nc.tensor.matmul(PS[:, 6, head * D:(head + 1) * D], prT[:, b % 2, c, :],
                                                  v[:, b, head * D:(head + 1) * D], start=True, stop=True)
                        mm.then_inc(s.o_psum, 1)
                        pe.wait_ge(s.out, m + 1)
                        pe.wait_ge(s.u, m)
                        for hp in range(HPAIRS):
                            mm = nc.tensor.transpose(PS[:, 7, hp * TOK:(hp + 1) * TOK], out[:, b % 2, hp * P:(hp + 1) * P],
                                                     ident[:])
                        mm.then_inc(s.outT_psum, 1)
                        pe.wait_ge(s.outT, m + 1)
                        for hp in range(HPAIRS):
                            mm = nc.tensor.matmul(PS[:, 7, 0:D], outT[:, b % 2, hp, :], wu[:, hp, :],
                                                  start=(hp == 0), stop=(hp == HPAIRS - 1))
                        mm.then_inc(s.u_psum, 1)
        p.end()


def experts(nc, A, h, PS):
    with ExitStack() as ctx:
        p = Part(nc, ctx, "ex")
        EP = EXPERTS // 2
        rw = p.sb("rw", [P, EXPERTS])
        w1 = p.sb("w1", [P, EP, P])
        w2 = p.sb("w2", [P, EP, D])
        b1 = p.sb("b1", [P, EP])
        b2 = p.sb("b2", [1, 2, 2 * EP * D])
        ones = p.sb("ones", [1, P])
        ident = p.sb("ident", [P, P])
        earlier = p.sb("earlier", [P, EXPERTS, EXPERTS])
        warm = p.sb("warm", [P, 1])
        ln = layer_norm_buffers(p, GROUP)
        xall = p.sb("xall", [P, SAMPLES, D])
        weight = p.sb("weight", [P, SAMPLES, EXPERTS])
        xT = p.sb("xT", [P, GP, TOK])
        prob = p.sb("prob", [P, GP, 2, EXPERTS])
        stat = p.sb("stat", [P, GROUP])
        above = p.sb("above", [P, GROUP, EXPERTS, EXPERTS])
        tie = p.sb("tie", [P, GROUP, EXPERTS, EXPERTS])
        rank = p.sb("rank", [P, GROUP, EXPERTS])
        xs = p.sb("xs", [P, GROUP, D])
        wg = p.sb("wg", [P, GROUP, EXPERTS])
        hid = p.sb("hid", [P, 2, EP, GP * TOK])
        part = p.sb("part", [P, 2, EXPERTS, D])
        acc = p.sb("acc", [P, GROUP, D])
        res = p.sb("res", [P, GROUP, D])
        s = p.sems(LN_SEMS + "weights warm x_kept xT_psum xT logit_psum r0 r1 r2 r3 r_exp r4 r5 r6 above tie rank0 rank "
                   "sel r7 r8 r9 weight x_copied wg xT2_psum xT2 y_psum scaled part_sum res out")
        hid_psum = [p.sem(f"hid_psum{m}") for m in range(4)]
        hid_done = [p.sem(f"hid{m}") for m in range(4)]
        loads = [(rw[:], A.ex_rw), (w1[:], A.ex_w1), (w2[:], A.ex_w2), (b1[:], A.ex_b1), (b2[:], A.ex_b2),
                 (ones[:], A.ones), (ident[:], A.ident), (earlier[:], A.earlier)]
        with nc.Block() as block:
            @block.sync
            def _(sp):
                for dst, src in loads:
                    sp.dma_start(dst, src).then_inc(s.weights, 16)

            @block.gpsimd
            def _(pool):
                nc.gpsimd.memset(ln.minus_half[:], -0.5).then_inc(s.half_set, 1)
                pool.wait_ge(s.half_set, 1)
                with pool.Fori(0, GROUPS) as n:
                    layer_norm_root(pool, nc, n, ln, s)

            @block.vector
            def _(dve):
                dve.wait_ge(s.weights, 16 * len(loads))
                with dve.Fori(0, GROUPS) as n:
                    hg = h[:, bass.ds(n * GROUP, GROUP), :]
                    layer_norm_start(dve, nc, n, hg, ln, s)
                    layer_norm_end(dve, nc, n, ln, s)
                    dve.wait_ge(s.ln_done, n + 1)
                    nc.vector.tensor_copy(xall[:, bass.ds(n * GROUP, GROUP), :], ln.xn[:])
                    nc.vector.tensor_tensor(hg, hg, ln.xn[:], ALU.add).then_inc(s.x_kept, 1)
                    dve.wait_ge(s.xT_psum, n + 1)
                    nc.vector.tensor_copy(xT[:].rearrange("p a b -> p (a b)"), PS[:, 0, :]).then_inc(s.xT, 1)
                    dve.wait_ge(s.logit_psum, n + 1)
                    for b in range(2):
                        nc.vector.tensor_copy(prob[:, :, b, :], PS[:, 1 + b, 0:GP * EXPERTS].rearrange(
                            "p (g e) -> p g e", g=GP)).then_inc(s.r0, 1)
                    dve.wait_ge(s.r0, 2 * n + 2)
                    pv = prob[:].rearrange("p g b e -> p (g b) e")
                    nc.vector.tensor_reduce(stat[:], pv, AX.X, ALU.max, negate=True).then_inc(s.r1, 1)
                    dve.wait_ge(s.r1, n + 1)
                    nc.vector.tensor_tensor(pv, pv, spread(stat[:], 2, EXPERTS), ALU.add).then_inc(s.r2, 1)
                    dve.wait_ge(s.r_exp, n + 1)
                    nc.vector.tensor_reduce(stat[:], pv, AX.X, ALU.add).then_inc(s.r3, 1)
                    dve.wait_ge(s.r3, n + 1)
                    nc.vector.reciprocal(stat[:], stat[:]).then_inc(s.r4, 1)
                    dve.wait_ge(s.r4, n + 1)
                    nc.vector.tensor_tensor(pv, pv, spread(stat[:], 2, EXPERTS), ALU.mult).then_inc(s.r5, 1)
                    dve.wait_ge(s.r5, n + 1)
                    own, other = spread(pv, 3, EXPERTS), spread(pv, 2, EXPERTS)
                    nc.vector.tensor_tensor(above[:], other, own, ALU.is_gt).then_inc(s.above, 1)
                    nc.vector.tensor_tensor(tie[:], other, own, ALU.is_equal).then_inc(s.tie, 1)
                    dve.wait_ge(s.tie, n + 1)
                    ev = earlier[:].rearrange("p a b -> p (a b)")
                    tv = tie[:].rearrange("p n a b -> p n (a b)")
                    nc.vector.tensor_tensor(tv, tv, spread(ev, 1, GROUP), ALU.mult).then_inc(s.rank0, 1)
                    dve.wait_ge(s.rank0, n + 1)
                    dve.wait_ge(s.above, n + 1)
                    nc.vector.tensor_tensor(tie[:], tie[:], above[:], ALU.add).then_inc(s.r6, 1)
                    dve.wait_ge(s.r6, n + 1)
                    nc.vector.tensor_reduce(rank[:], tie[:], AX.X, ALU.add).then_inc(s.rank, 1)
                    dve.wait_ge(s.rank, n + 1)
                    nc.vector.scalar_tensor_tensor(out=rank[:], in0=rank[:], scalar=2.0, in1=pv, op0=ALU.is_lt,
                                                   op1=ALU.mult).then_inc(s.sel, 1)
                    dve.wait_ge(s.sel, n + 1)
                    nc.vector.tensor_reduce(stat[:], rank[:], AX.X, ALU.add).then_inc(s.r7, 1)
                    dve.wait_ge(s.r7, n + 1)
                    nc.vector.tensor_scalar(stat[:], stat[:], 1e-12, None, ALU.max).then_inc(s.r8, 1)
                    dve.wait_ge(s.r8, n + 1)
                    nc.vector.reciprocal(stat[:], stat[:]).then_inc(s.r9, 1)
                    dve.wait_ge(s.r9, n + 1)
                    nc.vector.tensor_tensor(weight[:, bass.ds(n * GROUP, GROUP), :], rank[:],
                                            spread(stat[:], 2, EXPERTS), ALU.mult).then_inc(s.weight, 1)

            @block.scalar
            def _(act):
                act.wait_ge(s.weights, 16 * len(loads))
                nc.scalar.activation(warm[:], b1[:, 0:1], ACT.Exp).then_inc(s.warm, 1)
                with act.Fori(0, GROUPS) as n:
                    act.wait_ge(s.r2, n + 1)
                    nc.scalar.activation(prob[:], prob[:], ACT.Exp).then_inc(s.r_exp, 1)

            @block.tensor
            def _(pe):
                pe.wait_ge(s.weights, 16 * len(loads))
                with pe.Fori(0, GROUPS) as n:
                    pe.wait_ge(s.ln_done, n + 1)
                    for g in range(GP):
                        mm = nc.tensor.transpose(PS[:, 0, g * P:(g + 1) * P],
                                                 ln.xn[:, 2 * g:2 * g + 2, :].rearrange("p b w -> p (b w)"), ident[:])
                    mm.then_inc(s.xT_psum, 1)
                    pe.wait_ge(s.xT, n + 1)
                    for g in range(GP):
                        for b in range(2):
                            rows = slice(64 * b, 64 * b + 64)
                            mm = nc.tensor.matmul(PS[:, 1 + b, g * EXPERTS:(g + 1) * EXPERTS], xT[rows, g, :], rw[rows, :],
                                                  start=True, stop=True)
                    mm.then_inc(s.logit_psum, 1)

        out_v = A.out.rearrange("n t d -> t n d")
        with nc.Block() as block:
            @block.sync
            def _(sp):
                with sp.Fori(0, GROUPS) as n:
                    sp.wait_ge(s.res, n + 1)
                    sp.dma_start(out_v[:, bass.ds(n * GROUP, GROUP), :], res[:]).then_inc(s.out, 16)
                sp.wait_ge(s.out, 16 * GROUPS)

            @block.gpsimd
            def _(pool):
                with pool.Fori(0, GROUPS) as n:
                    pool.wait_ge(s.xT2_psum, n)
                    nc.gpsimd.tensor_copy(xs[:], xall[:, bass.ds(n * GROUP, GROUP), :]).then_inc(s.x_copied, 1)
                    pool.wait_ge(s.scaled, 2 * GP * n)
                    nc.gpsimd.tensor_copy(wg[:], weight[:, bass.ds(n * GROUP, GROUP), :]).then_inc(s.wg, 1)

            @block.vector
            def _(dve):
                with dve.Fori(0, GROUPS) as n:
                    dve.wait_ge(s.xT2_psum, n + 1)
                    nc.vector.tensor_copy(xT[:].rearrange("p a b -> p (a b)"), PS[:, 0, :]).then_inc(s.xT2, 1)
                    dve.wait_ge(s.wg, n + 1)
                    for g in range(GP):
                        for a in range(2):
                            if g == 0 or a == 0:
                                dve.wait_ge(s.y_psum, n * GP + g + 1)
                            if a == 0:
                                dve.wait_ge(s.part_sum, n * GP + g)
                            w = wg[:, 2 * g:2 * g + 2, a:EXPERTS:2]
                            nc.vector.tensor_tensor(part[:, :, a * EP:(a + 1) * EP, :],
                                                    PS[:, 5 + a, :].rearrange("p (b e d) -> p b e d", b=2, d=D),
                                                    spread(w, 3, D), ALU.mult).then_inc(s.scaled, 1)
                        dve.wait_ge(s.scaled, 2 * (n * GP + g) + 2)
                        nc.vector.tensor_reduce(acc[:, 2 * g:2 * g + 2, :], part[:].rearrange("p b e d -> p b d e"),
                                                AX.X, ALU.add).then_inc(s.part_sum, 1)
                    dve.wait_ge(s.part_sum, (n + 1) * GP)
                    dve.wait_ge(s.out, 16 * n)
                    nc.vector.tensor_tensor(res[:], h[:, bass.ds(n * GROUP, GROUP), :], acc[:], ALU.add)\
                        .then_inc(s.res, 1)

            @block.scalar
            def _(act):
                nc.scalar.activation(warm[:], b1[:, 0:1], ACT.Gelu).then_inc(s.warm, 1)
                with act.Fori(0, GROUPS) as n:
                    act.wait_ge(s.y_psum, n * GP)
                    for c in range(2 * EP):
                        r, e, b = c % 4, c // 2, c % 2
                        act.wait_ge(hid_psum[r], 2 * n + c // 4 + 1)
                        nc.scalar.activation(hid[:, b, e, :], PS[:, 1 + r, :], ACT.Gelu, bias=b1[:, e:e + 1])\
                            .then_inc(hid_done[r], 1)

            @block.tensor
            def _(pe):
                with pe.Fori(0, GROUPS) as n:
                    pe.wait_ge(s.x_copied, n + 1)
                    for g in range(GP):
                        mm = nc.tensor.transpose(PS[:, 0, g * P:(g + 1) * P],
                                                 xs[:, 2 * g:2 * g + 2, :].rearrange("p b w -> p (b w)"), ident[:])
                    mm.then_inc(s.xT2_psum, 1)
                    pe.wait_ge(s.xT2, n + 1)
                    for c in range(2 * EP):
                        r, e, b = c % 4, c // 2, c % 2
                        pe.wait_ge(hid_done[r], 2 * n + c // 4)
                        nc.tensor.matmul(PS[:, 1 + r, :], w1[64 * b:64 * b + 64, e, :],
                                         xT[64 * b:64 * b + 64].rearrange("p a b -> p (a b)"),
                                         start=True, stop=True).then_inc(hid_psum[r], 1)
                    for r in range(4):
                        pe.wait_ge(hid_done[r], 2 * n + 2)
                    for g in range(GP):
                        pe.wait_ge(s.scaled, 2 * (n * GP + g))
                        for a in range(2):
                            nc.tensor.matmul(PS[:, 5 + a, :], ones[:], b2[:, a, :], start=True, stop=False)
                        for b in range(2):
                            for e in range(EP):
                                for a in range(2):
                                    rows = slice(64 * a, 64 * a + 64)
                                    mm = nc.tensor.matmul(PS[:, 5 + a, (b * EP + e) * D:(b * EP + e + 1) * D],
                                                          hid[rows, b, e, g * TOK:(g + 1) * TOK], w2[rows, e, :],
                                                          start=False, stop=(b == 1 and e == EP - 1))
                        mm.then_inc(s.y_psum, 1)
        p.end()


def build(nc, A):
    with nc.sbuf_tensor("h", [P, SAMPLES, D], F32) as h, nc.psum_tensor("banks", [P, 8, 512], F32) as banks:
        tokenise(nc, A, h, banks)
        l1_attention(nc, A, h, banks)
        routed_layers(nc, A, h, banks)
        causal_attention(nc, A, h, banks)
        experts(nc, A, h, banks)


def _columns(np, *vectors):
    return np.stack([np.tile(v, P // v.shape[0]) for v in vectors], axis=1)


def _layouts(np, I):
    f = np.float32
    out = {}
    out["x_rows"] = I["x"].reshape(2 * SAMPLES, LEN)
    w1 = I["L0_tok_w1"]
    c1 = np.zeros((3, 8, 2, 8, 16), f)
    for b in range(8):
        c1[:, b, :, b, :] = w1.transpose(2, 1, 0)
    out["c1_w"] = c1.reshape(48, P)
    w2 = I["L0_tok_w2"]
    c2 = np.zeros((8, 16, 3, GP, 2, 64), f)
    for b in range(8):
        c2[b, :, :, b // 2, b % 2, :] = w2.transpose(1, 2, 0)
    out["c2_w"] = c2.reshape(P, 3 * GP, P)
    out["c3_w"] = np.tile(I["L0_tok_w3"].transpose(1, 2, 0), (2, 1, 1))
    out["norm_cols"] = np.stack([_columns(np, *(I[f"L0_tok_{v}{m}"] for v in ("b", "g", "be", "m", "v")))
                                 for m in (1, 2, 3)], axis=2)

    def two_blocks(w, width, step):
        o = np.zeros((P, width), f)
        o[0:64, 0:w.shape[1]] = w
        o[64:128, step:step + w.shape[1]] = w
        return o

    out["tok_wq"] = two_blocks(I["L0_tok_wq"].T, 40, 32)
    out["tok_wk"] = two_blocks(I["L0_tok_wk"].T, 40, 32)
    out["tok_wv"] = two_blocks(I["L0_tok_wv"].T, P, 64)
    bqk = np.zeros((40, 2), f)
    for b in range(2):
        bqk[32 * b:32 * b + 8, 0] = I["L0_tok_bq"]
        bqk[32 * b:32 * b + 8, 1] = I["L0_tok_bk"]
    out["tok_bqk"] = bqk
    out["tok_bv"] = np.broadcast_to(np.tile(I["L0_tok_bv"], 2), (P, P))
    out["gamma"] = np.broadcast_to(np.reshape(I["L0_tok_gamma"], (1, 1)), (P, 1))
    out["ident"] = np.eye(P, dtype=f)

    wqv = I["L0_attn_wqv_w"]
    q = wqv[0:HEADS * D].reshape(HEADS, D, D).transpose(2, 0, 1)
    wq = np.zeros((2, D, HEADS, 2, D), f)
    fan = np.zeros((2, D, 2, D), f)
    for b in range(2):
        wq[b, :, :, b, :] = q
        fan[b, :, b, :] = I["L0_attn_fanin_w"].T
    out["l1_wq"] = wq.reshape(P, HEADS, P)
    out["l1_wv"] = np.tile(wqv[HEADS * D:].T, (2, 1))
    out["l1_bv"] = np.broadcast_to(I["L0_attn_wqv_b"][HEADS * D:], (P, 2 * HEADS * D))
    out["l1_bq"] = np.tile(I["L0_attn_wqv_b"][0:HEADS * D].reshape(HEADS, D).T, (2, 1))
    out["wk_rows"] = np.broadcast_to(I["L0_attn_wk"].reshape(HEADS * D), (P, HEADS * D))
    out["wk_cols"] = np.tile(I["L0_attn_wk"].T, (2, 1))
    out["fan_w"] = fan.reshape(P, P)
    out["fan_b"] = np.broadcast_to(np.tile(I["L0_attn_fanin_b"], 2), (P, P))
    out["own_key"] = (np.arange(P)[:, None] // ROWS == np.arange(KEYS)[None, :]).astype(f)

    out["rt_wi"] = np.tile(I["L0_ffn_Wi"].T, (2, 1))
    out["rt_bi"] = I["L0_ffn_bi"][:, None]
    out["rt_wr"] = np.concatenate([I["L0_ffn_Wr"].transpose(3, 0, 1, 2), I["L0_ffn_br"].transpose(2, 0, 1)[..., None]], axis=3)
    out["rt_ws"] = np.concatenate([I["L0_ffn_Ws"][:, 0].transpose(2, 0, 1), I["L0_ffn_bs"][:, 0].T[..., None]], axis=2)
    out["rt_wo"] = I["L0_ffn_Wo"].T
    out["rt_bo"] = np.broadcast_to(I["L0_ffn_bo"], (P, D))
    out["route_id"] = I["L0_ffn_route_id"].reshape(1, PAIRS)
    out["ca_wqk"] = np.tile(np.stack([I["L1_attn_Wq"], I["L1_attn_Wk"]], axis=1), (2, 1, 1))
    out["ca_wv"] = np.tile(I["L1_attn_Wv"], (2, 1))
    out["ca_wu"] = I["L1_attn_Wu"].reshape(HEADS // 2, P, D).transpose(1, 0, 2)
    out["ca_bqk"] = np.stack([I["L1_attn_bq"], I["L1_attn_bk"]]).reshape(2, HEADS // 2, P).transpose(2, 0, 1)
    out["ca_bv"] = np.broadcast_to(I["L1_attn_bv"], (P, HEADS * D))
    out["ca_bu"] = np.broadcast_to(I["L1_attn_bu"], (P, D))
    out["mask"] = np.triu(np.full((P, TOK), MASKED, f))
    out["later"] = (np.arange(P) > 0).astype(f)[:, None]
    w1 = I["L1_ffn_w1"].reshape(EXPERTS // 2, 2, D, D)
    out["ex_rw"] = np.tile(I["L1_ffn_router_w"].T, (2, 1))
    out["ex_w1"] = np.tile(w1.transpose(2, 0, 1, 3).reshape(D, EXPERTS // 2, P), (2, 1, 1))
    out["ex_w2"] = I["L1_ffn_w2"].reshape(EXPERTS // 2, P, D).transpose(1, 0, 2)
    out["ex_b1"] = I["L1_ffn_b1"].reshape(EXPERTS // 2, P).T
    b2 = I["L1_ffn_b2"].reshape(EXPERTS // 2, 2, D).transpose(1, 0, 2).reshape(1, 2, 1, EXPERTS // 2 * D)
    out["ex_b2"] = np.broadcast_to(b2, (1, 2, 2, EXPERTS // 2 * D)).reshape(1, 2, EXPERTS * D)
    out["ones"] = np.ones((1, P), f)
    out["earlier"] = np.broadcast_to(np.tril(np.ones((EXPERTS, EXPERTS), f), -1), (P, EXPERTS, EXPERTS))
    return {n: np.ascontiguousarray(a) for n, a in out.items()}


def kernel(**inputs):
    import numpy as _np
    import concourse.bacc as _bacc
    from concourse import mybir as _mybir
    from concourse.bass_utils import run_bass_kernel_spmd as _run

    nc = _bacc.Bacc("TRN2", target_bir_lowering=False, num_devices=1)
    laid = _layouts(_np, {n: _np.asarray(a) for n, a in inputs.items()})
    arrays, aps = {}, {}
    for name, a in laid.items():
        arrays[f"in_{name}_dram"] = a
        aps[name] = nc.dram_tensor(f"in_{name}_dram", a.shape, _mybir.dt.from_np(a.dtype), kind="ExternalInput").ap()
    aps["out"] = nc.dram_tensor("out_dram", (SAMPLES, TOK, D), _mybir.dt.float32, kind="ExternalOutput").ap()
    build(nc, named(**aps))
    r = _run(nc, [arrays], core_ids=[0])
    return r.results[0]["out_dram"]
```

```python
from collections import namedtuple
from contextlib import ExitStack

import concourse.bass as bass
from concourse import mybir

F32 = mybir.dt.float32
I32 = mybir.dt.int32
ALU = mybir.AluOpType
ACT = mybir.ActivationFunctionType
AX = mybir.AxisListType

P = 128
SAMPLES = 128
PAIRS = SAMPLES // 2
TOK = 128
D = 64
HEADS = 8
HID = 128
LAYERS = 2
ROUTES = 16
EXPERTS = 8
GROUP = 8
GROUPS = SAMPLES // GROUP
GP = GROUP // 2
LEN = 4096
POOL1 = 8
POOL2 = 4
L1_LEN = LEN // POOL1
L2_LEN = L1_LEN // POOL2
EPS = 1e-5


def named(**things):
    return namedtuple("Named", list(things))(**things)


class Part:

    def __init__(self, nc, ctx, name):
        self.nc, self.ctx, self.name, self.mine = nc, ctx, name, []

    def sb(self, name, shape, dt=F32):
        return self.ctx.enter_context(self.nc.sbuf_tensor(f"{self.name}_{name}", shape, dt))

    def sem(self, name):
        s = self.ctx.enter_context(self.nc.semaphore(f"{self.name}_{name}"))
        self.mine.append(s)
        return s

    def sems(self, names):
        return named(**{n: self.sem(n) for n in names.split()})

    def end(self):
        with self.nc.Block() as block:
            @block.sync
            def _(sp):
                for s in self.mine:
                    sp.sem_clear(s)


def spread(ap, axis, size):
    a = ap.unsqueeze(axis)
    shape = list(a.shape)
    shape[axis] = size
    return a.broadcast_to(shape)


def layer_norm_start(dve, nc, n, src, b, s):
    nc.vector.tensor_reduce(b.sum[:], src, AX.X, ALU.add).then_inc(s.ln_sum, 1)
    dve.wait_ge(s.ln_sum, n + 1)
    nc.vector.scalar_tensor_tensor(out=b.xc[:], in0=spread(b.sum[:], 2, D), scalar=-1.0 / D, in1=src,
                                   op0=ALU.mult, op1=ALU.add).then_inc(s.ln_centred, 1)
    dve.wait_ge(s.ln_centred, n + 1)
    nc.vector.tensor_tensor(b.sq[:], b.xc[:], b.xc[:], ALU.mult).then_inc(s.ln_squared, 1)
    dve.wait_ge(s.ln_squared, n + 1)
    nc.vector.tensor_reduce(b.var[:], b.sq[:], AX.X, ALU.add).then_inc(s.ln_sumsq, 1)
    dve.wait_ge(s.ln_sumsq, n + 1)
    nc.vector.tensor_scalar(b.var[:], b.var[:], 1.0 / D, EPS, ALU.mult, ALU.add).then_inc(s.ln_var, 1)


def layer_norm_end(dve, nc, n, b, s):
    dve.wait_ge(s.ln_root, n + 1)
    nc.vector.tensor_tensor(b.xn[:], b.xc[:], spread(b.rstd[:], 2, D), ALU.mult).then_inc(s.ln_done, 1)


def layer_norm_root(pool, nc, n, b, s):
    pool.wait_ge(s.ln_var, n + 1)
    nc.gpsimd.tensor_tensor(b.rstd[:], b.var[:], b.minus_half[:], ALU.pow).then_inc(s.ln_root, 1)


LN_SEMS = "ln_sum ln_centred ln_squared ln_sumsq ln_var ln_root ln_done half_set "


def layer_norm_buffers(part, ns):
    return named(sum=part.sb("ln_sum", [P, ns]), var=part.sb("ln_var", [P, ns]),
                           rstd=part.sb("ln_rstd", [P, ns]), minus_half=part.sb("ln_minus_half", [P, ns]),
                           xc=part.sb("ln_xc", [P, ns, D]), sq=part.sb("ln_sq", [P, ns, D]),
                           xn=part.sb("ln_xn", [P, ns, D]))


def tokenise(nc, A, h, PS):
    with ExitStack() as ctx:
        p = Part(nc, ctx, "tok")
        w1 = p.sb("w1", [48, P])
        w2 = p.sb("w2", [P, 3 * GP, P])
        w3 = p.sb("w3", [P, 4, P])
        wq = p.sb("wq", [P, 40])
        wk = p.sb("wk", [P, 40])
        wv = p.sb("wv", [P, P])
        bqk = p.sb("bqk", [40, 2])
        bv = p.sb("bv", [P, P])
        gamma = p.sb("gamma", [P, 1])
        ident = p.sb("ident", [P, P])
        cols = p.sb("cols", [P, 5, 3])
        scale = p.sb("scale", [P, 3])
        veps = p.sb("veps", [P, 3])
        root = p.sb("root", [P, 3])
        half3 = p.sb("half3", [P, 3])
        shift = p.sb("shift", [P, 3])
        warm = p.sb("warm", [P, 1])
        xin = p.sb("xin", [48, 2, LEN])
        h1raw = p.sb("h1raw", [P, L1_LEN])
        h1 = p.sb("h1", [P, L1_LEN + 2])
        h2raw = p.sb("h2raw", [P, GP, L2_LEN])
        h2 = p.sb("h2", [P, GP, L2_LEN])
        q = p.sb("q", [40, GP, L2_LEN])
        k = p.sb("k", [40, GP, L2_LEN])
        vT = p.sb("vT", [P, GP, P])
        prob = p.sb("prob", [P, 2 * GP, L2_LEN])
        probT = p.sb("probT", [P, 2 * GP, L2_LEN])
        nmax = p.sb("nmax", [P, 2 * GP])
        total = p.sb("total", [P, 2 * GP])
        h3 = p.sb("h3", [P, GP, L2_LEN + 2])
        s = p.sems("weights half_set veps root scale rows folded shift0 shift edges_a edges_b warm "
                   "h1 h2 qk_psum q k e v_psum v nmax shifted exp total recip norm pT probT out h3 c3 done c1_used")
        x_in = [p.sem(f"x_in{j}") for j in range(2)]
        x_used = [p.sem(f"x_used{j}") for j in range(2)]
        conv1 = [p.sem(f"conv1_{j}") for j in range(2)]
        pool1 = [p.sem(f"pool1_{j}") for j in range(2)]
        conv2 = [p.sem(f"conv2_{j}") for j in range(2)]
        pool2 = [p.sem(f"pool2_{j}") for j in range(2)]
        loads = [(w1[:], A.c1_w), (w2[:], A.c2_w), (w3[:], A.c3_w), (wq[:], A.tok_wq), (wk[:], A.tok_wk),
                 (wv[:], A.tok_wv), (bqk[:], A.tok_bqk), (bv[:], A.tok_bv), (gamma[:], A.gamma),
                 (ident[:], A.ident), (cols[:], A.norm_cols)]
        TURNS = GROUPS // 2
        CH = LEN // 512

        with nc.Block() as block:
            @block.sync
            def _(sp):
                for dst, src in loads:
                    sp.dma_start(dst, src).then_inc(s.weights, 16)
                sp.wait_ge(s.edges_a, 1)
                with sp.Fori(0, TURNS) as i:
                    for j in range(2):
                        n = 2 * i + j
                        sp.wait_ge(x_used[j], i)
                        rows = A.x_rows[bass.ds(n * 16, 16), :]
                        sp.dma_start(xin[0:16, j, 1:LEN], rows[:, 0:LEN - 1]).then_inc(x_in[j], 16)
                        sp.dma_start(xin[16:32, j, :], rows).then_inc(x_in[j], 16)
                        sp.dma_start(xin[32:48, j, 0:LEN - 1], rows[:, 1:LEN]).then_inc(x_in[j], 16)

            @block.gpsimd
            def _(pool):
                nc.gpsimd.memset(half3[:], -0.5).then_inc(s.half_set, 1)
                nc.gpsimd.memset(h1[:], 0.0).then_inc(s.edges_b, 1)
                nc.gpsimd.memset(h3[:], 0.0).then_inc(s.edges_b, 1)
                pool.wait_ge(s.half_set, 1)
                pool.wait_ge(s.veps, 1)
                nc.gpsimd.tensor_tensor(root[:], veps[:], half3[:], ALU.pow).then_inc(s.root, 1)

            @block.vector
            def _(dve):
                nc.vector.memset(xin[:, :, 0:1], 0.0)
                nc.vector.memset(xin[:, :, LEN - 1:LEN], 0.0).then_inc(s.edges_a, 1)
                dve.wait_ge(s.weights, 16 * len(loads))
                nc.vector.tensor_scalar(veps[:], cols[:, 4, :], EPS, None, ALU.add).then_inc(s.veps, 1)
                dve.wait_ge(s.root, 1)
                nc.vector.tensor_tensor(scale[:], cols[:, 1, :], root[:], ALU.mult).then_inc(s.scale, 1)
                dve.wait_ge(s.scale, 1)
                nc.vector.tensor_tensor(shift[:], cols[:, 0, :], cols[:, 3, :], ALU.subtract).then_inc(s.shift0, 1)
                dve.wait_ge(s.shift0, 1)
                nc.vector.tensor_tensor(shift[:], shift[:], scale[:], ALU.mult).then_inc(s.shift0, 1)
                dve.wait_ge(s.shift0, 2)
                nc.vector.tensor_tensor(shift[:], shift[:], cols[:, 2, :], ALU.add).then_inc(s.shift, 1)
                dve.wait_ge(s.rows, 1)
                nc.vector.tensor_tensor(w1[:], w1[:], PS[0:48, 0, 0:P], ALU.mult).then_inc(s.folded, 1)
                nc.vector.tensor_tensor(w2[:], w2[:], spread(PS[:, 1, 0:P], 1, 3 * GP), ALU.mult).then_inc(s.folded, 1)
                nc.vector.tensor_tensor(w3[:], w3[:], spread(PS[:, 2, 0:P], 1, 4), ALU.mult).then_inc(s.folded, 1)
                with dve.Fori(0, TURNS) as i:
                    for j in range(2):
                        n = 2 * i + j
                        for c in range(CH):
                            dve.wait_ge(conv1[c % 2], n * (CH // 2) + c // 2 + 1)
                            if c == 0:
                                dve.wait_ge(s.h1, n)
                            nc.vector.tensor_reduce(
                                h1raw[:, c * 64:(c + 1) * 64], PS[:, c % 2, :].rearrange("p (a b) -> p a b", b=POOL1),
                                AX.X, ALU.max).then_inc(pool1[c % 2], 1)
                        for g in range(GP):
                            dve.wait_ge(conv2[g % 2], n * (GP // 2) + g // 2 + 1)
                            if g == 0:
                                dve.wait_ge(s.h2, n)
                            nc.vector.tensor_reduce(
                                h2raw[:, g, :], PS[:, 2 + g % 2, :].rearrange("p (a b) -> p a b", b=POOL2),
                                AX.X, ALU.max).then_inc(pool2[g % 2], 1)
                        dve.wait_ge(s.qk_psum, n + 1)
                        nc.vector.tensor_scalar(k[:].rearrange("p a b -> p (a b)"), PS[0:40, 5, :], bqk[:, 1:2], None,
                                                ALU.add).then_inc(s.k, 1)
                        dve.wait_ge(s.v_psum, n + 1)
                        nc.vector.tensor_tensor(vT[:], PS[:, 4, :].rearrange("p (a b) -> p a b", a=GP),
                                                spread(bv[:], 1, GP), ALU.add).then_inc(s.v, 1)
                        dve.wait_ge(s.e, n + 1)
                        energy = PS[:, 6:8, :].rearrange("p a (b c) -> p (a b) c", b=GP)
                        nc.vector.tensor_reduce(nmax[:], energy, AX.X, ALU.max, negate=True).then_inc(s.nmax, 1)
                        dve.wait_ge(s.nmax, n + 1)
                        nc.vector.tensor_tensor(prob[:], energy, spread(nmax[:], 2, L2_LEN), ALU.add)\
                            .then_inc(s.shifted, 1)
                        dve.wait_ge(s.exp, n + 1)
                        nc.vector.tensor_reduce(total[:], prob[:], AX.X, ALU.add).then_inc(s.total, 1)
                        dve.wait_ge(s.total, n + 1)
                        nc.vector.reciprocal(total[:], total[:]).then_inc(s.recip, 1)
                        dve.wait_ge(s.recip, n + 1)
                        nc.vector.tensor_tensor(prob[:], prob[:], spread(total[:], 2, L2_LEN), ALU.mult)\
                            .then_inc(s.norm, 1)
                        dve.wait_ge(s.out, n + 1)
                        nc.vector.scalar_tensor_tensor(
                            out=h3[:, :, 1:L2_LEN + 1], in0=PS[:, 5, :].rearrange("p (a b) -> p a b", a=GP),
                            scalar=gamma[:, 0:1], in1=h2[:], op0=ALU.mult, op1=ALU.add).then_inc(s.h3, 1)

            @block.scalar
            def _(act):
                act.wait_ge(s.edges_b, 2)
                nc.scalar.activation(warm[:], h1[:, 0:1], ACT.Exp).then_inc(s.warm, 1)
                act.wait_ge(s.shift, 1)
                with act.Fori(0, TURNS) as i:
                    for j in range(2):
                        n = 2 * i + j
                        act.wait_ge(pool1[0], (n + 1) * (CH // 2))
                        act.wait_ge(pool1[1], (n + 1) * (CH // 2))
                        act.wait_ge(s.qk_psum, n)
                        nc.scalar.activation(h1[:, 1:L1_LEN + 1], h1raw[:], ACT.Relu, bias=shift[:, 0:1])\
                            .then_inc(s.h1, 1)
                        act.wait_ge(pool2[0], (n + 1) * (GP // 2))
                        act.wait_ge(pool2[1], (n + 1) * (GP // 2))
                        act.wait_ge(s.h3, n)
                        nc.scalar.activation(h2[:], h2raw[:], ACT.Relu, bias=shift[:, 1:2]).then_inc(s.h2, 1)
                        act.wait_ge(s.qk_psum, n + 1)
                        nc.scalar.activation(q[:].rearrange("p a b -> p (a b)"), PS[0:40, 4, :], ACT.Identity,
                                             bias=bqk[:, 0:1]).then_inc(s.q, 1)
                        act.wait_ge(s.shifted, n + 1)
                        nc.scalar.activation(prob[:], prob[:], ACT.Exp).then_inc(s.exp, 1)
                        act.wait_ge(s.pT, n + 1)
                        nc.scalar.activation(probT[:], PS[:, 6:8, :].rearrange("p a (b c) -> p (a b) c", b=GP),
                                             ACT.Copy).then_inc(s.probT, 1)
                        act.wait_ge(s.c3, n + 1)
                        hv = h[:, bass.ds(n * GROUP, GROUP), :].rearrange("p (g b) d -> p b g d", b=2)
                        nc.scalar.activation(hv, PS[:, 4:6, 0:256].rearrange("p b (g d) -> p b g d", g=GP),
                                             ACT.Identity, bias=shift[:, 2:3]).then_inc(s.done, 1)

            @block.tensor
            def _(pe):
                pe.wait_ge(s.weights, 16 * len(loads))
                pe.wait_ge(s.scale, 1)
                for m in range(3):
                    mm = nc.tensor.matmul(PS[:, m, 0:P], scale[:, m:m + 1].broadcast_to([P, P]), ident[:],
                                          start=True, stop=True)
                mm.then_inc(s.rows, 1)
                pe.wait_ge(s.folded, 3)
                pe.wait_ge(s.edges_b, 2)
                with pe.Fori(0, TURNS) as i:
                    for j in range(2):
                        n = 2 * i + j
                        pe.wait_ge(x_in[j], 48 * i + 48)
                        for c in range(CH):
                            pe.wait_ge(pool1[c % 2], n * (CH // 2) + c // 2)
                            mm = nc.tensor.matmul(PS[:, c % 2, :], w1[:], xin[:, j, c * 512:(c + 1) * 512],
                                                  start=True, stop=True)
                            mm.then_inc(conv1[c % 2], 1)
                        pe.wait_ge(pool1[(CH - 1) % 2], (n + 1) * (CH // 2))
                        pe.sem_inc(x_used[j], 1)
                        pe.wait_ge(s.h1, n + 1)
                        for g in range(GP):
                            pe.wait_ge(pool2[g % 2], n * (GP // 2) + g // 2)
                            for tap in range(3):
                                mm = nc.tensor.matmul(PS[:, 2 + g % 2, :], w2[:, tap * GP + g, :],
                                                      h1[:, tap:tap + L1_LEN], start=(tap == 0), stop=(tap == 2))
                            mm.then_inc(conv2[g % 2], 1)
                        pe.wait_ge(s.h2, n + 1)
                        pe.wait_ge(s.done, n)
                        h2f = h2[:].rearrange("p a b -> p (a b)")
                        nc.tensor.matmul(PS[0:40, 4, :], wq[:], h2f, start=True, stop=True)
                        nc.tensor.matmul(PS[0:40, 5, :], wk[:], h2f, start=True, stop=True).then_inc(s.qk_psum, 1)
                        pe.wait_ge(s.q, n + 1)
                        for g in range(GP):
                            mm = nc.tensor.matmul(PS[:, 4, g * P:(g + 1) * P], h2[:, g, :], wv[:], start=True, stop=True)
                        mm.then_inc(s.v_psum, 1)
                        pe.wait_ge(s.k, n + 1)
                        pe.wait_ge(s.probT, n)
                        for b in range(2):
                            for g in range(GP):
                                mm = nc.tensor.matmul(PS[:, 6 + b, g * P:(g + 1) * P], q[32 * b:32 * b + 8, g, :],
                                                      k[32 * b:32 * b + 8, g, :], start=True, stop=True)
                        mm.then_inc(s.e, 1)
                        pe.wait_ge(s.norm, n + 1)
                        for m in range(2 * GP):
                            mm = nc.tensor.transpose(PS[:, 6 + m // GP, (m % GP) * P:(m % GP + 1) * P], prob[:, m, :],
                                                     ident[:])
                        mm.then_inc(s.pT, 1)
                        pe.wait_ge(s.probT, n + 1)
                        pe.wait_ge(s.v, n + 1)
                        for g in range(GP):
                            for b in range(2):
                                mm = nc.tensor.matmul(PS[64 * b:64 * b + 64, 5, g * P:(g + 1) * P],
                                                      vT[:, g, 64 * b:64 * b + 64], probT[:, b * GP + g, :],
                                                      start=True, stop=True)
                        mm.then_inc(s.out, 1)
                        pe.wait_ge(s.h3, n + 1)
                        for tap in range(4):
                            for b in range(2):
                                mm = nc.tensor.matmul(
                                    PS[:, 4 + b, 0:256], w3[64 * b:64 * b + 64, tap, :],
                                    h3[64 * b:64 * b + 64, :, tap:tap + L2_LEN - 1:2],
                                    start=(tap == 0), stop=(tap == 3))
                        mm.then_inc(s.c3, 1)
        p.end()


QUADS = 4
KEYS = 16
KGROUPS = TOK // KEYS
HG = 2
HH = HEADS // HG
ROWS = HH * 2
TINY = 1e-30


def on_scalar(u):
    return u in (3, 6, 7, 10, 11, 14, 15)


SCALAR_TILES = [u for u in range(KEYS) if on_scalar(u)]
VECTOR_TILES = [u for u in range(KEYS) if not on_scalar(u)]


def heads_diagonal(bank):
    a = bank[:, 0:HH * TOK]
    (pstep, pn), _ = a.ap[0], a.ap[1]
    return bass.AP(tensor=a.tensor, offset=a.offset, ap=[[pstep, pn], [TOK + 2, HH], [ROWS, KEYS], [1, 2]])


def l1_attention(nc, A, h, PS):
    with ExitStack() as ctx:
        p = Part(nc, ctx, "l1")
        wq = p.sb("wq", [P, HEADS, P])
        wv = p.sb("wv", [P, 2 * HEADS * D])
        bv = p.sb("bv", [P, 2 * HEADS * D])
        fan = p.sb("fan", [P, P])
        fan_b = p.sb("fan_b", [P, P])
        ident = p.sb("ident", [P, P])
        own_key = p.sb("own_key", [P, KEYS])
        wk_rows = p.sb("wk_rows", [P, HEADS * D])
        wk_cols = p.sb("wk_cols", [P, HEADS])
        bq = p.sb("bq", [P, HEADS])
        g1 = p.sb("g1", [P, HEADS * D])
        g2 = p.sb("g2", [P, HEADS * D])
        wsum = p.sb("wsum", [P, HG, 3 * ROWS + ROWS + 3 * ROWS])
        wall = p.sb("wall", [P, HG, KEYS * ROWS])
        warm = p.sb("warm", [P, 1])
        ln = layer_norm_buffers(p, 2)
        xT = p.sb("xT", [P, 2, TOK])
        nxT = p.sb("nxT", [P, 2, TOK])
        xpad = p.sb("xpad", [P, 2, 2, TOK])
        qs = p.sb("qs", [P, 2, HEADS * TOK])
        tiles = p.sb("tiles", [P, KEYS, HEADS * TOK])
        qterm = p.sb("qterm", [P, 2, HG * HH * TOK])
        xprod = p.sb("xprod", [P, HG * KGROUPS, KEYS])
        xterm = p.sb("xterm", [P, 2, HG * KGROUPS])
        v = p.sb("v", [P, 2, 2, 2 * HEADS * D])
        logit = p.sb("logit", [P, 2, HG, HH * TOK])
        e = p.sb("e", [P, 2, 2, HEADS, TOK])
        eT = p.sb("eT", [P, 2, HEADS, TOK])
        den = p.sb("den", [P, 2, HEADS])
        sig = p.sb("sig", [P, TOK])
        yT = p.sb("yT", [P, TOK])
        z = p.sb("z", [P, 2 * D])
        s = p.sems(LN_SEMS + "weights guard folded zeroed warm xres "
                   "tile_vector tile_scalar x_psum x q_psum q qterm_psum qterm xterm_psum xprod xterm "
                   "v_psum v eT_psum den0 den1 den eT a_psum a oT_psum sig_exp sig1 sig yT z_psum z added")
        used = [p.sem(f"quad_used{m}") for m in range(QUADS)]
        logit_done = [p.sem(f"logit_done{m}") for m in range(2)]
        lT_psum = [[p.sem(f"lT_psum{m}{g}") for g in range(HG)] for m in range(2)]
        e_done = [p.sem(f"e_done{m}") for m in range(HG)]
        o_psum = [p.sem(f"o_psum{m}") for m in range(2)]
        loads = [(wq[:], A.l1_wq), (wv[:], A.l1_wv), (bv[:], A.l1_bv), (fan[:], A.fan_w), (fan_b[:], A.fan_b),
                 (ident[:], A.ident), (own_key[:], A.own_key), (wk_rows[:], A.wk_rows), (wk_cols[:], A.wk_cols),
                 (bq[:], A.l1_bq)]
        T = TOK

        def body(step):
            def pair_steps(prev, this, nxt):
                for at in range(KGROUPS * QUADS):
                    step(at, prev, this, nxt)
            return pair_steps

        def run(eng, steps):
            steps(None, (0, 0, 0), (1, 1, 0))
            with eng.Fori(0, PAIRS // 2 - 1) as i:
                steps((2 * i, 0, i), (2 * i + 1, 1, i), (2 * i + 2, 0, i + 1))
                steps((2 * i + 1, 1, i), (2 * i + 2, 0, i + 1), (2 * i + 3, 1, i + 1))
            k = PAIRS // 2 - 1
            steps((2 * k, 0, k), (2 * k + 1, 1, k), None)
            steps((2 * k + 1, 1, k), None, None)

        with nc.Block() as block:
            @block.sync
            def _(sp):
                for dst, src in loads:
                    sp.dma_start(dst, src).then_inc(s.weights, 16)

            @block.gpsimd
            def _(pool):
                nc.gpsimd.memset(ln.minus_half[:], -0.5).then_inc(s.half_set, 1)
                nc.gpsimd.memset(wsum[:], 0.0).then_inc(s.zeroed, 1)
                nc.gpsimd.memset(wall[:], 0.0).then_inc(s.zeroed, 1)
                nc.gpsimd.memset(xpad[:], 0.0).then_inc(s.zeroed, 1)
                pool.wait_ge(s.half_set, 1)
                with pool.Fori(0, PAIRS) as n:
                    layer_norm_root(pool, nc, n, ln, s)

            @block.vector
            def _(dve):
                dve.wait_ge(s.weights, 16 * len(loads))
                dve.wait_ge(s.zeroed, 3)
                step = 0
                for w, width in ((wk_rows, HEADS * D), (wk_cols, HEADS)):
                    a, b = g1[:, 0:width], g2[:, 0:width]
                    nc.vector.tensor_scalar(a, w[:], -1.0, None, ALU.mult).then_inc(s.guard, 1)
                    dve.wait_ge(s.guard, step + 1)
                    nc.vector.tensor_tensor(a, a, w[:], ALU.max).then_inc(s.guard, 1)
                    dve.wait_ge(s.guard, step + 2)
                    nc.vector.tensor_scalar(b, a, TINY, None, ALU.is_ge).then_inc(s.guard, 1)
                    dve.wait_ge(s.guard, step + 3)
                    nc.vector.tensor_tensor(w[:], w[:], b, ALU.mult).then_inc(s.guard, 1)
                    dve.wait_ge(s.guard, step + 4)
                    nc.vector.tensor_scalar(b, a, TINY, TINY, ALU.is_lt, ALU.mult).then_inc(s.guard, 1)
                    dve.wait_ge(s.guard, step + 5)
                    nc.vector.tensor_tensor(w[:], w[:], b, ALU.add).then_inc(s.guard, 1)
                    dve.wait_ge(s.guard, step + 6)
                    nc.vector.tensor_tensor(a, a, b, ALU.max).then_inc(s.guard, 1)
                    nc.vector.reciprocal(w[:], w[:]).then_inc(s.guard, 1)
                    dve.wait_ge(s.guard, step + 8)
                    step += 8
                nc.vector.tensor_tensor(wq[:].rearrange("p h (b w) -> p h b w", b=2),
                                        wq[:].rearrange("p h (b w) -> p h b w", b=2),
                                        spread(wk_rows[:].rearrange("p (h w) -> p h w", h=HEADS), 2, 2),
                                        ALU.mult).then_inc(s.folded, 1)
                nc.vector.tensor_tensor(bq[:], bq[:], wk_cols[:], ALU.mult).then_inc(s.folded, 1)
                absk = g1[:, 0:HEADS].rearrange("p (g h) -> p g h", g=HG)
                for b in range(2):
                    rows = slice(64 * b, 64 * b + 64)
                    nc.vector.tensor_scalar(wsum[rows, :, 3 * ROWS + b:4 * ROWS:2], absk[rows], -0.25, None,
                                            ALU.mult).then_inc(s.folded, 1)
                    dst = wall[rows].rearrange("p g (v h b) -> p g v h b", v=KEYS, b=2)[:, :, :, :, b]
                    for g in range(HG):
                        nc.vector.tensor_scalar(dst[:, g], spread(absk[rows, g], 1, KEYS), 0.125, None,
                                                ALU.mult).then_inc(s.folded, 1)
                dve.wait_ge(s.folded, 8)

                def normalise_1(n):
                    hp = h[:, bass.ds(n * 2, 2), :]
                    layer_norm_start(dve, nc, n, hp, ln, s)

                def normalise_2(n):
                    dve.wait_ge(s.x_psum, n)
                    layer_norm_end(dve, nc, n, ln, s)
                    dve.wait_ge(s.ln_done, n + 1)
                    hp = h[:, bass.ds(n * 2, 2), :]
                    nc.vector.tensor_tensor(hp, hp, ln.xn[:], ALU.add).then_inc(s.xres, 1)

                def take_x(n, j):
                    dve.wait_ge(s.x_psum, n + 1)
                    nc.vector.tensor_copy(xT[:, j, :], PS[:, 7, 0:T])
                    nc.vector.tensor_scalar(nxT[:, j, :], PS[:, 7, 0:T], -1.0, None, ALU.mult)
                    nc.vector.tensor_copy(xpad[0:64, j, 0, :], PS[0:64, 7, 0:T])
                    nc.vector.tensor_copy(xpad[64:128, j, 1, :], PS[64:128, 7, 0:T]).then_inc(s.x, 1)

                def take_q(n, j):
                    dve.wait_ge(s.q_psum, n + 1)
                    nc.vector.tensor_tensor(
                        qs[:, j, :].rearrange("p (h t) -> p h t", h=HEADS),
                        PS[:, 6:8, :].rearrange("p a (h t) -> p (a h) t", t=T), spread(bq[:], 2, T), ALU.add)\
                        .then_inc(s.q, 1)

                def take_xterm(n, j):
                    dve.wait_ge(s.xterm_psum, n + 1)
                    nc.vector.tensor_tensor(xprod[:], PS[:, 6, 0:HG * T].rearrange("p (a v) -> p a v", v=KEYS),
                                            spread(own_key[:], 1, HG * KGROUPS), ALU.mult).then_inc(s.xprod, 1)
                    dve.wait_ge(s.xprod, n + 1)
                    nc.vector.tensor_reduce(xterm[:, j, :], xprod[:], AX.X, ALU.add).then_inc(s.xterm, 1)

                def take_v(n, j, b):
                    dve.wait_ge(s.v_psum, 2 * n + b + 1)
                    nc.vector.tensor_tensor(v[:, j, b, :], PS[:, 6:8, :].rearrange("p a c -> p (a c)"), bv[:], ALU.add)\
                        .then_inc(s.v, 1)

                def take_logits(n, j, k, g):
                    gs = g % 2
                    dve.wait_ge(used[QUADS - 1], n * KGROUPS + g + 1)
                    dve.wait_ge(s.qterm, n + 1)
                    dve.wait_ge(s.xterm, n + 1)
                    for hg in range(HG):
                        dve.wait_ge(lT_psum[gs][hg], n * (KGROUPS // 2) + g // 2)
                        nc.vector.scalar_tensor_tensor(
                            out=logit[:, gs, hg, :], in0=PS[:, 2 * gs + hg, :],
                            scalar=xterm[:, j, hg * KGROUPS + g:hg * KGROUPS + g + 1],
                            in1=qterm[:, j, hg * HH * T:(hg + 1) * HH * T],
                            op0=ALU.subtract, op1=ALU.add).then_inc(logit_done[gs], 1)

                def take_eT(n, b):
                    dve.wait_ge(s.eT_psum, 2 * n + b + 1)
                    et = PS[:, 6:8, :].rearrange("p a (h t) -> p (a h) t", t=T)
                    nc.vector.tensor_reduce(den[:, b, :], et, AX.X, ALU.add).then_inc(s.den0, 1)
                    dve.wait_ge(s.den0, 2 * n + b + 1)
                    nc.vector.tensor_scalar(den[:, b, :], den[:, b, :], 1.0, None, ALU.add).then_inc(s.den1, 1)
                    dve.wait_ge(s.den1, 2 * n + b + 1)
                    nc.vector.reciprocal(den[:, b, :], den[:, b, :]).then_inc(s.den, 1)
                    dve.wait_ge(s.den, 2 * n + b + 1)
                    nc.vector.tensor_tensor(eT[:, b], et, spread(den[:, b, :], 2, T), ALU.mult).then_inc(s.eT, 1)

                def gate(n, j, k):
                    dve.wait_ge(s.sig_exp, n + 1)
                    nc.vector.tensor_scalar(sig[:], sig[:], 1.0, None, ALU.add).then_inc(s.sig1, 1)
                    dve.wait_ge(s.sig1, n + 1)
                    nc.vector.reciprocal(sig[:], sig[:]).then_inc(s.sig, 1)
                    dve.wait_ge(s.sig, n + 1)
                    nc.vector.tensor_tensor(yT[:], PS[:, 6, 0:T], sig[:], ALU.mult).then_inc(s.yT, 1)

                def add_up(n):
                    dve.wait_ge(s.z_psum, n + 1)
                    nc.vector.tensor_tensor(z[:], PS[:, 6, 0:2 * D], fan_b[:], ALU.add).then_inc(s.z, 1)
                    dve.wait_ge(s.z, n + 1)
                    hp = h[:, bass.ds(n * 2, 2), :]
                    nc.vector.tensor_tensor(hp, hp, z[:].rearrange("p (b w) -> p b w", b=2), ALU.add)\
                        .then_inc(s.added, 1)

                def step(at, prev, this, nxt):
                    g, m = at // QUADS, at % QUADS
                    if prev and at == 1:
                        take_logits(*prev, KGROUPS - 2)
                    if prev and at == 5:
                        take_logits(*prev, KGROUPS - 1)
                    if this and at >= 9 and m == 1:
                        take_logits(*this, g - 2)
                    if this and at == 1:
                        take_xterm(this[0], this[1])
                    if this and at == 3:
                        take_v(this[0], this[1], 0)
                    if this and at == 6:
                        take_v(this[0], this[1], 1)
                    if nxt and at == 4:
                        normalise_1(nxt[0])
                    if nxt and at == 8:
                        normalise_2(nxt[0])
                    if prev and at == 11:
                        take_eT(prev[0], 0)
                    if prev and at == 16:
                        take_eT(prev[0], 1)
                    if prev and at == 22:
                        gate(*prev)
                    if prev and at == 25:
                        add_up(prev[0])
                    if nxt and at == 27:
                        take_x(nxt[0], nxt[1])
                    if nxt and at == 29:
                        take_q(nxt[0], nxt[1])
                    if this:
                        n, j, _ = this
                        mine = [c for c in range(4) if 4 * m + c in VECTOR_TILES]
                        dve.wait_ge(used[m], n * KGROUPS + g)
                        for c in mine:
                            key = g * KEYS + 4 * c + m
                            nc.vector.tensor_scalar(tiles[:, 4 * m + c, :], qs[:, j, :], xT[:, j, key:key + 1], 0.0,
                                                    ALU.subtract, ALU.max).then_inc(s.tile_vector, 1)

                normalise_1(0)
                normalise_2(0)
                take_x(0, 0)
                take_q(0, 0)
                dve.wait_ge(s.x, 1)
                dve.wait_ge(s.q, 1)
                run(dve, body(step))

            @block.scalar
            def _(act):
                act.wait_ge(s.zeroed, 3)
                nc.scalar.activation(warm[:], wsum[:, 0, 0:1], ACT.Exp).then_inc(s.warm, 1)

                def take_qterm(n, j):
                    act.wait_ge(s.qterm_psum, n + 1)
                    nc.scalar.activation(qterm[:, j, :], PS[:, 6:8, :].rearrange("p a c -> p (a c)"), ACT.Copy)\
                        .then_inc(s.qterm, 1)

                def exponentials(n, j, k, g):
                    if g == 0:
                        act.wait_ge(o_psum[j], k)
                    for hg in range(HG):
                        act.wait_ge(lT_psum[g % 2][hg], n * (KGROUPS // 2) + g // 2 + 1)
                        dst = e[:, j, :, hg * HH:(hg + 1) * HH, g * KEYS:(g + 1) * KEYS]
                        nc.scalar.activation(dst.rearrange("p b h t -> p h t b"), heads_diagonal(PS[:, 4 + hg, :]),
                                             ACT.Exp).then_inc(e_done[hg], 1)

                def take_a(n, j, b):
                    act.wait_ge(s.a_psum, 2 * n + b + 1)
                    nc.scalar.activation(e[:, j, b], PS[:, 6:8, :].rearrange("p a (h t) -> p (a h) t", t=T), ACT.Copy)\
                        .then_inc(s.a, 1)

                def gate_exp(n, j, k):
                    act.wait_ge(o_psum[j], k + 1)
                    nc.scalar.activation(sig[:], PS[:, 6, 0:T], ACT.Exp, scale=-1.702).then_inc(s.sig_exp, 1)

                def step(at, prev, this, nxt):
                    g, m = at // QUADS, at % QUADS
                    if prev and at in (0, 4, 8):
                        exponentials(*prev, KGROUPS - 3 + g)
                    if this and at >= 12 and m == 0:
                        exponentials(*this, g - 3)
                    if prev and at in (14, 19):
                        take_a(prev[0], prev[1], (at - 14) // 5)
                    if prev and at == 21:
                        gate_exp(*prev)
                    if nxt and at == 31:
                        take_qterm(nxt[0], nxt[1])
                    if this:
                        n, j, _ = this
                        if at == 0:
                            act.wait_ge(s.x, n + 1)
                            act.wait_ge(s.q, n + 1)
                        mine = [c for c in range(4) if 4 * m + c in SCALAR_TILES]
                        act.wait_ge(used[m], n * KGROUPS + g)
                        for c in mine:
                            key = g * KEYS + 4 * c + m
                            nc.scalar.activation(tiles[:, 4 * m + c, :], qs[:, j, :], ACT.Relu,
                                                 bias=nxT[:, j, key:key + 1]).then_inc(s.tile_scalar, 1)

                take_qterm(0, 0)
                run(act, body(step))

            @block.tensor
            def _(pe):
                pe.wait_ge(s.weights, 16 * len(loads))
                pe.wait_ge(s.folded, 8)

                def quad(n, g, m):
                    vdone = sum(u < 4 * m + 4 for u in VECTOR_TILES)
                    sdone = sum(u < 4 * m + 4 for u in SCALAR_TILES)
                    pe.wait_ge(s.tile_vector, (n * KGROUPS + g) * len(VECTOR_TILES) + vdone)
                    pe.wait_ge(s.tile_scalar, (n * KGROUPS + g) * len(SCALAR_TILES) + sdone)
                    gs = g % 2
                    if m == 0:
                        pe.wait_ge(logit_done[gs], (n * (KGROUPS // 2) + g // 2) * HG)
                    for hg in range(HG):
                        for c in range(4):
                            mm = nc.tensor.matmul(
                                PS[32 * c:32 * c + 32, 2 * gs + hg, :],
                                wsum[:, hg, (3 - m) * ROWS:(7 - m) * ROWS],
                                tiles[:, 4 * m + c, hg * HH * T:(hg + 1) * HH * T], start=(m == 0), stop=(m == QUADS - 1))
                    mm.then_inc(used[m], 1)

                def transpose_logits(n, j, k, g):
                    gs = g % 2
                    for hg in range(HG):
                        pe.wait_ge(logit_done[gs], (n * (KGROUPS // 2) + g // 2) * HG + hg + 1)
                        pe.wait_ge(e_done[hg], n * KGROUPS + g)
                        for hh in range(HH):
                            mm = nc.tensor.transpose(PS[:, 4 + hg, hh * T:(hh + 1) * T],
                                                     logit[:, gs, hg, hh * T:(hh + 1) * T], ident[:])
                        mm.then_inc(lT_psum[gs][hg], 1)

                def make_x(n):
                    pe.wait_ge(s.ln_done, n + 1)
                    nc.tensor.transpose(PS[:, 7, 0:T], ln.xn[:].rearrange("p b w -> p (b w)"), ident[:])\
                        .then_inc(s.x_psum, 1)

                def make_q(n, j):
                    pe.wait_ge(s.x, n + 1)
                    for hh in range(HEADS):
                        mm = nc.tensor.matmul(PS[:, 6 + hh // 4, (hh % 4) * T:(hh % 4 + 1) * T], wq[:, hh, :],
                                              xT[:, j, :], start=True, stop=True)
                    mm.then_inc(s.q_psum, 1)

                def make_qterm(n, j):
                    pe.wait_ge(s.q, n + 1)
                    for hg in range(HG):
                        mm = nc.tensor.matmul(PS[:, 6 + hg, :], wall[:, hg, :], qs[:, j, hg * HH * T:(hg + 1) * HH * T],
                                              start=True, stop=True)
                    mm.then_inc(s.qterm_psum, 1)

                def make_xterm(n, j):
                    pe.wait_ge(s.qterm, n + 1)
                    for hg in range(HG):
                        mm = nc.tensor.matmul(PS[:, 6, hg * T:(hg + 1) * T], wall[:, hg, :], xT[:, j, :],
                                              start=True, stop=True)
                    mm.then_inc(s.xterm_psum, 1)

                def make_v(n, j, b):
                    if b == 0:
                        pe.wait_ge(s.xprod, n + 1)
                    else:
                        pe.wait_ge(s.v, 2 * n + 1)
                    for c in range(2):
                        mm = nc.tensor.matmul(PS[:, 6 + c, :], xpad[:, j, b, :],
                                              wv[:, c * HEADS * D:(c + 1) * HEADS * D],
                                              start=True, stop=True)
                    mm.then_inc(s.v_psum, 1)

                def transpose_e(n, j, b):
                    if b == 0:
                        for hg in range(HG):
                            pe.wait_ge(e_done[hg], (n + 1) * KGROUPS)
                        pe.wait_ge(s.v, 2 * n + 4 if not is_last(n) else 2 * n + 2)
                    else:
                        pe.wait_ge(s.a, 2 * n + 1)
                    for hh in range(HEADS):
                        mm = nc.tensor.transpose(PS[:, 6 + hh // 4, (hh % 4) * T:(hh % 4 + 1) * T], e[:, j, b, hh, :],
                                                 ident[:])
                    mm.then_inc(s.eT_psum, 1)

                def is_last(n):
                    return isinstance(n, int) and n == PAIRS - 1

                def transpose_back(n, b):
                    pe.wait_ge(s.eT, 2 * n + b + 1)
                    for hh in range(HEADS):
                        mm = nc.tensor.transpose(PS[:, 6 + hh // 4, (hh % 4) * T:(hh % 4 + 1) * T], eT[:, b, hh, :],
                                                 ident[:])
                    mm.then_inc(s.a_psum, 1)

                def attend(n, j):
                    pe.wait_ge(s.a, 2 * n + 2)
                    pe.wait_ge(s.v, 2 * n + 2)
                    for hh in range(HEADS):
                        for b in range(2):
                            nc.tensor.matmul(PS[64 * b:64 * b + 64, 6, 0:T], v[:, j, b, hh * D:(hh + 1) * D],
                                             e[:, j, b, hh, :], start=(hh == 0), stop=False)
                    for hh in range(HEADS):
                        for b in range(2):
                            mm = nc.tensor.matmul(PS[64 * b:64 * b + 64, 6, 0:T],
                                                  v[:, j, b, (HEADS + hh) * D:(HEADS + hh + 1) * D],
                                                  eT[:, b, hh, :], start=False, stop=(hh == HEADS - 1))
                    mm.then_inc(o_psum[j], 1)

                def fan_in(n):
                    pe.wait_ge(s.yT, n + 1)
                    nc.tensor.matmul(PS[:, 6, 0:2 * D], yT[:], fan[:], start=True, stop=True).then_inc(s.z_psum, 1)

                def step(at, prev, this, nxt):
                    g, m = at // QUADS, at % QUADS
                    if prev and at == 3:
                        transpose_logits(*prev, KGROUPS - 1)
                    if this and at >= 7 and m == 3:
                        transpose_logits(*this, g - 1)
                    if this and at == 1:
                        make_v(this[0], this[1], 1)
                    if prev and at in (6, 11):
                        transpose_e(prev[0], prev[1], (at - 6) // 5)
                    if prev and at in (9, 14):
                        transpose_back(prev[0], (at - 9) // 5)
                    if prev and at == 16:
                        attend(prev[0], prev[1])
                    if prev and at == 20:
                        fan_in(prev[0])
                    if nxt and at == 22:
                        if not prev:
                            pe.wait_ge(s.v, 2 * this[0] + 2)
                        make_x(nxt[0])
                    if nxt and at == 24:
                        if prev:
                            pe.wait_ge(s.z, prev[0] + 1)
                        make_q(nxt[0], nxt[1])
                    if nxt and at == 26:
                        make_qterm(nxt[0], nxt[1])
                    if nxt and at == 28:
                        make_xterm(nxt[0], nxt[1])
                    if nxt and at == 30:
                        make_v(nxt[0], nxt[1], 0)
                    if this:
                        quad(this[0], g, m)

                make_x(0)
                make_q(0, 0)
                make_qterm(0, 0)
                make_xterm(0, 0)
                make_v(0, 0, 0)
                run(pe, body(step))
        p.end()


def routed_layers(nc, A, h, PS):
    with ExitStack() as ctx:
        p = Part(nc, ctx, "rt")
        wi = p.sb("wi", [P, HID])
        wr = p.sb("wr", [P, LAYERS, ROUTES + 1, HID + 1])
        ws = p.sb("ws", [P, LAYERS, HID + 1])
        wo = p.sb("wo", [P, D])
        bi = p.sb("bi", [P, 1])
        bo = p.sb("bo", [P, D])
        ident = p.sb("ident", [P, P])
        ids = p.sb("ids", [1, PAIRS], I32)
        idf = p.sb("idf", [1, PAIRS])
        m1 = p.sb("m1", [1, PAIRS])
        m2 = p.sb("m2", [1, PAIRS])
        route = p.sb("route", [1, PAIRS], I32)
        warm = p.sb("warm", [P, 1])
        ln = layer_norm_buffers(p, GROUP)
        xT = p.sb("xT", [P, GP, TOK])
        hid = p.sb("hid", [P, LAYERS + 1, GP, 2, TOK])
        own = p.sb("own", [P, LAYERS, GP, HID + 1])
        res = p.sb("res", [P, GROUP, D])
        s = p.sems(LN_SEMS + "weights ids ones shared residual route_steps route warm xT_psum xT h0_psum "
                   "h0 own o_psum o added")
        hl_psum = [p.sem(f"layer_psum{m}") for m in range(LAYERS)]
        hl = [p.sem(f"layer{m}") for m in range(LAYERS)]
        loads = [(wi[:], A.rt_wi), (wr[:, :, 0:ROUTES, :], A.rt_wr), (ws[:], A.rt_ws), (wo[:], A.rt_wo),
                 (bi[:], A.rt_bi), (bo[:], A.rt_bo), (ident[:], A.ident), (ids[:], A.route_id)]
        with nc.Block() as block:
            @block.sync
            def _(sp):
                for dst, src in loads:
                    sp.dma_start(dst, src).then_inc(s.weights, 16)

            @block.gpsimd
            def _(pool):
                nc.gpsimd.memset(ln.minus_half[:], -0.5).then_inc(s.half_set, 1)
                pool.wait_ge(s.half_set, 1)
                pool.wait_ge(s.residual, 1)
                pool.wait_ge(s.route, 1)
                with pool.Fori(0, GROUPS) as n:
                    layer_norm_root(pool, nc, n, ln, s)
                    for l in range(LAYERS):
                        pool.wait_ge(hl[l], GP * n)
                    for g in range(GP):
                        r = pool.value_load(route[0:1, bass.ds(n * GP + g, 1)], min_val=0, max_val=ROUTES)
                        last = nc.gpsimd.tensor_copy(own[:, :, g, :], wr[:, :, bass.ds(r, 1), :].rearrange(
                            "p l o c -> p (l o) c"))
                        last.then_inc(s.own, 1)

            @block.vector
            def _(dve):
                dve.wait_ge(s.weights, 16 * len(loads))
                nc.vector.tensor_tensor(ws[:, :, 0:HID], ws[:, :, 0:HID], spread(ident[:], 1, LAYERS), ALU.add)\
                    .then_inc(s.shared, 1)
                dve.wait_ge(s.shared, 1)
                nc.vector.tensor_copy(wr[:, :, ROUTES, :], ws[:])
                nc.vector.tensor_tensor(wr[:, :, 0:ROUTES, :], wr[:, :, 0:ROUTES, :], spread(ws[:], 2, ROUTES),
                                        ALU.add).then_inc(s.residual, 1)
                nc.vector.tensor_copy(idf[:], ids[:]).then_inc(s.route_steps, 1)
                dve.wait_ge(s.route_steps, 1)
                nc.vector.tensor_scalar(m1[:], idf[:], 0.0, None, ALU.is_ge).then_inc(s.route_steps, 1)
                nc.vector.tensor_scalar(m2[:], idf[:], float(ROUTES - 1), None, ALU.is_le).then_inc(s.route_steps, 1)
                dve.wait_ge(s.route_steps, 3)
                nc.vector.tensor_tensor(m1[:], m1[:], m2[:], ALU.mult).then_inc(s.route_steps, 1)
                nc.vector.tensor_scalar(idf[:], idf[:], -float(ROUTES), None, ALU.add).then_inc(s.route_steps, 1)
                dve.wait_ge(s.route_steps, 5)
                nc.vector.tensor_tensor(idf[:], idf[:], m1[:], ALU.mult).then_inc(s.route_steps, 1)
                dve.wait_ge(s.route_steps, 6)
                nc.vector.tensor_scalar(route[:], idf[:], float(ROUTES), None, ALU.add).then_inc(s.route, 1)
                with dve.Fori(0, GROUPS) as n:
                    hg = h[:, bass.ds(n * GROUP, GROUP), :]
                    layer_norm_start(dve, nc, n, hg, ln, s)
                    layer_norm_end(dve, nc, n, ln, s)
                    dve.wait_ge(s.xT_psum, n + 1)
                    nc.vector.tensor_copy(xT[:].rearrange("p a b -> p (a b)"), PS[:, 0, :]).then_inc(s.xT, 1)
                    dve.wait_ge(s.o_psum, n + 1)
                    nc.vector.tensor_tensor(res[:], PS[:, 7, :].rearrange("p (a b) -> p a b", a=GROUP),
                                            spread(bo[:], 1, GROUP), ALU.add).then_inc(s.o, 1)
                    dve.wait_ge(s.o, n + 1)
                    nc.vector.tensor_tensor(hg, hg, res[:], ALU.add).then_inc(s.added, 1)

            @block.scalar
            def _(act):
                act.wait_ge(s.weights, 16 * len(loads))
                nc.scalar.activation(warm[:], bi[:], ACT.Relu).then_inc(s.warm, 1)
                with act.Fori(0, GROUPS) as n:
                    act.wait_ge(s.h0_psum, n + 1)
                    for b in range(2):
                        nc.scalar.activation(hid[:, 0, :, b, :], PS[:, 1 + b, :].rearrange("p (g t) -> p g t", g=GP),
                                             ACT.Relu, bias=bi[:]).then_inc(s.h0, 1)
                    for l in range(LAYERS):
                        for g in range(GP):
                            act.wait_ge(hl_psum[l], GP * n + g // 2 * 2 + 2)
                            nc.scalar.activation(hid[:, l + 1, g], PS[:, 3 + 2 * l + g // 2, (g % 2) * 256:(g % 2) * 256 + 256]
                                                 .rearrange("p (b t) -> p b t", b=2), ACT.Relu,
                                                 bias=own[:, l, g, HID:HID + 1]).then_inc(hl[l], 1)

            @block.tensor
            def _(pe):
                pe.wait_ge(s.weights, 16 * len(loads))
                with pe.Fori(0, GROUPS) as n:
                    pe.wait_ge(s.ln_done, n + 1)
                    for g in range(GP):
                        mm = nc.tensor.transpose(PS[:, 0, g * P:(g + 1) * P],
                                                 ln.xn[:, 2 * g:2 * g + 2, :].rearrange("p b w -> p (b w)"), ident[:])
                    mm.then_inc(s.xT_psum, 1)
                    pe.wait_ge(s.xT, n + 1)
                    for b in range(2):
                        mm = nc.tensor.matmul(PS[:, 1 + b, :], wi[64 * b:64 * b + 64, :],
                                              xT[64 * b:64 * b + 64].rearrange("p a b -> p (a b)"), start=True, stop=True)
                    mm.then_inc(s.h0_psum, 1)
                    pe.wait_ge(s.own, GP * n + GP)
                    for l in range(LAYERS):
                        for g in range(GP):
                            if l == 0:
                                pe.wait_ge(s.h0, 2 * n + 2)
                            else:
                                pe.wait_ge(hl[l - 1], GP * n + g + 1)
                            nc.tensor.matmul(PS[:, 3 + 2 * l + g // 2, (g % 2) * 256:(g % 2) * 256 + 256],
                                             own[:, l, g, 0:HID], hid[:, l, g].rearrange("p b t -> p (b t)"),
                                             start=True, stop=True).then_inc(hl_psum[l], 1)
                    for g in range(GP):
                        pe.wait_ge(hl[LAYERS - 1], GP * n + g + 1)
                        for b in range(2):
                            mm = nc.tensor.matmul(PS[:, 7, (2 * g + b) * D:(2 * g + b + 1) * D], hid[:, LAYERS, g, b, :],
                                                  wo[:], start=True, stop=True)
                    mm.then_inc(s.o_psum, 1)
        p.end()


MASKED = -1e30
CG = 4
CGROUPS = SAMPLES // CG
HPAIRS = HEADS // 2


def count(value):
    return max(value, 0) if isinstance(value, int) else value


def causal_attention(nc, A, h, PS):
    with ExitStack() as ctx:
        p = Part(nc, ctx, "ca")
        wqk = p.sb("wqk", [P, 2, HEADS * D])
        wv = p.sb("wv", [P, HEADS * D])
        wu = p.sb("wu", [P, HPAIRS, D])
        bqk = p.sb("bqk", [P, 2, HPAIRS])
        bv = p.sb("bv", [P, HEADS * D])
        bu = p.sb("bu", [P, 1])
        ident = p.sb("ident", [P, P])
        mask = p.sb("mask", [P, TOK])
        later = p.sb("later", [P, 1])
        warm = p.sb("warm", [P, 1])
        ln = layer_norm_buffers(p, CG)
        xpad = p.sb("xpad", [P, 2, CG // 2, 2, TOK])
        q = p.sb("q", [P, 2, HPAIRS, CG, TOK])
        kpad = p.sb("kpad", [P, 2, HPAIRS, CG, 2, TOK])
        v = p.sb("v", [P, 2, CG, HEADS * D])
        sc = p.sb("sc", [P, 2, HEADS, TOK])
        nmax = p.sb("nmax", [P, 2, HEADS])
        pr = p.sb("pr", [P, 2, HEADS, TOK])
        tot = p.sb("tot", [P, 2, HEADS])
        prT = p.sb("prT", [P, HEADS, TOK])
        outT = p.sb("outT", [P, HPAIRS, CG, TOK])
        uT = p.sb("uT", [P, CG, TOK])
        s = p.sems(LN_SEMS + "weights warm zeroed x_psum xpad q_psum q k_psum k_low k_high v_psum v scores masked nmax "
                   "exp recip rinv norm prT_psum prT o_psum outT uT_psum uT u_psum half_added added")
        loads = [(wqk[:], A.ca_wqk), (wv[:], A.ca_wv), (wu[:], A.ca_wu), (bqk[:], A.ca_bqk), (bv[:], A.ca_bv),
                 (bu[:], A.ca_bu), (ident[:], A.ident), (mask[:], A.mask), (later[:], A.later)]
        SKEW = 3

        def run(eng, step):
            def group(n, slot):
                for b in range(CG):
                    step(n, slot, b)
            for n in range(-SKEW, 2):
                group(n, n % 2)
            middle = (CGROUPS - SKEW) // 2
            with eng.Fori(1, middle) as i:
                group(2 * i, 0)
                group(2 * i + 1, 1)
            for n in range(2 * middle, CGROUPS + 1):
                group(n, n % 2)

        def there(first, b=0):
            return not isinstance(first, int) or 0 <= first + b < SAMPLES

        with nc.Block() as block:
            @block.sync
            def _(sp):
                for dst, src in loads:
                    sp.dma_start(dst, src).then_inc(s.weights, 16)

            @block.gpsimd
            def _(pool):
                nc.gpsimd.memset(ln.minus_half[:], -0.5).then_inc(s.half_set, 1)
                nc.gpsimd.memset(xpad[:], 0.0).then_inc(s.zeroed, 1)
                nc.gpsimd.memset(kpad[:], 0.0).then_inc(s.zeroed, 1)
                pool.wait_ge(s.half_set, 1)
                with pool.Fori(0, CGROUPS) as g:
                    layer_norm_root(pool, nc, g, ln, s)

            @block.vector
            def _(dve):
                dve.wait_ge(s.weights, 16 * len(loads))
                dve.wait_ge(s.zeroed, 2)

                def step(n, slot, b):
                    t = CG * n + b
                    if there(t):
                        dve.wait_ge(s.exp, t + 1)
                        nc.vector.reciprocal(tot[:, b % 2], tot[:, b % 2]).then_inc(s.recip, 1)
                    if there(t):
                        dve.wait_ge(s.recip, t + 1)
                        nc.vector.tensor_scalar(tot[:, b % 2], tot[:, b % 2], later[:], None, ALU.mult).then_inc(s.rinv, 1)
                        dve.wait_ge(s.rinv, t + 1)
                        nc.vector.tensor_tensor(pr[:, b % 2], pr[:, b % 2], spread(tot[:, b % 2], 2, TOK), ALU.mult)\
                            .then_inc(s.norm, 1)
                    if there(CG * (n + 2)) and b == 0:
                        dve.wait_ge(s.x_psum, n + 3)
                        xv = PS[:, 7, 0:CG // 2 * TOK].rearrange("p (a t) -> p a t", t=TOK)
                        dve.wait_ge(s.v_psum, count(CG * (n + 1)))
                        nc.vector.tensor_copy(xpad[0:64, slot, :, 0, :], xv[0:64])
                        nc.vector.tensor_copy(xpad[64:128, slot, :, 1, :], xv[64:128]).then_inc(s.xpad, 1)
                    if there(t + 3):
                        vslot = slot if b == 0 else 1 - slot
                        dve.wait_ge(s.v_psum, t + 4)
                        dve.wait_ge(s.o_psum, count(t - 4))
                        nc.vector.tensor_tensor(v[:, vslot, (b + 3) % CG, :], PS[:, 0, :], bv[:], ALU.add)\
                            .then_inc(s.v, 1)
                    if there(t + 2):
                        dve.wait_ge(s.scores, t + 3)
                        nc.vector.scalar_tensor_tensor(
                            out=sc[:, b % 2], in0=PS[:, 2:4, :].rearrange("p a (h t) -> p (a h) t", t=TOK),
                            scalar=D ** -0.5, in1=spread(mask[:], 1, HEADS), op0=ALU.mult, op1=ALU.add)\
                            .then_inc(s.masked, 1)
                        dve.wait_ge(s.masked, t + 3)
                        nc.vector.tensor_reduce(nmax[:, b % 2], sc[:, b % 2], AX.X, ALU.max, negate=True)\
                            .then_inc(s.nmax, 1)
                    if there(t + 6):
                        kslot = 1 - slot if b < 2 else slot
                        hp = (b + 2) % CG
                        dve.wait_ge(s.k_psum, t + 7)
                        dve.wait_ge(s.scores, count(CG * n + (0 if b < 2 else CG)))
                        nc.vector.tensor_scalar(kpad[0:64, kslot, hp, :, 0, :],
                                                PS[0:64, 1, :].rearrange("p (a t) -> p a t", t=TOK),
                                                bqk[0:64, 1, hp:hp + 1], None, ALU.add).then_inc(s.k_low, 1)
                    if there(CG * (n - 1)) and b == 1:
                        dve.wait_ge(s.u_psum, n)
                        uv = PS[:, 7, :].rearrange("p (a c w) -> p a c w", a=CG, c=2)
                        hg = h[:, bass.ds(CG * (n - 1), CG), :]
                        nc.vector.tensor_tensor(hg, hg, uv[:, :, 0, :], ALU.add).then_inc(s.half_added, 1)
                        dve.wait_ge(s.half_added, n)
                        nc.vector.tensor_tensor(hg, hg, uv[:, :, 1, :], ALU.add).then_inc(s.added, 1)
                    if there(CG * (n + 3)) and b == 2:
                        layer_norm_start(dve, nc, n + 3, h[:, bass.ds(CG * (n + 3), CG), :], ln, s)
                    if there(CG * (n + 3)) and b == 3:
                        dve.wait_ge(s.x_psum, n + 3)
                        layer_norm_end(dve, nc, n + 3, ln, s)

                run(dve, step)

            @block.scalar
            def _(act):
                act.wait_ge(s.weights, 16 * len(loads))
                act.wait_ge(s.zeroed, 2)
                nc.scalar.activation(warm[:], later[:], ACT.Exp).then_inc(s.warm, 1)

                def step(n, slot, b):
                    t = CG * n + b
                    if there(t - 1):
                        act.wait_ge(s.o_psum, t)
                        nc.scalar.activation(outT[:, :, (b - 1) % CG, :], PS[:, 6, :].rearrange("p (a t) -> p a t", t=TOK),
                                             ACT.Copy).then_inc(s.outT, 1)
                    if there(t + 1):
                        e = (b + 1) % 2
                        act.wait_ge(s.nmax, t + 2)
                        act.wait_ge(s.prT_psum, count(t))
                        for c in range(HEADS):
                            last = nc.scalar.activation(pr[:, e, c, :], sc[:, e, c, :], ACT.Exp, bias=nmax[:, e, c:c + 1],
                                                        accum_out=tot[:, e, c:c + 1])
                        last.then_inc(s.exp, 1)
                    if there(t):
                        act.wait_ge(s.prT_psum, t + 1)
                        nc.scalar.activation(prT[:], PS[:, 4:6, :].rearrange("p a (h t) -> p (a h) t", t=TOK),
                                             ACT.Copy).then_inc(s.prT, 1)
                    if there(t + 6):
                        kslot = 1 - slot if b < 2 else slot
                        hp = (b + 2) % CG
                        act.wait_ge(s.scores, count(CG * n + (0 if b < 2 else CG)))
                        act.wait_ge(s.q_psum, t + 7)
                        nc.scalar.activation(q[:, kslot, hp].rearrange("p a t -> p (a t)"), PS[:, 0, :], ACT.Identity,
                                             bias=bqk[:, 0, hp:hp + 1]).then_inc(s.q, 1)
                        act.wait_ge(s.k_psum, t + 7)
                        act.wait_ge(s.k_low, t + 7)
                        nc.scalar.activation(kpad[64:128, kslot, hp, :, 1, :],
                                             PS[64:128, 1, :].rearrange("p (a t) -> p a t", t=TOK), ACT.Identity,
                                             bias=bqk[64:128, 1, hp:hp + 1]).then_inc(s.k_high, 1)
                    if there(CG * (n - 1)) and b == 0:
                        act.wait_ge(s.uT_psum, n)
                        nc.scalar.activation(uT[:].rearrange("p a t -> p (a t)"), PS[:, 7, :], ACT.Identity, bias=bu[:])\
                            .then_inc(s.uT, 1)

                run(act, step)

            @block.tensor
            def _(pe):
                pe.wait_ge(s.weights, 16 * len(loads))

                def step(n, slot, b):
                    t = CG * n + b
                    other = 1 - slot
                    if there(t + 2):
                        kslot, kb = (slot, b + 2) if b < 2 else (other, b - 2)
                        made = CG * n + CG if b < 2 else CG * n + 2 * CG
                        pe.wait_ge(s.q, made)
                        pe.wait_ge(s.k_high, made)
                        pe.wait_ge(s.masked, t + 2)
                        for hp in range(HPAIRS):
                            mm = nc.tensor.matmul(PS[:, 2 + hp // 2, (hp % 2) * 2 * TOK:(hp % 2 + 1) * 2 * TOK],
                                                  q[:, kslot, hp, kb, :],
                                                  kpad[:, kslot, hp, kb].rearrange("p a t -> p (a t)"),
                                                  start=True, stop=True)
                        mm.then_inc(s.scores, 1)
                    if there(t):
                        pe.wait_ge(s.norm, t + 1)
                        pe.wait_ge(s.prT, t)
                        for c in range(HEADS):
                            mm = nc.tensor.transpose(PS[:, 4 + c // 4, (c % 4) * TOK:(c % 4 + 1) * TOK], pr[:, b % 2, c, :],
                                                     ident[:])
                        mm.then_inc(s.prT_psum, 1)
                    if there(t + 6):
                        xslot = other if b < 2 else slot
                        hp = (b + 2) % CG
                        xv = xpad[:, xslot].rearrange("p a c t -> p (a c t)")
                        if b == 2:
                            pe.wait_ge(s.xpad, n + 3)
                        pe.wait_ge(s.v, count(t + 4))
                        if not there(t + 3):
                            pe.wait_ge(s.q, t + 6)
                        nc.tensor.matmul(PS[:, 0, :], wqk[:, 0, hp * P:(hp + 1) * P], xv, start=True, stop=True)\
                            .then_inc(s.q_psum, 1)
                        pe.wait_ge(s.k_high, t + 6)
                        nc.tensor.matmul(PS[:, 1, :], wqk[:, 1, hp * P:(hp + 1) * P], xv, start=True, stop=True)\
                            .then_inc(s.k_psum, 1)
                    if there(CG * (n - 1)) and b == 0:
                        pe.wait_ge(s.outT, CG * n)
                        if there(CG * (n + 2)):
                            pe.wait_ge(s.xpad, n + 3)
                        for hp in range(HPAIRS):
                            a = hp % 2
                            mm = nc.tensor.matmul(PS[64 * a:64 * a + 64, 7, :], wu[:, hp, :],
                                                  outT[:, hp].rearrange("p a t -> p (a t)"), start=(hp < 2), stop=(hp >= 2))
                        mm.then_inc(s.uT_psum, 1)
                    if there(CG * (n - 1)) and b == 1:
                        pe.wait_ge(s.uT, n)
                        for m in range(CG):
                            mm = nc.tensor.transpose(PS[:, 7, m * TOK:(m + 1) * TOK], uT[:, m, :], ident[:])
                        mm.then_inc(s.u_psum, 1)
                    if there(t):
                        pe.wait_ge(s.prT, t + 1)
                        pe.wait_ge(s.v, t + 1)
                        pe.wait_ge(s.outT, t)
                        for c in range(HEADS):
                            hp, a = c // 2, c % 2
                            mm = nc.tensor.matmul(PS[64 * a:64 * a + 64, 6, hp * TOK:(hp + 1) * TOK],
                                                  v[:, slot, b, c * D:(c + 1) * D], prT[:, c, :], start=True, stop=True)
                        mm.then_inc(s.o_psum, 1)
                    if there(t + 4):
                        if there(t + 6):
                            pe.wait_ge(s.q, t + 7)
                        else:
                            pe.wait_ge(s.v, t + 4)
                        nc.tensor.matmul(PS[:, 0, :], xpad[:, other, b // 2, b % 2, :], wv[:], start=True, stop=True)\
                            .then_inc(s.v_psum, 1)
                    if there(CG * (n + 3)) and b == 3:
                        pe.wait_ge(s.ln_done, n + 4)
                        pe.wait_ge(s.added, count(n))
                        for m in range(CG // 2):
                            mm = nc.tensor.transpose(PS[:, 7, m * P:(m + 1) * P],
                                                     ln.xn[:, 2 * m:2 * m + 2, :].rearrange("p b w -> p (b w)"), ident[:])
                        mm.then_inc(s.x_psum, 1)

                run(pe, step)
        p.end()


def experts(nc, A, h, PS):
    with ExitStack() as ctx:
        p = Part(nc, ctx, "ex")
        EP = EXPERTS // 2
        rw = p.sb("rw", [P, EXPERTS])
        w1 = p.sb("w1", [P, EP, P])
        w2 = p.sb("w2", [P, EP, D])
        b1 = p.sb("b1", [P, EP])
        b2 = p.sb("b2", [1, 2, 2 * EP * D])
        ones = p.sb("ones", [1, P])
        ident = p.sb("ident", [P, P])
        earlier = p.sb("earlier", [P, EXPERTS, EXPERTS])
        warm = p.sb("warm", [P, 1])
        ln = layer_norm_buffers(p, GROUP)
        xall = p.sb("xall", [P, SAMPLES, D])
        weight = p.sb("weight", [P, SAMPLES, EXPERTS])
        xT = p.sb("xT", [P, GP, TOK])
        prob = p.sb("prob", [P, GP, 2, EXPERTS])
        stat = p.sb("stat", [P, GROUP])
        above = p.sb("above", [P, GROUP, EXPERTS, EXPERTS])
        tie = p.sb("tie", [P, GROUP, EXPERTS, EXPERTS])
        rank = p.sb("rank", [P, GROUP, EXPERTS])
        xs = p.sb("xs", [P, GROUP, D])
        wg = p.sb("wg", [P, GROUP, EXPERTS])
        hid = p.sb("hid", [P, 2, EP, GP * TOK])
        part = p.sb("part", [P, 2, EXPERTS, D])
        acc = p.sb("acc", [P, GROUP, D])
        res = p.sb("res", [P, GROUP, D])
        s = p.sems(LN_SEMS + "weights warm x_kept xT_psum xT logit_psum r0 r1 r2 r3 r_exp r4 r5 r6 above tie rank0 rank "
                   "sel r7 r8 r9 weight x_copied wg xT2_psum xT2 y_psum scaled part_sum res out")
        hid_psum = [p.sem(f"hid_psum{m}") for m in range(4)]
        hid_done = [p.sem(f"hid{m}") for m in range(4)]
        loads = [(rw[:], A.ex_rw), (w1[:], A.ex_w1), (w2[:], A.ex_w2), (b1[:], A.ex_b1), (b2[:], A.ex_b2),
                 (ones[:], A.ones), (ident[:], A.ident), (earlier[:], A.earlier)]
        with nc.Block() as block:
            @block.sync
            def _(sp):
                for dst, src in loads:
                    sp.dma_start(dst, src).then_inc(s.weights, 16)

            @block.gpsimd
            def _(pool):
                nc.gpsimd.memset(ln.minus_half[:], -0.5).then_inc(s.half_set, 1)
                pool.wait_ge(s.half_set, 1)
                with pool.Fori(0, GROUPS) as n:
                    layer_norm_root(pool, nc, n, ln, s)

            @block.vector
            def _(dve):
                dve.wait_ge(s.weights, 16 * len(loads))
                with dve.Fori(0, GROUPS) as n:
                    hg = h[:, bass.ds(n * GROUP, GROUP), :]
                    layer_norm_start(dve, nc, n, hg, ln, s)
                    layer_norm_end(dve, nc, n, ln, s)
                    dve.wait_ge(s.ln_done, n + 1)
                    nc.vector.tensor_copy(xall[:, bass.ds(n * GROUP, GROUP), :], ln.xn[:])
                    nc.vector.tensor_tensor(hg, hg, ln.xn[:], ALU.add).then_inc(s.x_kept, 1)
                    dve.wait_ge(s.xT_psum, n + 1)
                    nc.vector.tensor_copy(xT[:].rearrange("p a b -> p (a b)"), PS[:, 0, :]).then_inc(s.xT, 1)
                    dve.wait_ge(s.logit_psum, n + 1)
                    for b in range(2):
                        nc.vector.tensor_copy(prob[:, :, b, :], PS[:, 1 + b, 0:GP * EXPERTS].rearrange(
                            "p (g e) -> p g e", g=GP)).then_inc(s.r0, 1)
                    dve.wait_ge(s.r0, 2 * n + 2)
                    pv = prob[:].rearrange("p g b e -> p (g b) e")
                    nc.vector.tensor_reduce(stat[:], pv, AX.X, ALU.max, negate=True).then_inc(s.r1, 1)
                    dve.wait_ge(s.r1, n + 1)
                    nc.vector.tensor_tensor(pv, pv, spread(stat[:], 2, EXPERTS), ALU.add).then_inc(s.r2, 1)
                    dve.wait_ge(s.r_exp, n + 1)
                    nc.vector.tensor_reduce(stat[:], pv, AX.X, ALU.add).then_inc(s.r3, 1)
                    dve.wait_ge(s.r3, n + 1)
                    nc.vector.reciprocal(stat[:], stat[:]).then_inc(s.r4, 1)
                    dve.wait_ge(s.r4, n + 1)
                    nc.vector.tensor_tensor(pv, pv, spread(stat[:], 2, EXPERTS), ALU.mult).then_inc(s.r5, 1)
                    dve.wait_ge(s.r5, n + 1)
                    own, other = spread(pv, 3, EXPERTS), spread(pv, 2, EXPERTS)
                    nc.vector.tensor_tensor(above[:], other, own, ALU.is_gt).then_inc(s.above, 1)
                    nc.vector.tensor_tensor(tie[:], other, own, ALU.is_equal).then_inc(s.tie, 1)
                    dve.wait_ge(s.tie, n + 1)
                    ev = earlier[:].rearrange("p a b -> p (a b)")
                    tv = tie[:].rearrange("p n a b -> p n (a b)")
                    nc.vector.tensor_tensor(tv, tv, spread(ev, 1, GROUP), ALU.mult).then_inc(s.rank0, 1)
                    dve.wait_ge(s.rank0, n + 1)
                    dve.wait_ge(s.above, n + 1)
                    nc.vector.tensor_tensor(tie[:], tie[:], above[:], ALU.add).then_inc(s.r6, 1)
                    dve.wait_ge(s.r6, n + 1)
                    nc.vector.tensor_reduce(rank[:], tie[:], AX.X, ALU.add).then_inc(s.rank, 1)
                    dve.wait_ge(s.rank, n + 1)
                    nc.vector.scalar_tensor_tensor(out=rank[:], in0=rank[:], scalar=2.0, in1=pv, op0=ALU.is_lt,
                                                   op1=ALU.mult).then_inc(s.sel, 1)
                    dve.wait_ge(s.sel, n + 1)
                    nc.vector.tensor_reduce(stat[:], rank[:], AX.X, ALU.add).then_inc(s.r7, 1)
                    dve.wait_ge(s.r7, n + 1)
                    nc.vector.tensor_scalar(stat[:], stat[:], 1e-12, None, ALU.max).then_inc(s.r8, 1)
                    dve.wait_ge(s.r8, n + 1)
                    nc.vector.reciprocal(stat[:], stat[:]).then_inc(s.r9, 1)
                    dve.wait_ge(s.r9, n + 1)
                    nc.vector.tensor_tensor(weight[:, bass.ds(n * GROUP, GROUP), :], rank[:],
                                            spread(stat[:], 2, EXPERTS), ALU.mult).then_inc(s.weight, 1)

            @block.scalar
            def _(act):
                act.wait_ge(s.weights, 16 * len(loads))
                nc.scalar.activation(warm[:], b1[:, 0:1], ACT.Exp).then_inc(s.warm, 1)
                with act.Fori(0, GROUPS) as n:
                    act.wait_ge(s.r2, n + 1)
                    nc.scalar.activation(prob[:], prob[:], ACT.Exp).then_inc(s.r_exp, 1)

            @block.tensor
            def _(pe):
                pe.wait_ge(s.weights, 16 * len(loads))
                with pe.Fori(0, GROUPS) as n:
                    pe.wait_ge(s.ln_done, n + 1)
                    for g in range(GP):
                        mm = nc.tensor.transpose(PS[:, 0, g * P:(g + 1) * P],
                                                 ln.xn[:, 2 * g:2 * g + 2, :].rearrange("p b w -> p (b w)"), ident[:])
                    mm.then_inc(s.xT_psum, 1)
                    pe.wait_ge(s.xT, n + 1)
                    for g in range(GP):
                        for b in range(2):
                            rows = slice(64 * b, 64 * b + 64)
                            mm = nc.tensor.matmul(PS[:, 1 + b, g * EXPERTS:(g + 1) * EXPERTS], xT[rows, g, :], rw[rows, :],
                                                  start=True, stop=True)
                    mm.then_inc(s.logit_psum, 1)

        out_v = A.out.rearrange("n t d -> t n d")
        with nc.Block() as block:
            @block.sync
            def _(sp):
                with sp.Fori(0, GROUPS) as n:
                    sp.wait_ge(s.res, n + 1)
                    sp.dma_start(out_v[:, bass.ds(n * GROUP, GROUP), :], res[:]).then_inc(s.out, 16)
                sp.wait_ge(s.out, 16 * GROUPS)

            @block.gpsimd
            def _(pool):
                with pool.Fori(0, GROUPS) as n:
                    pool.wait_ge(s.xT2_psum, n)
                    nc.gpsimd.tensor_copy(xs[:], xall[:, bass.ds(n * GROUP, GROUP), :]).then_inc(s.x_copied, 1)
                    pool.wait_ge(s.scaled, 2 * GP * n)
                    nc.gpsimd.tensor_copy(wg[:], weight[:, bass.ds(n * GROUP, GROUP), :]).then_inc(s.wg, 1)

            @block.vector
            def _(dve):
                with dve.Fori(0, GROUPS) as n:
                    dve.wait_ge(s.xT2_psum, n + 1)
                    nc.vector.tensor_copy(xT[:].rearrange("p a b -> p (a b)"), PS[:, 0, :]).then_inc(s.xT2, 1)
                    dve.wait_ge(s.wg, n + 1)
                    for g in range(GP):
                        for a in range(2):
                            if g == 0 or a == 0:
                                dve.wait_ge(s.y_psum, n * GP + g + 1)
                            if a == 0:
                                dve.wait_ge(s.part_sum, n * GP + g)
                            w = wg[:, 2 * g:2 * g + 2, a:EXPERTS:2]
                            nc.vector.tensor_tensor(part[:, :, a * EP:(a + 1) * EP, :],
                                                    PS[:, 5 + a, :].rearrange("p (b e d) -> p b e d", b=2, d=D),
                                                    spread(w, 3, D), ALU.mult).then_inc(s.scaled, 1)
                        dve.wait_ge(s.scaled, 2 * (n * GP + g) + 2)
                        nc.vector.tensor_reduce(acc[:, 2 * g:2 * g + 2, :], part[:].rearrange("p b e d -> p b d e"),
                                                AX.X, ALU.add).then_inc(s.part_sum, 1)
                    dve.wait_ge(s.part_sum, (n + 1) * GP)
                    dve.wait_ge(s.out, 16 * n)
                    nc.vector.tensor_tensor(res[:], h[:, bass.ds(n * GROUP, GROUP), :], acc[:], ALU.add)\
                        .then_inc(s.res, 1)

            @block.scalar
            def _(act):
                nc.scalar.activation(warm[:], b1[:, 0:1], ACT.Gelu).then_inc(s.warm, 1)
                with act.Fori(0, GROUPS) as n:
                    act.wait_ge(s.y_psum, n * GP)
                    for c in range(2 * EP):
                        r, e, b = c % 4, c // 2, c % 2
                        act.wait_ge(hid_psum[r], 2 * n + c // 4 + 1)
                        nc.scalar.activation(hid[:, b, e, :], PS[:, 1 + r, :], ACT.Gelu, bias=b1[:, e:e + 1])\
                            .then_inc(hid_done[r], 1)

            @block.tensor
            def _(pe):
                with pe.Fori(0, GROUPS) as n:
                    pe.wait_ge(s.x_copied, n + 1)
                    for g in range(GP):
                        mm = nc.tensor.transpose(PS[:, 0, g * P:(g + 1) * P],
                                                 xs[:, 2 * g:2 * g + 2, :].rearrange("p b w -> p (b w)"), ident[:])
                    mm.then_inc(s.xT2_psum, 1)
                    pe.wait_ge(s.xT2, n + 1)
                    for c in range(2 * EP):
                        r, e, b = c % 4, c // 2, c % 2
                        pe.wait_ge(hid_done[r], 2 * n + c // 4)
                        nc.tensor.matmul(PS[:, 1 + r, :], w1[64 * b:64 * b + 64, e, :],
                                         xT[64 * b:64 * b + 64].rearrange("p a b -> p (a b)"),
                                         start=True, stop=True).then_inc(hid_psum[r], 1)
                    for r in range(4):
                        pe.wait_ge(hid_done[r], 2 * n + 2)
                    for g in range(GP):
                        pe.wait_ge(s.scaled, 2 * (n * GP + g))
                        for a in range(2):
                            nc.tensor.matmul(PS[:, 5 + a, :], ones[:], b2[:, a, :], start=True, stop=False)
                        for b in range(2):
                            for e in range(EP):
                                for a in range(2):
                                    rows = slice(64 * a, 64 * a + 64)
                                    mm = nc.tensor.matmul(PS[:, 5 + a, (b * EP + e) * D:(b * EP + e + 1) * D],
                                                          hid[rows, b, e, g * TOK:(g + 1) * TOK], w2[rows, e, :],
                                                          start=False, stop=(b == 1 and e == EP - 1))
                        mm.then_inc(s.y_psum, 1)
        p.end()


def build(nc, A):
    with nc.sbuf_tensor("h", [P, SAMPLES, D], F32) as h, nc.psum_tensor("banks", [P, 8, 512], F32) as banks:
        tokenise(nc, A, h, banks)
        l1_attention(nc, A, h, banks)
        routed_layers(nc, A, h, banks)
        causal_attention(nc, A, h, banks)
        experts(nc, A, h, banks)


def _columns(np, *vectors):
    return np.stack([np.tile(v, P // v.shape[0]) for v in vectors], axis=1)


def _layouts(np, I):
    f = np.float32
    out = {}
    out["x_rows"] = I["x"].reshape(2 * SAMPLES, LEN)
    w1 = I["L0_tok_w1"]
    c1 = np.zeros((3, 8, 2, 8, 16), f)
    for b in range(8):
        c1[:, b, :, b, :] = w1.transpose(2, 1, 0)
    out["c1_w"] = c1.reshape(48, P)
    w2 = I["L0_tok_w2"]
    c2 = np.zeros((8, 16, 3, GP, 2, 64), f)
    for b in range(8):
        c2[b, :, :, b // 2, b % 2, :] = w2.transpose(1, 2, 0)
    out["c2_w"] = c2.reshape(P, 3 * GP, P)
    out["c3_w"] = np.tile(I["L0_tok_w3"].transpose(1, 2, 0), (2, 1, 1))
    out["norm_cols"] = np.stack([_columns(np, *(I[f"L0_tok_{v}{m}"] for v in ("b", "g", "be", "m", "v")))
                                 for m in (1, 2, 3)], axis=2)

    def two_blocks(w, width, step):
        o = np.zeros((P, width), f)
        o[0:64, 0:w.shape[1]] = w
        o[64:128, step:step + w.shape[1]] = w
        return o

    out["tok_wq"] = two_blocks(I["L0_tok_wq"].T, 40, 32)
    out["tok_wk"] = two_blocks(I["L0_tok_wk"].T, 40, 32)
    out["tok_wv"] = two_blocks(I["L0_tok_wv"].T, P, 64)
    bqk = np.zeros((40, 2), f)
    for b in range(2):
        bqk[32 * b:32 * b + 8, 0] = I["L0_tok_bq"]
        bqk[32 * b:32 * b + 8, 1] = I["L0_tok_bk"]
    out["tok_bqk"] = bqk
    out["tok_bv"] = np.broadcast_to(np.tile(I["L0_tok_bv"], 2), (P, P))
    out["gamma"] = np.broadcast_to(np.reshape(I["L0_tok_gamma"], (1, 1)), (P, 1))
    out["ident"] = np.eye(P, dtype=f)

    wqv = I["L0_attn_wqv_w"]
    q = wqv[0:HEADS * D].reshape(HEADS, D, D).transpose(2, 0, 1)
    wq = np.zeros((2, D, HEADS, 2, D), f)
    fan = np.zeros((2, D, 2, D), f)
    for b in range(2):
        wq[b, :, :, b, :] = q
        fan[b, :, b, :] = I["L0_attn_fanin_w"].T
    out["l1_wq"] = wq.reshape(P, HEADS, P)
    out["l1_wv"] = np.tile(wqv[HEADS * D:].T, (2, 1))
    out["l1_bv"] = np.broadcast_to(I["L0_attn_wqv_b"][HEADS * D:], (P, 2 * HEADS * D))
    out["l1_bq"] = np.tile(I["L0_attn_wqv_b"][0:HEADS * D].reshape(HEADS, D).T, (2, 1))
    out["wk_rows"] = np.broadcast_to(I["L0_attn_wk"].reshape(HEADS * D), (P, HEADS * D))
    out["wk_cols"] = np.tile(I["L0_attn_wk"].T, (2, 1))
    out["fan_w"] = fan.reshape(P, P)
    out["fan_b"] = np.broadcast_to(np.tile(I["L0_attn_fanin_b"], 2), (P, P))
    out["own_key"] = (np.arange(P)[:, None] // ROWS == np.arange(KEYS)[None, :]).astype(f)

    out["rt_wi"] = np.tile(I["L0_ffn_Wi"].T, (2, 1))
    out["rt_bi"] = I["L0_ffn_bi"][:, None]
    out["rt_wr"] = np.concatenate([I["L0_ffn_Wr"].transpose(3, 0, 1, 2), I["L0_ffn_br"].transpose(2, 0, 1)[..., None]], axis=3)
    out["rt_ws"] = np.concatenate([I["L0_ffn_Ws"][:, 0].transpose(2, 0, 1), I["L0_ffn_bs"][:, 0].T[..., None]], axis=2)
    out["rt_wo"] = I["L0_ffn_Wo"].T
    out["rt_bo"] = np.broadcast_to(I["L0_ffn_bo"], (P, D))
    out["route_id"] = I["L0_ffn_route_id"].reshape(1, PAIRS)
    out["ca_wqk"] = np.tile(np.stack([I["L1_attn_Wq"], I["L1_attn_Wk"]], axis=1), (2, 1, 1))
    out["ca_wv"] = np.tile(I["L1_attn_Wv"], (2, 1))
    out["ca_wu"] = I["L1_attn_Wu"].reshape(HEADS // 2, P, D).transpose(1, 0, 2)
    out["ca_bqk"] = np.stack([I["L1_attn_bq"], I["L1_attn_bk"]]).reshape(2, HEADS // 2, P).transpose(2, 0, 1)
    out["ca_bv"] = np.broadcast_to(I["L1_attn_bv"], (P, HEADS * D))
    out["ca_bu"] = np.concatenate([I["L1_attn_bu"], np.zeros(D, f)])[:, None]
    out["mask"] = np.triu(np.full((P, TOK), MASKED, f))
    out["later"] = (np.arange(P) > 0).astype(f)[:, None]
    w1 = I["L1_ffn_w1"].reshape(EXPERTS // 2, 2, D, D)
    out["ex_rw"] = np.tile(I["L1_ffn_router_w"].T, (2, 1))
    out["ex_w1"] = np.tile(w1.transpose(2, 0, 1, 3).reshape(D, EXPERTS // 2, P), (2, 1, 1))
    out["ex_w2"] = I["L1_ffn_w2"].reshape(EXPERTS // 2, P, D).transpose(1, 0, 2)
    out["ex_b1"] = I["L1_ffn_b1"].reshape(EXPERTS // 2, P).T
    b2 = I["L1_ffn_b2"].reshape(EXPERTS // 2, 2, D).transpose(1, 0, 2).reshape(1, 2, 1, EXPERTS // 2 * D)
    out["ex_b2"] = np.broadcast_to(b2, (1, 2, 2, EXPERTS // 2 * D)).reshape(1, 2, EXPERTS * D)
    out["ones"] = np.ones((1, P), f)
    out["earlier"] = np.broadcast_to(np.tril(np.ones((EXPERTS, EXPERTS), f), -1), (P, EXPERTS, EXPERTS))
    return {n: np.ascontiguousarray(a) for n, a in out.items()}


def kernel(**inputs):
    import numpy as _np
    import concourse.bacc as _bacc
    from concourse import mybir as _mybir
    from concourse.bass_utils import run_bass_kernel_spmd as _run

    nc = _bacc.Bacc("TRN2", target_bir_lowering=False, num_devices=1)
    laid = _layouts(_np, {n: _np.asarray(a) for n, a in inputs.items()})
    arrays, aps = {}, {}
    for name, a in laid.items():
        arrays[f"in_{name}_dram"] = a
        aps[name] = nc.dram_tensor(f"in_{name}_dram", a.shape, _mybir.dt.from_np(a.dtype), kind="ExternalInput").ap()
    aps["out"] = nc.dram_tensor("out_dram", (SAMPLES, TOK, D), _mybir.dt.float32, kind="ExternalOutput").ap()
    build(nc, named(**aps))
    r = _run(nc, [arrays], core_ids=[0])
    return r.results[0]["out_dram"]
```

```python
from collections import namedtuple
from contextlib import ExitStack

import concourse.bass as bass
from concourse import mybir

F32 = mybir.dt.float32
BF16 = mybir.dt.bfloat16
I32 = mybir.dt.int32
ALU = mybir.AluOpType
ACT = mybir.ActivationFunctionType
AX = mybir.AxisListType

P = 128
SAMPLES = 128
PAIRS = SAMPLES // 2
TOK = 128
D = 64
HEADS = 8
HID = 128
LAYERS = 2
ROUTES = 16
EXPERTS = 8
GROUP = 8
GROUPS = SAMPLES // GROUP
GP = GROUP // 2
LEN = 4096
POOL1 = 8
POOL2 = 4
L1_LEN = LEN // POOL1
L2_LEN = L1_LEN // POOL2
EPS = 1e-5


def named(**things):
    return namedtuple("Named", list(things))(**things)


class Part:

    def __init__(self, nc, ctx, name):
        self.nc, self.ctx, self.name, self.mine = nc, ctx, name, []

    def sb(self, name, shape, dt=F32):
        return self.ctx.enter_context(self.nc.sbuf_tensor(f"{self.name}_{name}", shape, dt))

    def sem(self, name):
        s = self.ctx.enter_context(self.nc.semaphore(f"{self.name}_{name}"))
        self.mine.append(s)
        return s

    def sems(self, names):
        return named(**{n: self.sem(n) for n in names.split()})

    def end(self):
        with self.nc.Block() as block:
            @block.sync
            def _(sp):
                for s in self.mine:
                    sp.sem_clear(s)


def spread(ap, axis, size):
    a = ap.unsqueeze(axis)
    shape = list(a.shape)
    shape[axis] = size
    return a.broadcast_to(shape)


def count(value):
    return max(value, 0) if isinstance(value, int) else value


def layer_norm_start(dve, nc, n, src, b, s):
    nc.vector.tensor_reduce(b.sum[:], src, AX.X, ALU.add).then_inc(s.ln_sum, 1)
    dve.wait_ge(s.ln_sum, n + 1)
    nc.vector.scalar_tensor_tensor(out=b.xc[:], in0=spread(b.sum[:], 2, D), scalar=-1.0 / D, in1=src,
                                   op0=ALU.mult, op1=ALU.add).then_inc(s.ln_centred, 1)
    dve.wait_ge(s.ln_centred, n + 1)
    nc.vector.tensor_tensor(b.sq[:], b.xc[:], b.xc[:], ALU.mult).then_inc(s.ln_squared, 1)
    dve.wait_ge(s.ln_squared, n + 1)
    nc.vector.tensor_reduce(b.var[:], b.sq[:], AX.X, ALU.add).then_inc(s.ln_sumsq, 1)
    dve.wait_ge(s.ln_sumsq, n + 1)
    nc.vector.tensor_scalar(b.var[:], b.var[:], 1.0 / D, EPS, ALU.mult, ALU.add).then_inc(s.ln_var, 1)


def layer_norm_end(dve, nc, n, b, s):
    dve.wait_ge(s.ln_root, n + 1)
    nc.vector.tensor_tensor(b.xn[:], b.xc[:], spread(b.rstd[:], 2, D), ALU.mult).then_inc(s.ln_done, 1)


def layer_norm_root(pool, nc, n, b, s):
    pool.wait_ge(s.ln_var, n + 1)
    nc.gpsimd.tensor_tensor(b.rstd[:], b.var[:], b.minus_half[:], ALU.pow).then_inc(s.ln_root, 1)


LN_SEMS = "ln_sum ln_centred ln_squared ln_sumsq ln_var ln_root ln_done half_set "


def layer_norm_buffers(part, ns):
    return named(sum=part.sb("ln_sum", [P, ns]), var=part.sb("ln_var", [P, ns]),
                           rstd=part.sb("ln_rstd", [P, ns]), minus_half=part.sb("ln_minus_half", [P, ns]),
                           xc=part.sb("ln_xc", [P, ns, D]), sq=part.sb("ln_sq", [P, ns, D]),
                           xn=part.sb("ln_xn", [P, ns, D]))


def tokenise(nc, A, h, PS, early):
    with ExitStack() as ctx:
        p = Part(nc, ctx, "tok")
        w1 = p.sb("w1", [P, P])
        w2 = p.sb("w2", [96, P])
        w3 = p.sb("w3", [P, 2, 4, P])
        wq = p.sb("wq", [P, P])
        wk = p.sb("wk", [P, 2, P])
        wv = p.sb("wv", [P, P])
        bqk = p.sb("bqk", [P, 3])
        bv = p.sb("bv", [P, P])
        gamma = p.sb("gamma", [P, 1])
        ident = p.sb("ident", [P, P])
        cols = p.sb("cols", [P, 5, 3])
        scale = p.sb("scale", [P, 3])
        veps = p.sb("veps", [P, 3])
        root = p.sb("root", [P, 3])
        half3 = p.sb("half3", [P, 3])
        shift = p.sb("shift", [P, 3])
        warm = p.sb("warm", [P, 1])
        xin = p.sb("xin", [P, 2, LEN])
        h1raw = p.sb("h1raw", [P, L1_LEN])
        h1 = p.sb("h1", [P, L1_LEN + 2])
        taps = p.sb("taps", [96, GP, L1_LEN])
        h2raw = p.sb("h2raw", [P, GP, L2_LEN])
        h2 = p.sb("h2", [P, GP, L2_LEN])
        q = p.sb("q", [P, GP, L2_LEN])
        keys = p.sb("keys", [P, GP, 2, L2_LEN])
        vT = p.sb("vT", [P, GP, P])
        prob = p.sb("prob", [P, 2 * GP, L2_LEN])
        probT = p.sb("probT", [P, 2 * GP, L2_LEN])
        nmax = p.sb("nmax", [P, 2 * GP])
        total = p.sb("total", [P, 2 * GP])
        h3 = p.sb("h3", [P, GP, L2_LEN + 2])
        s = p.sems("weights half_set veps root scale rows folded shift0 shift edges_a edges_b warm "
                   "h1 h2 q_psum k_psum q k e v_psum v nmax exp recip norm pT probT out h3 c3 done taps")
        x_in = [p.sem(f"x_in{j}") for j in range(2)]
        conv1_psum = [p.sem(f"conv1_psum{j}") for j in range(2)]
        pool1 = [p.sem(f"pool1_{j}") for j in range(2)]
        conv2 = [p.sem(f"conv2_{j}") for j in range(2)]
        pool2 = [p.sem(f"pool2_{j}") for j in range(2)]
        loads = [(w1[:], A.c1_w), (w2[:], A.c2_w), (w3[:], A.c3_w), (wq[:], A.tok_wq), (wk[:], A.tok_wk),
                 (wv[:], A.tok_wv), (bqk[:], A.tok_bqk), (bv[:], A.tok_bv), (gamma[:], A.gamma),
                 (ident[:], A.ident), (cols[:], A.norm_cols)]
        CONV2_AT = (6, 8, 9, 10)
        CH = LEN // 512

        def run(eng, step):
            def turn(n, j, loaded):
                for k in range(CH + GP):
                    step(n, j, k, loaded)
            turn(-2, 0, 0)
            turn(-1, 1, 0)
            turn(0, 0, 1)
            turn(1, 1, 1)
            with eng.Fori(1, GROUPS // 2 - 1) as i:
                turn(2 * i, 0, i + 1)
                turn(2 * i + 1, 1, i + 1)
            turn(GROUPS - 2, 0, GROUPS // 2)
            turn(GROUPS - 1, 1, GROUPS // 2)

        def there(n):
            return not isinstance(n, int) or 0 <= n < GROUPS

        with nc.Block() as block:
            @block.sync
            def _(sp):
                for dst, src in loads:
                    sp.dma_start(dst, src).then_inc(s.weights, 16)
                sp.wait_ge(s.edges_a, 1)

                def load(n, j):
                    rows = A.x_rows[bass.ds(n * 16, 16), :]
                    sp.dma_start(xin[0:16, j, 1:LEN], rows[:, 0:LEN - 1]).then_inc(x_in[j], 16)
                    sp.dma_start(xin[16:32, j, :], rows).then_inc(x_in[j], 16)
                    sp.dma_start(xin[32:48, j, 0:LEN - 1], rows[:, 1:LEN]).then_inc(x_in[j], 16)

                def stack():
                    for g in range(GP):
                        for tap in range(3):
                            sp.dma_start(taps[32 * tap:32 * tap + 32, g, :], h1[32 * g:32 * g + 32, tap:tap + L1_LEN])\
                                .then_inc(s.taps, 16)

                load(0, 0)
                load(1, 1)
                for weights in early:
                    for dst, src in weights.loads:
                        sp.dma_start(dst, src).then_inc(weights.loaded, 16)
                sp.wait_ge(s.h1, 1)
                stack()
                with sp.Fori(1, GROUPS // 2) as i:
                    for j in range(2):
                        sp.wait_ge(conv1_psum[1], (2 * i + j - 1) * (CH // 2))
                        load(2 * i + j, j)
                        sp.wait_ge(pool2[1], (2 * i + j - 1) * (GP // 2))
                        stack()
                sp.wait_ge(pool2[1], (GROUPS - 1) * (GP // 2))
                stack()

            @block.gpsimd
            def _(pool):
                nc.gpsimd.memset(half3[:], -0.5).then_inc(s.half_set, 1)
                nc.gpsimd.memset(h1[:], 0.0).then_inc(s.edges_b, 1)
                nc.gpsimd.memset(h3[:], 0.0).then_inc(s.edges_b, 1)
                pool.wait_ge(s.half_set, 1)
                pool.wait_ge(s.veps, 1)
                nc.gpsimd.tensor_tensor(root[:], veps[:], half3[:], ALU.pow).then_inc(s.root, 1)

            @block.vector
            def _(dve):
                nc.vector.memset(xin[:], 0.0).then_inc(s.edges_a, 1)
                dve.wait_ge(s.weights, 16 * len(loads))
                nc.vector.tensor_scalar(veps[:], cols[:, 4, :], EPS, None, ALU.add).then_inc(s.veps, 1)
                dve.wait_ge(s.root, 1)
                nc.vector.tensor_tensor(scale[:], cols[:, 1, :], root[:], ALU.mult).then_inc(s.scale, 1)
                dve.wait_ge(s.scale, 1)
                nc.vector.tensor_tensor(shift[:], cols[:, 0, :], cols[:, 3, :], ALU.subtract).then_inc(s.shift0, 1)
                dve.wait_ge(s.shift0, 1)
                nc.vector.tensor_tensor(shift[:], shift[:], scale[:], ALU.mult).then_inc(s.shift0, 1)
                dve.wait_ge(s.shift0, 2)
                nc.vector.tensor_tensor(shift[:], shift[:], cols[:, 2, :], ALU.add).then_inc(s.shift, 1)
                dve.wait_ge(s.rows, 1)
                nc.vector.tensor_tensor(w1[:], w1[:], PS[:, 0, 0:P], ALU.mult).then_inc(s.folded, 1)
                nc.vector.tensor_tensor(w2[:], w2[:], PS[0:96, 1, 0:P], ALU.mult).then_inc(s.folded, 1)
                w3v = w3[:].rearrange("p b t c -> p (b t) c")
                nc.vector.tensor_tensor(w3v, w3v, spread(PS[:, 2, 0:P], 1, 8), ALU.mult).then_inc(s.folded, 1)

                def step(n, j, k, loaded):
                    c, f = n + 2, n + 1
                    if there(c) and k < CH:
                        dve.wait_ge(conv1_psum[k % 2], c * (CH // 2) + k // 2 + 1)
                        if k == 0:
                            dve.wait_ge(s.h1, c)
                        nc.vector.tensor_reduce(h1raw[:, k * 64:(k + 1) * 64], PS[:, k % 2, :].rearrange(
                            "p (a b) -> p a b", b=POOL1), AX.X, ALU.max).then_inc(pool1[k % 2], 1)
                    if there(f) and k in CONV2_AT:
                        g = CONV2_AT.index(k)
                        dve.wait_ge(conv2[g % 2], f * (GP // 2) + g // 2 + 1)
                        if g == 0:
                            dve.wait_ge(s.h2, f)
                        if g == GP - 1 and there(c):
                            dve.wait_ge(s.h1, c + 1)
                        nc.vector.tensor_reduce(h2raw[:, g, :], PS[:, 2 + g % 2, :].rearrange("p (a b) -> p a b", b=POOL2),
                                                AX.X, ALU.max).then_inc(pool2[g % 2], 1)
                    if not there(n):
                        return
                    if k in (1, 2):
                        b = k - 1
                        dve.wait_ge(s.k_psum, 2 * n + b + 1)
                        nc.vector.tensor_scalar(keys[:, :, b, :], PS[:, 5 - b, :].rearrange("p (g t) -> p g t", g=GP),
                                                bqk[:, 1 + b:2 + b], None, ALU.add).then_inc(s.k, 1)
                    if k == 4:
                        dve.wait_ge(s.e, n + 1)
                        nc.vector.tensor_reduce(nmax[:], PS[:, 6:8, :].rearrange("p a (b c) -> p (a b) c", b=GP), AX.X,
                                                ALU.max, negate=True).then_inc(s.nmax, 1)
                    if k == 7:
                        dve.wait_ge(s.exp, n + 1)
                        nc.vector.reciprocal(total[:], total[:]).then_inc(s.recip, 1)
                        dve.wait_ge(s.recip, n + 1)
                        nc.vector.tensor_tensor(prob[:], prob[:], spread(total[:], 2, L2_LEN), ALU.mult)\
                            .then_inc(s.norm, 1)
                        dve.wait_ge(s.v_psum, n + 1)
                        nc.vector.tensor_tensor(vT[:], PS[:, 5, :].rearrange("p (a b) -> p a b", a=GP),
                                                spread(bv[:], 1, GP), ALU.add).then_inc(s.v, 1)
                    if k == 10:
                        dve.wait_ge(s.out, n + 1)
                        nc.vector.scalar_tensor_tensor(
                            out=h3[:, :, 1:L2_LEN + 1], in0=PS[:, 5, :].rearrange("p (a b) -> p a b", a=GP),
                            scalar=gamma[:, 0:1], in1=h2[:], op0=ALU.mult, op1=ALU.add).then_inc(s.h3, 1)

                run(dve, step)

            @block.scalar
            def _(act):
                act.wait_ge(s.edges_b, 2)
                nc.scalar.activation(warm[:], h1[:, 0:1], ACT.Exp).then_inc(s.warm, 1)
                act.wait_ge(s.shift, 1)

                def step(n, j, k, loaded):
                    c = n + 2
                    if there(n) and k == 0:
                        act.wait_ge(pool2[0], (n + 1) * (GP // 2))
                        act.wait_ge(pool2[1], (n + 1) * (GP // 2))
                        act.wait_ge(s.h3, n)
                        nc.scalar.activation(h2[:], h2raw[:], ACT.Relu, bias=shift[:, 1:2]).then_inc(s.h2, 1)
                    if there(n) and k == 1:
                        act.wait_ge(s.q_psum, n + 1)
                        nc.scalar.activation(q[:].rearrange("p a b -> p (a b)"), PS[:, 4, :], ACT.Identity,
                                             bias=bqk[:, 0:1]).then_inc(s.q, 1)
                    if there(n) and k == 5:
                        act.wait_ge(s.nmax, n + 1)
                        for m in range(2 * GP):
                            last = nc.scalar.activation(prob[:, m, :], PS[:, 6 + m // 4, (m % 4) * L2_LEN:(m % 4 + 1) * L2_LEN],
                                                        ACT.Exp, bias=nmax[:, m:m + 1], accum_out=total[:, m:m + 1])
                        last.then_inc(s.exp, 1)
                    if there(c) and k == CH - 1:
                        act.wait_ge(pool1[0], (c + 1) * (CH // 2))
                        act.wait_ge(pool1[1], (c + 1) * (CH // 2))
                        act.wait_ge(s.taps, 16 * 3 * GP * c)
                        nc.scalar.activation(h1[:, 1:L1_LEN + 1], h1raw[:], ACT.Relu, bias=shift[:, 0:1])\
                            .then_inc(s.h1, 1)
                    if there(n) and k == 9:
                        act.wait_ge(s.pT, n + 1)
                        nc.scalar.activation(probT[:], PS[:, 6:8, :].rearrange("p a (b c) -> p (a b) c", b=GP),
                                             ACT.Copy).then_inc(s.probT, 1)
                    if there(n) and k == 11:
                        act.wait_ge(s.c3, n + 1)
                        hv = h[:, bass.ds(n * GROUP, GROUP), :].rearrange("p (g b) d -> p b g d", b=2)
                        nc.scalar.activation(hv, PS[:, 4, :].rearrange("p (b g d) -> p b g d", b=2, g=GP),
                                             ACT.Identity, bias=shift[:, 2:3]).then_inc(s.done, 1)

                run(act, step)

            @block.tensor
            def _(pe):
                pe.wait_ge(s.weights, 16 * len(loads))
                pe.wait_ge(s.scale, 1)
                for m in range(3):
                    mm = nc.tensor.matmul(PS[:, m, 0:P], scale[:, m:m + 1].broadcast_to([P, P]), ident[:],
                                          start=True, stop=True)
                mm.then_inc(s.rows, 1)
                pe.wait_ge(s.folded, 3)
                pe.wait_ge(s.edges_b, 2)

                def step(n, j, k, loaded):
                    c, f = n + 2, n + 1
                    if there(c) and k < CH:
                        if k == 0:
                            pe.wait_ge(x_in[j], 48 * (loaded + 1))
                        pe.wait_ge(pool1[k % 2], c * (CH // 2) + k // 2)
                        mm = nc.tensor.matmul(PS[:, k % 2, :], w1[:], xin[:, j, k * 512:(k + 1) * 512], start=True, stop=True)
                        mm.then_inc(conv1_psum[k % 2], 1)
                    h2f = h2[:].rearrange("p a b -> p (a b)")
                    if there(n) and k == 1:
                        pe.wait_ge(s.h2, n + 1)
                        pe.wait_ge(s.done, n)
                        nc.tensor.matmul(PS[:, 4, :], wq[:], h2f, start=True, stop=True).then_inc(s.q_psum, 1)
                        nc.tensor.matmul(PS[:, 5, :], wk[:, 0, :], h2f, start=True, stop=True).then_inc(s.k_psum, 1)
                    if there(n) and k == 2:
                        pe.wait_ge(s.q, n + 1)
                        nc.tensor.matmul(PS[:, 4, :], wk[:, 1, :], h2f, start=True, stop=True).then_inc(s.k_psum, 1)
                    if there(n) and k == 3:
                        pe.wait_ge(s.k, 2 * n + 2)
                        pe.wait_ge(s.probT, n)
                        for g in range(GP):
                            mm = nc.tensor.matmul(PS[:, 6 + g // 2, (g % 2) * 256:(g % 2 + 1) * 256], q[:, g, :],
                                                  keys[:, g].rearrange("p b t -> p (b t)"), start=True, stop=True)
                        mm.then_inc(s.e, 1)
                    if there(n) and k == 7:
                        for g in range(GP):
                            mm = nc.tensor.matmul(PS[:, 5, g * P:(g + 1) * P], h2[:, g, :], wv[:], start=True, stop=True)
                        mm.then_inc(s.v_psum, 1)
                    if there(f) and k in CONV2_AT:
                        g = CONV2_AT.index(k)
                        if g == 0:
                            pe.wait_ge(s.taps, 16 * 3 * GP * (f + 1))
                        pe.wait_ge(pool2[g % 2], f * (GP // 2) + g // 2)
                        nc.tensor.matmul(PS[:, 2 + g % 2, :], w2[:], taps[:, g, :], start=True, stop=True)\
                            .then_inc(conv2[g % 2], 1)
                    if there(n) and k == 9:
                        pe.wait_ge(s.norm, n + 1)
                        for m in range(2 * GP):
                            mm = nc.tensor.transpose(PS[:, 6 + m // GP, (m % GP) * P:(m % GP + 1) * P], prob[:, m, :],
                                                     ident[:])
                        mm.then_inc(s.pT, 1)
                    if there(n) and k == 10:
                        pe.wait_ge(s.probT, n + 1)
                        pe.wait_ge(s.v, n + 1)
                        for g in range(GP):
                            for b in range(2):
                                mm = nc.tensor.matmul(PS[64 * b:64 * b + 64, 5, g * P:(g + 1) * P],
                                                      vT[:, g, 64 * b:64 * b + 64], probT[:, 2 * g + b, :],
                                                      start=True, stop=True)
                        mm.then_inc(s.out, 1)
                    if there(n) and k == 11:
                        pe.wait_ge(s.h3, n + 1)
                        for b in range(2):
                            for tap in range(4):
                                mm = nc.tensor.matmul(PS[:, 4, b * 256:(b + 1) * 256], w3[:, b, tap, :],
                                                      h3[:, :, tap:tap + L2_LEN - 1:2], start=(tap == 0), stop=(tap == 3))
                        mm.then_inc(s.c3, 1)

                run(pe, step)
        p.end()


QUADS = 4
KEYS = 16
KGROUPS = TOK // KEYS
HG = 2
HH = HEADS // HG
ROWS = HH * 2
TINY = 1e-30


def on_scalar(u):
    return u in (2, 3, 6, 9, 10, 11, 14, 15)


VECTOR_AT = dict(logits=0, terms=1, v0=3, v1=6, norm=4, norm_end=8, e0=9, e1=16, gate=22, add=23, x=27, q=29)
SCALAR_AT = dict(exp=0, a0=14, a1=17, gate=21)
TENSOR_AT = dict(logits=3, v1=3, e0=6, back0=9, e1=11, back1=15, attend=16, fan=20, x=20, q=24, terms=28, v0=31)
SCALAR_TILES = [u for u in range(KEYS) if on_scalar(u)]
VECTOR_TILES = [u for u in range(KEYS) if not on_scalar(u)]


def heads_diagonal(bank):
    a = bank[:, 0:HH * TOK]
    (pstep, pn), _ = a.ap[0], a.ap[1]
    return bass.AP(tensor=a.tensor, offset=a.offset, ap=[[pstep, pn], [TOK + 2, HH], [ROWS, KEYS], [1, 2]])


def l1_weights(nc, ctx, A):
    p = Part(nc, ctx, "l1w")
    wq = p.sb("wq", [P, HEADS, P])
    wv = p.sb("wv", [P, 2 * HEADS * D])
    bv = p.sb("bv", [P, 2 * HEADS * D])
    fan = p.sb("fan", [P, P])
    fan_b = p.sb("fan_b", [P, P])
    ident = p.sb("ident", [P, P])
    own_key = p.sb("own_key", [P, KEYS])
    wk_rows = p.sb("wk_rows", [P, HEADS * D])
    wk_cols = p.sb("wk_cols", [P, HEADS])
    bq = p.sb("bq", [P, HEADS])
    loads = [(wq[:], A.l1_wq), (wv[:], A.l1_wv), (bv[:], A.l1_bv), (fan[:], A.fan_w), (fan_b[:], A.fan_b),
             (ident[:], A.ident), (own_key[:], A.own_key), (wk_rows[:], A.wk_rows), (wk_cols[:], A.wk_cols),
             (bq[:], A.l1_bq)]
    return named(wq=wq, wv=wv, bv=bv, fan=fan, fan_b=fan_b, ident=ident, own_key=own_key, wk_rows=wk_rows,
                 wk_cols=wk_cols, bq=bq, loads=loads, loaded=p.sem("loaded"))


def l1_attention(nc, A, h, PS, given):
    with ExitStack() as ctx:
        p = Part(nc, ctx, "l1")
        p.mine.append(given.loaded)
        wq, wv, bv, fan, fan_b, ident, own_key, wk_rows, wk_cols, bq = (
            given.wq, given.wv, given.bv, given.fan, given.fan_b, given.ident, given.own_key, given.wk_rows,
            given.wk_cols, given.bq)
        g1 = p.sb("g1", [P, HEADS * D])
        g2 = p.sb("g2", [P, HEADS * D])
        wsum = p.sb("wsum", [P, HG, 3 * ROWS + ROWS + 3 * ROWS])
        wall = p.sb("wall", [P, HG, KEYS * ROWS])
        warm = p.sb("warm", [P, 1])
        ln = layer_norm_buffers(p, 2)
        xT = p.sb("xT", [P, 2, TOK])
        nxT = p.sb("nxT", [P, 2, TOK])
        xpad = p.sb("xpad", [P, 2, 2, TOK])
        qs = p.sb("qs", [P, 2, HEADS * TOK])
        tiles = p.sb("tiles", [P, KEYS, HEADS * TOK])
        qterm = p.sb("qterm", [P, 2, HG, TOK])
        qsum = p.sb("qsum", [P, HG, P])
        qsum_b = p.sb("qsum_b", [P, HG])
        ones = p.sb("ones", [P, 2])
        xprod = p.sb("xprod", [P, HG * KGROUPS, KEYS])
        xterm = p.sb("xterm", [P, 2, HG * KGROUPS])
        v = p.sb("v", [P, 2, 2, 2 * HEADS * D])
        logit = p.sb("logit", [P, 2, HG, HH * TOK])
        e = p.sb("e", [P, 2, 2, HEADS, TOK])
        eT = p.sb("eT", [P, 2, HEADS, TOK])
        den = p.sb("den", [P, 2, HEADS])
        sig = p.sb("sig", [P, TOK])
        yT = p.sb("yT", [P, TOK])
        z = p.sb("z", [P, 2 * D])
        s = p.sems(LN_SEMS + "guard folded zeroed warm xres wqT_psum wqT bias_prod qsum_psum qsum "
                   "tile_vector tile_scalar x_psum x q_psum q qterm xterm_psum xprod xterm "
                   "v_psum v eT_psum den0 den1 den eT a_psum a sig_exp sig1 sig yT z_psum z added")
        used = [p.sem(f"quad_used{m}") for m in range(QUADS)]
        logit_done = [p.sem(f"logit_done{m}") for m in range(2)]
        lT_psum = [[p.sem(f"lT_psum{m}{g}") for g in range(HG)] for m in range(2)]
        e_done = [p.sem(f"e_done{m}") for m in range(HG)]
        o_psum = [p.sem(f"o_psum{m}") for m in range(2)]
        T = TOK

        def body(step):
            def pair_steps(prev, this, nxt):
                for at in range(KGROUPS * QUADS):
                    step(at, prev, this, nxt)
            return pair_steps

        def run(eng, steps):
            steps(None, (0, 0, 0), (1, 1, 0))

            def two(i):
                steps((2 * i, 0, i), (2 * i + 1, 1, i), (2 * i + 2, 0, i + 1))
                steps((2 * i + 1, 1, i), (2 * i + 2, 0, i + 1), (2 * i + 3, 1, i + 1))
            two(0)
            with eng.Fori(1, PAIRS // 2 - 1) as i:
                two(i)
            k = PAIRS // 2 - 1
            steps((2 * k, 0, k), (2 * k + 1, 1, k), None)
            steps((2 * k + 1, 1, k), None, None)

        with nc.Block() as block:
            @block.gpsimd
            def _(pool):
                nc.gpsimd.memset(ln.minus_half[:], -0.5).then_inc(s.half_set, 1)
                nc.gpsimd.memset(wsum[:], 0.0).then_inc(s.zeroed, 1)
                nc.gpsimd.memset(wall[:], 0.0).then_inc(s.zeroed, 1)
                nc.gpsimd.memset(xpad[:], 0.0).then_inc(s.zeroed, 1)
                nc.gpsimd.memset(ones[:], 1.0).then_inc(s.zeroed, 1)
                pool.wait_ge(s.half_set, 1)
                with pool.Fori(0, PAIRS) as n:
                    layer_norm_root(pool, nc, n, ln, s)

            @block.vector
            def _(dve):
                dve.wait_ge(given.loaded, 16 * len(given.loads))
                dve.wait_ge(s.zeroed, 4)
                step = 0
                for w, width in ((wk_rows, HEADS * D), (wk_cols, HEADS)):
                    a, b = g1[:, 0:width], g2[:, 0:width]
                    nc.vector.tensor_scalar(a, w[:], -1.0, None, ALU.mult).then_inc(s.guard, 1)
                    dve.wait_ge(s.guard, step + 1)
                    nc.vector.tensor_tensor(a, a, w[:], ALU.max).then_inc(s.guard, 1)
                    dve.wait_ge(s.guard, step + 2)
                    nc.vector.tensor_scalar(b, a, TINY, None, ALU.is_ge).then_inc(s.guard, 1)
                    dve.wait_ge(s.guard, step + 3)
                    nc.vector.tensor_tensor(w[:], w[:], b, ALU.mult).then_inc(s.guard, 1)
                    dve.wait_ge(s.guard, step + 4)
                    nc.vector.tensor_scalar(b, a, TINY, TINY, ALU.is_lt, ALU.mult).then_inc(s.guard, 1)
                    dve.wait_ge(s.guard, step + 5)
                    nc.vector.tensor_tensor(w[:], w[:], b, ALU.add).then_inc(s.guard, 1)
                    dve.wait_ge(s.guard, step + 6)
                    nc.vector.tensor_tensor(a, a, b, ALU.max).then_inc(s.guard, 1)
                    nc.vector.reciprocal(w[:], w[:]).then_inc(s.guard, 1)
                    dve.wait_ge(s.guard, step + 8)
                    step += 8
                nc.vector.tensor_tensor(wq[:].rearrange("p h (b w) -> p h b w", b=2),
                                        wq[:].rearrange("p h (b w) -> p h b w", b=2),
                                        spread(wk_rows[:].rearrange("p (h w) -> p h w", h=HEADS), 2, 2),
                                        ALU.mult).then_inc(s.folded, 1)
                nc.vector.tensor_tensor(bq[:], bq[:], wk_cols[:], ALU.mult).then_inc(s.folded, 1)
                absk = g1[:, 0:HEADS].rearrange("p (g h) -> p g h", g=HG)
                for b in range(2):
                    rows = slice(64 * b, 64 * b + 64)
                    nc.vector.tensor_scalar(wsum[rows, :, 3 * ROWS + b:4 * ROWS:2], absk[rows], -0.25, None,
                                            ALU.mult).then_inc(s.folded, 1)
                    dst = wall[rows].rearrange("p g (v h b) -> p g v h b", v=KEYS, b=2)[:, :, :, :, b]
                    for g in range(HG):
                        nc.vector.tensor_scalar(dst[:, g], spread(absk[rows, g], 1, KEYS), 0.125, None,
                                                ALU.mult).then_inc(s.folded, 1)
                dve.wait_ge(s.folded, 8)
                dve.wait_ge(s.wqT_psum, 1)
                nc.vector.tensor_copy(tiles[:, 0, :], PS[:, 0:2, :].rearrange("p a c -> p (a c)")).then_inc(s.wqT, 1)
                for g in range(HG):
                    rows = lambda ap: ap.rearrange("p (v h b) -> p v h b", h=HH, b=2)
                    for b in range(2):
                        nc.vector.tensor_tensor(
                            rows(tiles[:, 1, g * P:(g + 1) * P])[:, :, :, b], rows(wall[:, g, :])[:, :, :, b],
                            spread(bq[:, g * HH:(g + 1) * HH], 1, KEYS), ALU.mult).then_inc(s.bias_prod, 1)
                dve.wait_ge(s.qsum_psum, 1)
                nc.vector.tensor_copy(qsum[:].rearrange("p a c -> p (a c)"), PS[:, 2, 0:HG * P]).then_inc(s.qsum, 1)
                nc.vector.tensor_copy(qsum_b[:], PS[:, 3, 0:2 * HG:2]).then_inc(s.qsum, 1)
                dve.wait_ge(s.qsum, 2)

                def normalise_1(n):
                    hp = h[:, bass.ds(n * 2, 2), :]
                    layer_norm_start(dve, nc, n, hp, ln, s)

                def normalise_2(n):
                    dve.wait_ge(s.x_psum, n)
                    layer_norm_end(dve, nc, n, ln, s)
                    dve.wait_ge(s.ln_done, n + 1)
                    hp = h[:, bass.ds(n * 2, 2), :]
                    nc.vector.tensor_tensor(hp, hp, ln.xn[:], ALU.add).then_inc(s.xres, 1)

                def take_x(n, j):
                    dve.wait_ge(s.x_psum, n + 1)
                    nc.vector.tensor_copy(xT[:, j, :], PS[:, 7, 0:T])
                    nc.vector.tensor_scalar(nxT[:, j, :], PS[:, 7, 0:T], -1.0, None, ALU.mult)
                    nc.vector.tensor_copy(xpad[0:64, j, 0, :], PS[0:64, 7, 0:T])
                    nc.vector.tensor_copy(xpad[64:128, j, 1, :], PS[64:128, 7, 0:T]).then_inc(s.x, 1)

                def take_q(n, j):
                    dve.wait_ge(s.q_psum, n + 1)
                    nc.vector.tensor_tensor(
                        qs[:, j, :].rearrange("p (h t) -> p h t", h=HEADS),
                        PS[:, 6:8, :].rearrange("p a (h t) -> p (a h) t", t=T), spread(bq[:], 2, T), ALU.add)\
                            .then_inc(s.q, 1)

                def take_terms(n, j):
                    dve.wait_ge(s.xterm_psum, n + 1)
                    for g in range(HG):
                        nc.vector.tensor_scalar(qterm[:, j, g, :], PS[:, 6, g * T:(g + 1) * T], qsum_b[:, g:g + 1], None,
                                                ALU.add).then_inc(s.qterm, 1)
                    nc.vector.tensor_tensor(xprod[:], PS[:, 6, HG * T:2 * HG * T].rearrange("p (a v) -> p a v", v=KEYS),
                                            spread(own_key[:], 1, HG * KGROUPS), ALU.mult).then_inc(s.xprod, 1)
                    dve.wait_ge(s.xprod, n + 1)
                    nc.vector.tensor_reduce(xterm[:, j, :], xprod[:], AX.X, ALU.add).then_inc(s.xterm, 1)

                def take_v(n, j, b):
                    dve.wait_ge(s.v_psum, 2 * n + b + 1)
                    nc.vector.tensor_tensor(v[:, j, b, :], PS[:, 6:8, :].rearrange("p a c -> p (a c)"), bv[:], ALU.add)\
                        .then_inc(s.v, 1)

                def take_logits(n, j, k, g):
                    gs = g % 2
                    dve.wait_ge(used[QUADS - 1], n * KGROUPS + g + 1)
                    dve.wait_ge(s.qterm, HG * (n + 1))
                    dve.wait_ge(s.xterm, n + 1)
                    for hg in range(HG):
                        dve.wait_ge(lT_psum[gs][hg], n * (KGROUPS // 2) + g // 2)
                        nc.vector.scalar_tensor_tensor(
                            out=logit[:, gs, hg, :].rearrange("p (h t) -> p h t", t=T),
                            in0=PS[:, 2 * gs + hg, :].rearrange("p (h t) -> p h t", t=T),
                            scalar=xterm[:, j, hg * KGROUPS + g:hg * KGROUPS + g + 1],
                            in1=spread(qterm[:, j, hg, :], 1, HH),
                            op0=ALU.subtract, op1=ALU.add).then_inc(logit_done[gs], 1)

                def take_eT(n, b):
                    dve.wait_ge(s.eT_psum, 2 * n + b + 1)
                    et = PS[:, 6:8, :].rearrange("p a (h t) -> p (a h) t", t=T)
                    nc.vector.tensor_reduce(den[:, b, :], et, AX.X, ALU.add).then_inc(s.den0, 1)
                    dve.wait_ge(s.den0, 2 * n + b + 1)
                    nc.vector.tensor_scalar(den[:, b, :], den[:, b, :], 1.0, None, ALU.add).then_inc(s.den1, 1)
                    dve.wait_ge(s.den1, 2 * n + b + 1)
                    nc.vector.reciprocal(den[:, b, :], den[:, b, :]).then_inc(s.den, 1)
                    dve.wait_ge(s.den, 2 * n + b + 1)
                    nc.vector.tensor_tensor(eT[:, b], et, spread(den[:, b, :], 2, T), ALU.mult).then_inc(s.eT, 1)

                def gate(n, j, k):
                    dve.wait_ge(s.sig_exp, n + 1)
                    nc.vector.tensor_scalar(sig[:], sig[:], 1.0, None, ALU.add).then_inc(s.sig1, 1)
                    dve.wait_ge(s.sig1, n + 1)
                    nc.vector.reciprocal(sig[:], sig[:]).then_inc(s.sig, 1)
                    dve.wait_ge(s.sig, n + 1)
                    nc.vector.tensor_tensor(yT[:], PS[:, 6, 0:T], sig[:], ALU.mult).then_inc(s.yT, 1)

                def add_up(n):
                    dve.wait_ge(s.z_psum, n + 1)
                    nc.vector.tensor_tensor(z[:], PS[:, 6, 0:2 * D], fan_b[:], ALU.add).then_inc(s.z, 1)
                    dve.wait_ge(s.z, n + 1)
                    hp = h[:, bass.ds(n * 2, 2), :]
                    nc.vector.tensor_tensor(hp, hp, z[:].rearrange("p (b w) -> p b w", b=2), ALU.add)\
                        .then_inc(s.added, 1)

                def step(at, prev, this, nxt):
                    g, m = at // QUADS, at % QUADS
                    if prev and at == VECTOR_AT['logits']:
                        take_logits(*prev, KGROUPS - 2)
                    if prev and at == VECTOR_AT['logits'] + QUADS:
                        take_logits(*prev, KGROUPS - 1)
                    if this and at >= 2 * QUADS and m == VECTOR_AT['logits']:
                        take_logits(*this, g - 2)
                    if this and at == VECTOR_AT['terms']:
                        take_terms(this[0], this[1])
                    if this and at == VECTOR_AT['v0']:
                        take_v(this[0], this[1], 0)
                    if this and at == VECTOR_AT['v1']:
                        take_v(this[0], this[1], 1)
                    if nxt and at == VECTOR_AT['norm']:
                        normalise_1(nxt[0])
                    if nxt and at == VECTOR_AT['norm_end']:
                        normalise_2(nxt[0])
                    if prev and at == VECTOR_AT['e0']:
                        take_eT(prev[0], 0)
                    if prev and at == VECTOR_AT['e1']:
                        take_eT(prev[0], 1)
                    if prev and at == VECTOR_AT['gate']:
                        gate(*prev)
                    if prev and at == VECTOR_AT['add']:
                        add_up(prev[0])
                    if nxt and at == VECTOR_AT['x']:
                        take_x(nxt[0], nxt[1])
                    if nxt and at == VECTOR_AT['q']:
                        take_q(nxt[0], nxt[1])
                    if this:
                        n, j, _ = this
                        mine = [c for c in range(4) if 4 * m + c in VECTOR_TILES]
                        dve.wait_ge(used[m], n * KGROUPS + g)
                        for c in mine:
                            key = g * KEYS + 4 * c + m
                            nc.vector.tensor_scalar(tiles[:, 4 * m + c, :], qs[:, j, :], xT[:, j, key:key + 1], 0.0,
                                                    ALU.subtract, ALU.max).then_inc(s.tile_vector, 1)

                normalise_1(0)
                normalise_2(0)
                take_x(0, 0)
                take_q(0, 0)
                dve.wait_ge(s.x, 1)
                dve.wait_ge(s.q, 1)
                run(dve, body(step))

            @block.scalar
            def _(act):
                act.wait_ge(s.zeroed, 4)
                nc.scalar.activation(warm[:], wsum[:, 0, 0:1], ACT.Exp).then_inc(s.warm, 1)

                def exponentials(n, j, k, g):
                    if g == 0:
                        act.wait_ge(o_psum[j], k)
                    for hg in range(HG):
                        act.wait_ge(lT_psum[g % 2][hg], n * (KGROUPS // 2) + g // 2 + 1)
                        dst = e[:, j, :, hg * HH:(hg + 1) * HH, g * KEYS:(g + 1) * KEYS]
                        nc.scalar.activation(dst.rearrange("p b h t -> p h t b"), heads_diagonal(PS[:, 4 + hg, :]),
                                             ACT.Exp).then_inc(e_done[hg], 1)

                def take_a(n, j, b):
                    act.wait_ge(s.a_psum, 2 * n + b + 1)
                    nc.scalar.activation(e[:, j, b], PS[:, 6:8, :].rearrange("p a (h t) -> p (a h) t", t=T), ACT.Copy)\
                        .then_inc(s.a, 1)

                def gate_exp(n, j, k):
                    act.wait_ge(o_psum[j], k + 1)
                    nc.scalar.activation(sig[:], PS[:, 6, 0:T], ACT.Exp, scale=-1.702).then_inc(s.sig_exp, 1)

                def step(at, prev, this, nxt):
                    g, m = at // QUADS, at % QUADS
                    if prev and at in (SCALAR_AT['exp'], SCALAR_AT['exp'] + QUADS, SCALAR_AT['exp'] + 2 * QUADS):
                        exponentials(*prev, KGROUPS - 3 + g)
                    if this and at >= 3 * QUADS and m == SCALAR_AT['exp']:
                        exponentials(*this, g - 3)
                    if prev and at in (SCALAR_AT['a0'], SCALAR_AT['a1']):
                        take_a(prev[0], prev[1], int(at == SCALAR_AT['a1']))
                    if prev and at == SCALAR_AT['gate']:
                        gate_exp(*prev)
                    if this:
                        n, j, _ = this
                        if at == 0:
                            act.wait_ge(s.x, n + 1)
                            act.wait_ge(s.q, n + 1)
                        mine = [c for c in range(4) if 4 * m + c in SCALAR_TILES]
                        act.wait_ge(used[m], n * KGROUPS + g)
                        for c in mine:
                            key = g * KEYS + 4 * c + m
                            nc.scalar.activation(tiles[:, 4 * m + c, :], qs[:, j, :], ACT.Relu,
                                                 bias=nxT[:, j, key:key + 1]).then_inc(s.tile_scalar, 1)

                run(act, body(step))

            @block.tensor
            def _(pe):
                pe.wait_ge(given.loaded, 16 * len(given.loads))
                pe.wait_ge(s.folded, 8)
                for hh in range(HEADS):
                    mm = nc.tensor.transpose(PS[:, hh // 4, (hh % 4) * P:(hh % 4 + 1) * P], wq[:, hh, :], ident[:])
                mm.then_inc(s.wqT_psum, 1)
                pe.wait_ge(s.wqT, 1)
                pe.wait_ge(s.bias_prod, 2 * HG)
                for hh in range(HEADS):
                    mine = lambda ap: ap.rearrange("p (v h b) -> p v h b", h=HH, b=2)[:, :, hh % HH, :]
                    hg = hh // HH
                    nc.tensor.matmul(mine(PS[:, 2, hg * P:(hg + 1) * P]), tiles[:, 0, hh * P:(hh + 1) * P],
                                     mine(wall[:, hg, :]), start=True, stop=True)
                for hg in range(HG):
                    mm = nc.tensor.matmul(PS[:, 3, 2 * hg:2 * hg + 2], tiles[:, 1, hg * P:(hg + 1) * P], ones[:],
                                          start=True, stop=True)
                mm.then_inc(s.qsum_psum, 1)

                def quad(n, g, m):
                    vdone = sum(u < 4 * m + 4 for u in VECTOR_TILES)
                    sdone = sum(u < 4 * m + 4 for u in SCALAR_TILES)
                    pe.wait_ge(s.tile_vector, (n * KGROUPS + g) * len(VECTOR_TILES) + vdone)
                    pe.wait_ge(s.tile_scalar, (n * KGROUPS + g) * len(SCALAR_TILES) + sdone)
                    gs = g % 2
                    if m == 0:
                        pe.wait_ge(logit_done[gs], (n * (KGROUPS // 2) + g // 2) * HG)
                    for hg in range(HG):
                        for c in range(4):
                            mm = nc.tensor.matmul(
                                PS[32 * c:32 * c + 32, 2 * gs + hg, :],
                                wsum[:, hg, (3 - m) * ROWS:(7 - m) * ROWS],
                                tiles[:, 4 * m + c, hg * HH * T:(hg + 1) * HH * T], start=(m == 0), stop=(m == QUADS - 1))
                    mm.then_inc(used[m], 1)

                def transpose_logits(n, j, k, g):
                    gs = g % 2
                    for hg in range(HG):
                        pe.wait_ge(logit_done[gs], (n * (KGROUPS // 2) + g // 2) * HG + hg + 1)
                        pe.wait_ge(e_done[hg], n * KGROUPS + g)
                        for hh in range(HH):
                            mm = nc.tensor.transpose(PS[:, 4 + hg, hh * T:(hh + 1) * T],
                                                     logit[:, gs, hg, hh * T:(hh + 1) * T], ident[:])
                        mm.then_inc(lT_psum[gs][hg], 1)

                def make_x(n):
                    pe.wait_ge(s.ln_done, n + 1)
                    nc.tensor.transpose(PS[:, 7, 0:T], ln.xn[:].rearrange("p b w -> p (b w)"), ident[:])\
                        .then_inc(s.x_psum, 1)

                def make_q(n, j):
                    pe.wait_ge(s.x, n + 1)
                    for hh in range(HEADS):
                        mm = nc.tensor.matmul(PS[:, 6 + hh // 4, (hh % 4) * T:(hh % 4 + 1) * T], wq[:, hh, :],
                                              xT[:, j, :], start=True, stop=True)
                    mm.then_inc(s.q_psum, 1)

                def make_terms(n, j):
                    pe.wait_ge(s.q, n + 1)
                    for m, w in enumerate((qsum, wall)):
                        for hg in range(HG):
                            a = (m * HG + hg) * T
                            mm = nc.tensor.matmul(PS[:, 6, a:a + T], w[:, hg, :], xT[:, j, :], start=True, stop=True)
                    mm.then_inc(s.xterm_psum, 1)

                def make_v(n, j, b):
                    if b == 0:
                        pe.wait_ge(s.xprod, n + 1)
                    else:
                        pe.wait_ge(s.v, 2 * n + 1)
                    for c in range(2):
                        mm = nc.tensor.matmul(PS[:, 6 + c, :], xpad[:, j, b, :],
                                              wv[:, c * HEADS * D:(c + 1) * HEADS * D],
                                              start=True, stop=True)
                    mm.then_inc(s.v_psum, 1)

                def transpose_e(n, j, b):
                    if b == 0:
                        for hg in range(HG):
                            pe.wait_ge(e_done[hg], (n + 1) * KGROUPS)
                        pe.wait_ge(s.v, 2 * n + 4 if not is_last(n) else 2 * n + 2)
                    else:
                        pe.wait_ge(s.a, 2 * n + 1)
                    for hh in range(HEADS):
                        mm = nc.tensor.transpose(PS[:, 6 + hh // 4, (hh % 4) * T:(hh % 4 + 1) * T], e[:, j, b, hh, :],
                                                 ident[:])
                    mm.then_inc(s.eT_psum, 1)

                def is_last(n):
                    return isinstance(n, int) and n == PAIRS - 1

                def transpose_back(n, b):
                    pe.wait_ge(s.eT, 2 * n + b + 1)
                    for hh in range(HEADS):
                        mm = nc.tensor.transpose(PS[:, 6 + hh // 4, (hh % 4) * T:(hh % 4 + 1) * T], eT[:, b, hh, :],
                                                 ident[:])
                    mm.then_inc(s.a_psum, 1)

                def attend(n, j):
                    pe.wait_ge(s.a, 2 * n + 2)
                    pe.wait_ge(s.v, 2 * n + 2)
                    for hh in range(HEADS):
                        for b in range(2):
                            nc.tensor.matmul(PS[64 * b:64 * b + 64, 6, 0:T], v[:, j, b, hh * D:(hh + 1) * D],
                                             e[:, j, b, hh, :], start=(hh == 0), stop=False)
                    for hh in range(HEADS):
                        for b in range(2):
                            mm = nc.tensor.matmul(PS[64 * b:64 * b + 64, 6, 0:T],
                                                  v[:, j, b, (HEADS + hh) * D:(HEADS + hh + 1) * D],
                                                  eT[:, b, hh, :], start=False, stop=(hh == HEADS - 1))
                    mm.then_inc(o_psum[j], 1)

                def fan_in(n):
                    pe.wait_ge(s.yT, n + 1)
                    nc.tensor.matmul(PS[:, 6, 0:2 * D], yT[:], fan[:], start=True, stop=True).then_inc(s.z_psum, 1)

                def step(at, prev, this, nxt):
                    g, m = at // QUADS, at % QUADS
                    if prev and at == TENSOR_AT['logits']:
                        transpose_logits(*prev, KGROUPS - 1)
                    if this and at >= QUADS and m == TENSOR_AT['logits']:
                        transpose_logits(*this, g - 1)
                    if this and at == TENSOR_AT['v1']:
                        make_v(this[0], this[1], 1)
                    if prev and at in (TENSOR_AT['e0'], TENSOR_AT['e1']):
                        transpose_e(prev[0], prev[1], int(at == TENSOR_AT['e1']))
                    if prev and at in (TENSOR_AT['back0'], TENSOR_AT['back1']):
                        transpose_back(prev[0], int(at == TENSOR_AT['back1']))
                    if prev and at == TENSOR_AT['attend']:
                        attend(prev[0], prev[1])
                    if prev and at == TENSOR_AT['fan']:
                        fan_in(prev[0])
                    if nxt and at == TENSOR_AT['x']:
                        if not prev:
                            pe.wait_ge(s.v, 2 * this[0] + 2)
                        make_x(nxt[0])
                    if nxt and at == TENSOR_AT['q']:
                        if prev:
                            pe.wait_ge(s.z, prev[0] + 1)
                        make_q(nxt[0], nxt[1])
                    if nxt and at == TENSOR_AT['terms']:
                        make_terms(nxt[0], nxt[1])
                    if nxt and at == TENSOR_AT['v0']:
                        make_v(nxt[0], nxt[1], 0)
                    if this:
                        quad(this[0], g, m)

                make_x(0)
                make_q(0, 0)
                make_terms(0, 0)
                make_v(0, 0, 0)
                run(pe, body(step))
        p.end()


def routed_weights(nc, ctx, A):
    p = Part(nc, ctx, "rtw")
    wi = p.sb("wi", [P, 2, HID])
    wr = p.sb("wr", [P, LAYERS, ROUTES + 1, HID + 1])
    ws = p.sb("ws", [P, LAYERS, HID + 1])
    wo = p.sb("wo", [P, D])
    bi = p.sb("bi", [P, 1])
    bo = p.sb("bo", [P, D])
    ident = p.sb("ident", [P, P])
    ids = p.sb("ids", [1, PAIRS], I32)
    loads = [(wi[:], A.rt_wi), (wr[:, :, 0:ROUTES, :], A.rt_wr), (ws[:], A.rt_ws), (wo[:], A.rt_wo),
             (bi[:], A.rt_bi), (bo[:], A.rt_bo), (ident[:], A.ident), (ids[:], A.route_id)]
    return named(wi=wi, wr=wr, ws=ws, wo=wo, bi=bi, bo=bo, ident=ident, ids=ids, loads=loads,
                 loaded=p.sem("loaded"))


def routed_layers(nc, A, h, PS, given, early):
    with ExitStack() as ctx:
        p = Part(nc, ctx, "rt")
        p.mine.append(given.loaded)
        wi, wr, ws, wo, bi, bo, ident, ids = (
            given.wi, given.wr, given.ws, given.wo, given.bi, given.bo, given.ident, given.ids)
        idf = p.sb("idf", [1, PAIRS])
        m1 = p.sb("m1", [1, PAIRS])
        m2 = p.sb("m2", [1, PAIRS])
        route = p.sb("route", [1, PAIRS], I32)
        warm = p.sb("warm", [P, 1])
        ln = layer_norm_buffers(p, GROUP)
        xT = p.sb("xT", [P, GP, TOK])
        hid = p.sb("hid", [P, LAYERS + 1, GP, 2, TOK])
        own = p.sb("own", [P, 2, LAYERS, GP, HID + 1])
        res = p.sb("res", [P, GROUP, D])
        s = p.sems(LN_SEMS + "shared residual route_steps route warm x_psum xT h0_psum "
                   "h0 own o_psum o added")
        hl_psum = [p.sem(f"layer_psum{m}") for m in range(LAYERS)]
        hl = [p.sem(f"layer{m}") for m in range(LAYERS)]
        def run(eng, step):
            step(-1, 1)
            step(0, 0)
            step(1, 1)
            with eng.Fori(1, GROUPS // 2 - 1) as i:
                step(2 * i, 0)
                step(2 * i + 1, 1)
            step(GROUPS - 2, 0)
            step(GROUPS - 1, 1)

        def there(n):
            return not isinstance(n, int) or 0 <= n < GROUPS

        with nc.Block() as block:
            @block.sync
            def _(sp):
                for weights in early:
                    for dst, src in weights.loads:
                        sp.dma_start(dst, src).then_inc(weights.loaded, 16)

            @block.gpsimd
            def _(pool):
                nc.gpsimd.memset(ln.minus_half[:], -0.5).then_inc(s.half_set, 1)
                pool.wait_ge(s.half_set, 1)
                pool.wait_ge(s.residual, 1)
                pool.wait_ge(s.route, 1)

                def step(n, slot):
                    f = n + 1
                    if not there(f):
                        return
                    layer_norm_root(pool, nc, f, ln, s)
                    pool.wait_ge(hl[LAYERS - 1], GP * count(f - 1))
                    for g in range(GP):
                        r = pool.value_load(route[0:1, bass.ds(f * GP + g, 1)], min_val=0, max_val=ROUTES)
                        last = nc.gpsimd.tensor_copy(own[:, 1 - slot, :, g, :], wr[:, :, bass.ds(r, 1), :].rearrange(
                            "p l o c -> p (l o) c"))
                        last.then_inc(s.own, 1)

                run(pool, step)

            @block.vector
            def _(dve):
                dve.wait_ge(given.loaded, 16 * len(given.loads))
                nc.vector.tensor_tensor(ws[:, :, 0:HID], ws[:, :, 0:HID], spread(ident[:], 1, LAYERS), ALU.add)\
                    .then_inc(s.shared, 1)
                dve.wait_ge(s.shared, 1)
                nc.vector.tensor_copy(wr[:, :, ROUTES, :], ws[:])
                nc.vector.tensor_tensor(wr[:, :, 0:ROUTES, :], wr[:, :, 0:ROUTES, :], spread(ws[:], 2, ROUTES),
                                        ALU.add).then_inc(s.residual, 1)
                nc.vector.tensor_copy(idf[:], ids[:]).then_inc(s.route_steps, 1)
                dve.wait_ge(s.route_steps, 1)
                nc.vector.tensor_scalar(m1[:], idf[:], 0.0, None, ALU.is_ge).then_inc(s.route_steps, 1)
                nc.vector.tensor_scalar(m2[:], idf[:], float(ROUTES - 1), None, ALU.is_le).then_inc(s.route_steps, 1)
                dve.wait_ge(s.route_steps, 3)
                nc.vector.tensor_tensor(m1[:], m1[:], m2[:], ALU.mult).then_inc(s.route_steps, 1)
                nc.vector.tensor_scalar(idf[:], idf[:], -float(ROUTES), None, ALU.add).then_inc(s.route_steps, 1)
                dve.wait_ge(s.route_steps, 5)
                nc.vector.tensor_tensor(idf[:], idf[:], m1[:], ALU.mult).then_inc(s.route_steps, 1)
                dve.wait_ge(s.route_steps, 6)
                nc.vector.tensor_scalar(route[:], idf[:], float(ROUTES), None, ALU.add).then_inc(s.route, 1)

                def step(n, slot):
                    f = n + 1
                    if there(f):
                        dve.wait_ge(s.x_psum, f)
                        layer_norm_end(dve, nc, f, ln, s)
                        dve.wait_ge(s.h0_psum, f)
                        dve.wait_ge(s.x_psum, f + 1)
                        nc.vector.tensor_copy(xT[:].rearrange("p a b -> p (a b)"), PS[:, 0, :]).then_inc(s.xT, 1)
                    if there(n + 2):
                        dve.wait_ge(s.ln_done, f + 1)
                        layer_norm_start(dve, nc, n + 2, h[:, bass.ds((n + 2) * GROUP, GROUP), :], ln, s)
                    if there(n):
                        hg = h[:, bass.ds(n * GROUP, GROUP), :]
                        dve.wait_ge(s.o_psum, n + 1)
                        dve.wait_ge(s.added, n)
                        nc.vector.tensor_tensor(res[:], PS[:, 7, :].rearrange("p (a b) -> p a b", a=GROUP),
                                                spread(bo[:], 1, GROUP), ALU.add).then_inc(s.o, 1)
                        dve.wait_ge(s.o, n + 1)
                        nc.vector.tensor_tensor(hg, hg, res[:], ALU.add).then_inc(s.added, 1)

                layer_norm_start(dve, nc, 0, h[:, 0:GROUP, :], ln, s)
                run(dve, step)

            @block.scalar
            def _(act):
                act.wait_ge(given.loaded, 16 * len(given.loads))
                nc.scalar.activation(warm[:], bi[:], ACT.Relu).then_inc(s.warm, 1)

                def step(n, slot):
                    if not there(n):
                        return
                    for b in range(2):
                        act.wait_ge(s.h0_psum, n + 1)
                        nc.scalar.activation(hid[:, 0, :, b, :], PS[:, 1 + b, :].rearrange("p (g t) -> p g t", g=GP),
                                             ACT.Relu, bias=bi[:]).then_inc(s.h0, 1)
                    for l in range(LAYERS):
                        for g in range(GP):
                            act.wait_ge(hl_psum[l], GP * n + g + 1)
                            nc.scalar.activation(hid[:, l + 1, g], PS[:, 3 + g, l * 256:(l + 1) * 256]
                                                 .rearrange("p (b t) -> p b t", b=2), ACT.Relu,
                                                 bias=own[:, slot, l, g, HID:HID + 1]).then_inc(hl[l], 1)

                run(act, step)

            @block.tensor
            def _(pe):
                pe.wait_ge(given.loaded, 16 * len(given.loads))

                def step(n, slot):
                    f = n + 1
                    if there(n):
                        pe.wait_ge(s.xT, n + 1)
                        for b in range(2):
                            mm = nc.tensor.matmul(PS[:, 1 + b, :], wi[:, b, :], xT[:].rearrange("p a b -> p (a b)"),
                                                  start=True, stop=True)
                        mm.then_inc(s.h0_psum, 1)
                        pe.wait_ge(s.own, GP * n + GP)
                    for l in range(LAYERS):
                        if there(f) and l == 1:
                            pe.wait_ge(s.ln_done, f + 1)
                            for g in range(GP):
                                mm = nc.tensor.transpose(PS[:, 0, g * P:(g + 1) * P],
                                                         ln.xn[:, 2 * g:2 * g + 2, :].rearrange("p b w -> p (b w)"), ident[:])
                            mm.then_inc(s.x_psum, 1)
                        for g in range(GP):
                            if not there(n):
                                continue
                            if l == 0:
                                pe.wait_ge(s.h0, 2 * n + 2)
                            else:
                                pe.wait_ge(hl[l - 1], GP * n + g + 1)
                            nc.tensor.matmul(PS[:, 3 + g, l * 256:(l + 1) * 256],
                                             own[:, slot, l, g, 0:HID], hid[:, l, g].rearrange("p b t -> p (b t)"),
                                             start=True, stop=True).then_inc(hl_psum[l], 1)
                    for g in range(GP):
                        if not there(n):
                            continue
                        pe.wait_ge(hl[LAYERS - 1], GP * n + g + 1)
                        if g == 0:
                            pe.wait_ge(s.o, n)
                        for b in range(2):
                            mm = nc.tensor.matmul(PS[:, 7, (2 * g + b) * D:(2 * g + b + 1) * D], hid[:, LAYERS, g, b, :],
                                                  wo[:], start=True, stop=True)
                    if there(n):
                        mm.then_inc(s.o_psum, 1)

                run(pe, step)
        p.end()


MASKED = -1e30
CG = 4
CGROUPS = SAMPLES // CG
HPAIRS = HEADS // 2


def causal_weights(nc, ctx, A):
    p = Part(nc, ctx, "caw")
    wqk = p.sb("wqk", [P, 2, HEADS * D])
    wv = p.sb("wv", [P, HEADS * D])
    wu = p.sb("wu", [P, HPAIRS, D])
    bqk = p.sb("bqk", [P, 2, HPAIRS])
    bv = p.sb("bv", [P, HEADS * D])
    bu = p.sb("bu", [P, 1])
    ident = p.sb("ident", [P, P])
    mask = p.sb("mask", [P, TOK])
    later = p.sb("later", [P, 1])
    loads = [(wqk[:], A.ca_wqk), (wv[:], A.ca_wv), (wu[:], A.ca_wu), (bqk[:], A.ca_bqk), (bv[:], A.ca_bv),
             (bu[:], A.ca_bu), (ident[:], A.ident), (mask[:], A.mask), (later[:], A.later)]
    return named(wqk=wqk, wv=wv, wu=wu, bqk=bqk, bv=bv, bu=bu, ident=ident, mask=mask, later=later,
                 loads=loads, loaded=p.sem("loaded"))


def causal_attention(nc, A, h, PS, given):
    with ExitStack() as ctx:
        p = Part(nc, ctx, "ca")
        p.mine.append(given.loaded)
        wqk, wv, wu, bqk, bv, bu, ident, mask, later = (
            given.wqk, given.wv, given.wu, given.bqk, given.bv, given.bu, given.ident, given.mask,
            given.later)
        warm = p.sb("warm", [P, 1])
        ln = layer_norm_buffers(p, CG)
        xpad = p.sb("xpad", [P, 2, CG // 2, 2, TOK])
        q = p.sb("q", [P, 2, HPAIRS, CG, TOK])
        kpad = p.sb("kpad", [P, 2, HPAIRS, CG, 2, TOK])
        v = p.sb("v", [P, 2, CG, HEADS * D])
        sc = p.sb("sc", [P, 2, HEADS, TOK])
        nmax = p.sb("nmax", [P, 2, HEADS])
        pr = p.sb("pr", [P, 2, HEADS, TOK])
        tot = p.sb("tot", [P, 2, HEADS])
        prT = p.sb("prT", [P, HEADS, TOK])
        outT = p.sb("outT", [P, HPAIRS, CG, TOK])
        uT = p.sb("uT", [P, CG, TOK])
        s = p.sems(LN_SEMS + "warm zeroed x_psum xpad q_psum q k_psum k_low k_high v_psum v scores masked nmax "
                   "exp recip rinv norm prT_psum prT o_psum outT uT_psum uT u_psum half_added added")
        SKEW = 3

        def run(eng, step):
            def group(n, slot):
                for b in range(CG):
                    step(n, slot, b)
            for n in range(-SKEW, 2):
                group(n, n % 2)
            middle = (CGROUPS - SKEW) // 2
            with eng.Fori(1, middle) as i:
                group(2 * i, 0)
                group(2 * i + 1, 1)
            for n in range(2 * middle, CGROUPS + 1):
                group(n, n % 2)

        def there(first, b=0):
            return not isinstance(first, int) or 0 <= first + b < SAMPLES

        with nc.Block() as block:
            @block.gpsimd
            def _(pool):
                nc.gpsimd.memset(ln.minus_half[:], -0.5).then_inc(s.half_set, 1)
                nc.gpsimd.memset(xpad[:], 0.0).then_inc(s.zeroed, 1)
                nc.gpsimd.memset(kpad[:], 0.0).then_inc(s.zeroed, 1)
                pool.wait_ge(s.half_set, 1)
                with pool.Fori(0, CGROUPS) as g:
                    layer_norm_root(pool, nc, g, ln, s)

            @block.vector
            def _(dve):
                dve.wait_ge(given.loaded, 16 * len(given.loads))
                dve.wait_ge(s.zeroed, 2)

                def step(n, slot, b):
                    t = CG * n + b
                    if there(t):
                        dve.wait_ge(s.exp, t + 1)
                        nc.vector.reciprocal(tot[:, b % 2], tot[:, b % 2]).then_inc(s.recip, 1)
                    if there(t):
                        dve.wait_ge(s.recip, t + 1)
                        nc.vector.tensor_scalar(tot[:, b % 2], tot[:, b % 2], later[:], None, ALU.mult).then_inc(s.rinv, 1)
                        dve.wait_ge(s.rinv, t + 1)
                        nc.vector.tensor_tensor(pr[:, b % 2], pr[:, b % 2], spread(tot[:, b % 2], 2, TOK), ALU.mult)\
                            .then_inc(s.norm, 1)
                    if there(CG * (n + 2)) and b == 0:
                        dve.wait_ge(s.x_psum, n + 3)
                        xv = PS[:, 7, 0:CG // 2 * TOK].rearrange("p (a t) -> p a t", t=TOK)
                        dve.wait_ge(s.v_psum, count(CG * (n + 1)))
                        nc.vector.tensor_copy(xpad[0:64, slot, :, 0, :], xv[0:64])
                        nc.vector.tensor_copy(xpad[64:128, slot, :, 1, :], xv[64:128]).then_inc(s.xpad, 1)
                    if there(t + 3):
                        vslot = slot if b == 0 else 1 - slot
                        dve.wait_ge(s.v_psum, t + 4)
                        dve.wait_ge(s.o_psum, count(t - 4))
                        nc.vector.tensor_tensor(v[:, vslot, (b + 3) % CG, :], PS[:, 0, :], bv[:], ALU.add)\
                            .then_inc(s.v, 1)
                    if there(t + 2):
                        dve.wait_ge(s.scores, t + 3)
                        nc.vector.scalar_tensor_tensor(
                            out=sc[:, b % 2], in0=PS[:, 2:4, :].rearrange("p a (h t) -> p (a h) t", t=TOK),
                            scalar=D ** -0.5, in1=spread(mask[:], 1, HEADS), op0=ALU.mult, op1=ALU.add)\
                            .then_inc(s.masked, 1)
                        dve.wait_ge(s.masked, t + 3)
                        nc.vector.tensor_reduce(nmax[:, b % 2], sc[:, b % 2], AX.X, ALU.max, negate=True)\
                            .then_inc(s.nmax, 1)
                    if there(t + 6):
                        kslot = 1 - slot if b < 2 else slot
                        hp = (b + 2) % CG
                        dve.wait_ge(s.k_psum, t + 7)
                        dve.wait_ge(s.scores, count(CG * n + (0 if b < 2 else CG)))
                        nc.vector.tensor_scalar(kpad[0:64, kslot, hp, :, 0, :],
                                                PS[0:64, 1, :].rearrange("p (a t) -> p a t", t=TOK),
                                                bqk[0:64, 1, hp:hp + 1], None, ALU.add).then_inc(s.k_low, 1)
                    if there(CG * (n - 1)) and b == 1:
                        dve.wait_ge(s.u_psum, n)
                        uv = PS[:, 7, :].rearrange("p (a c w) -> p a c w", a=CG, c=2)
                        hg = h[:, bass.ds(CG * (n - 1), CG), :]
                        nc.vector.tensor_tensor(hg, hg, uv[:, :, 0, :], ALU.add).then_inc(s.half_added, 1)
                        dve.wait_ge(s.half_added, n)
                        nc.vector.tensor_tensor(hg, hg, uv[:, :, 1, :], ALU.add).then_inc(s.added, 1)
                    if there(CG * (n + 3)) and b == 2:
                        layer_norm_start(dve, nc, n + 3, h[:, bass.ds(CG * (n + 3), CG), :], ln, s)
                    if there(CG * (n + 3)) and b == 3:
                        dve.wait_ge(s.x_psum, n + 3)
                        layer_norm_end(dve, nc, n + 3, ln, s)

                run(dve, step)

            @block.scalar
            def _(act):
                act.wait_ge(given.loaded, 16 * len(given.loads))
                act.wait_ge(s.zeroed, 2)
                nc.scalar.activation(warm[:], later[:], ACT.Exp).then_inc(s.warm, 1)

                def step(n, slot, b):
                    t = CG * n + b
                    if there(t - 1):
                        act.wait_ge(s.o_psum, t)
                        nc.scalar.activation(outT[:, :, (b - 1) % CG, :], PS[:, 6, :].rearrange("p (a t) -> p a t", t=TOK),
                                             ACT.Copy).then_inc(s.outT, 1)
                    if there(t + 1):
                        e = (b + 1) % 2
                        act.wait_ge(s.nmax, t + 2)
                        act.wait_ge(s.prT_psum, count(t))
                        for c in range(HEADS):
                            last = nc.scalar.activation(pr[:, e, c, :], sc[:, e, c, :], ACT.Exp, bias=nmax[:, e, c:c + 1],
                                                        accum_out=tot[:, e, c:c + 1])
                        last.then_inc(s.exp, 1)
                    if there(t):
                        act.wait_ge(s.prT_psum, t + 1)
                        nc.scalar.activation(prT[:], PS[:, 4:6, :].rearrange("p a (h t) -> p (a h) t", t=TOK),
                                             ACT.Copy).then_inc(s.prT, 1)
                    if there(t + 6):
                        kslot = 1 - slot if b < 2 else slot
                        hp = (b + 2) % CG
                        act.wait_ge(s.scores, count(CG * n + (0 if b < 2 else CG)))
                        act.wait_ge(s.q_psum, t + 7)
                        nc.scalar.activation(q[:, kslot, hp].rearrange("p a t -> p (a t)"), PS[:, 0, :], ACT.Identity,
                                             bias=bqk[:, 0, hp:hp + 1]).then_inc(s.q, 1)
                        act.wait_ge(s.k_psum, t + 7)
                        act.wait_ge(s.k_low, t + 7)
                        nc.scalar.activation(kpad[64:128, kslot, hp, :, 1, :],
                                             PS[64:128, 1, :].rearrange("p (a t) -> p a t", t=TOK), ACT.Identity,
                                             bias=bqk[64:128, 1, hp:hp + 1]).then_inc(s.k_high, 1)
                    if there(CG * (n - 1)) and b == 0:
                        act.wait_ge(s.uT_psum, n)
                        nc.scalar.activation(uT[:].rearrange("p a t -> p (a t)"), PS[:, 7, :], ACT.Identity, bias=bu[:])\
                            .then_inc(s.uT, 1)

                run(act, step)

            @block.tensor
            def _(pe):
                pe.wait_ge(given.loaded, 16 * len(given.loads))

                def step(n, slot, b):
                    t = CG * n + b
                    other = 1 - slot
                    if there(t + 2):
                        kslot, kb = (slot, b + 2) if b < 2 else (other, b - 2)
                        made = CG * n + CG if b < 2 else CG * n + 2 * CG
                        pe.wait_ge(s.q, made)
                        pe.wait_ge(s.k_high, made)
                        pe.wait_ge(s.masked, t + 2)
                        for hp in range(HPAIRS):
                            mm = nc.tensor.matmul(PS[:, 2 + hp // 2, (hp % 2) * 2 * TOK:(hp % 2 + 1) * 2 * TOK],
                                                  q[:, kslot, hp, kb, :],
                                                  kpad[:, kslot, hp, kb].rearrange("p a t -> p (a t)"),
                                                  start=True, stop=True)
                        mm.then_inc(s.scores, 1)
                    if there(t):
                        pe.wait_ge(s.norm, t + 1)
                        pe.wait_ge(s.prT, t)
                        for c in range(HEADS):
                            mm = nc.tensor.transpose(PS[:, 4 + c // 4, (c % 4) * TOK:(c % 4 + 1) * TOK], pr[:, b % 2, c, :],
                                                     ident[:])
                        mm.then_inc(s.prT_psum, 1)
                    if there(t + 6):
                        xslot = other if b < 2 else slot
                        hp = (b + 2) % CG
                        xv = xpad[:, xslot].rearrange("p a c t -> p (a c t)")
                        if b == 2:
                            pe.wait_ge(s.xpad, n + 3)
                        pe.wait_ge(s.v, count(t + 4))
                        if not there(t + 3):
                            pe.wait_ge(s.q, t + 6)
                        nc.tensor.matmul(PS[:, 0, :], wqk[:, 0, hp * P:(hp + 1) * P], xv, start=True, stop=True)\
                            .then_inc(s.q_psum, 1)
                        pe.wait_ge(s.k_high, t + 6)
                        nc.tensor.matmul(PS[:, 1, :], wqk[:, 1, hp * P:(hp + 1) * P], xv, start=True, stop=True)\
                            .then_inc(s.k_psum, 1)
                    if there(CG * (n - 1)) and b == 0:
                        pe.wait_ge(s.outT, CG * n)
                        if there(CG * (n + 2)):
                            pe.wait_ge(s.xpad, n + 3)
                        for hp in range(HPAIRS):
                            a = hp % 2
                            mm = nc.tensor.matmul(PS[64 * a:64 * a + 64, 7, :], wu[:, hp, :],
                                                  outT[:, hp].rearrange("p a t -> p (a t)"), start=(hp < 2), stop=(hp >= 2))
                        mm.then_inc(s.uT_psum, 1)
                    if there(CG * (n - 1)) and b == 1:
                        pe.wait_ge(s.uT, n)
                        for m in range(CG):
                            mm = nc.tensor.transpose(PS[:, 7, m * TOK:(m + 1) * TOK], uT[:, m, :], ident[:])
                        mm.then_inc(s.u_psum, 1)
                    if there(t):
                        pe.wait_ge(s.prT, t + 1)
                        pe.wait_ge(s.v, t + 1)
                        pe.wait_ge(s.outT, t)
                        for c in range(HEADS):
                            hp, a = c // 2, c % 2
                            mm = nc.tensor.matmul(PS[64 * a:64 * a + 64, 6, hp * TOK:(hp + 1) * TOK],
                                                  v[:, slot, b, c * D:(c + 1) * D], prT[:, c, :], start=True, stop=True)
                        mm.then_inc(s.o_psum, 1)
                    if there(t + 4):
                        if there(t + 6):
                            pe.wait_ge(s.q, t + 7)
                        else:
                            pe.wait_ge(s.v, t + 4)
                        nc.tensor.matmul(PS[:, 0, :], xpad[:, other, b // 2, b % 2, :], wv[:], start=True, stop=True)\
                            .then_inc(s.v_psum, 1)
                    if there(CG * (n + 3)) and b == 3:
                        pe.wait_ge(s.ln_done, n + 4)
                        pe.wait_ge(s.added, count(n))
                        for m in range(CG // 2):
                            mm = nc.tensor.transpose(PS[:, 7, m * P:(m + 1) * P],
                                                     ln.xn[:, 2 * m:2 * m + 2, :].rearrange("p b w -> p (b w)"), ident[:])
                        mm.then_inc(s.x_psum, 1)

                run(pe, step)
        p.end()


ET = 16
TURNS_E = SAMPLES // ET
EP = EXPERTS // 2
HALF = ET // 2


def expert_weights(nc, ctx, A):
    p = Part(nc, ctx, "exw")
    rw = p.sb("rw", [P, 2 * EXPERTS])
    w1 = p.sb("w1", [P, EP, 2, P])
    w2 = p.sb("w2", [P, EP, D])
    b1 = p.sb("b1", [P, EP])
    b2 = p.sb("b2", [P, 2, HALF * D])
    ident = p.sb("ident", [P, P])
    earlier = p.sb("earlier", [P, EXPERTS * EXPERTS])
    select_f32 = p.sb("select_f32", [P, 4, EP, P])
    loads = [(rw[:], A.ex_rw), (w1[:], A.ex_w1), (w2[:], A.ex_w2), (b1[:], A.ex_b1), (b2[:], A.ex_b2),
             (ident[:], A.ident), (earlier[:], A.earlier), (select_f32[:], A.ex_select)]
    return named(rw=rw, w1=w1, w2=w2, b1=b1, b2=b2, ident=ident, earlier=earlier, select_f32=select_f32,
                 loads=loads, loaded=p.sem("loaded"))


def experts(nc, A, h, PS, given):
    with ExitStack() as ctx:
        p = Part(nc, ctx, "ex")
        p.mine.append(given.loaded)
        rw, w1, w2, b1, b2, ident, earlier, select_f32 = (
            given.rw, given.w1, given.w2, given.b1, given.b2, given.ident, given.earlier, given.select_f32)
        warm = p.sb("warm", [P, 1])
        ln = layer_norm_buffers(p, ET)
        xT = p.sb("xT", [P, 2, ET // 2, TOK])
        select = p.sb("select", [P, 4, EP, P], BF16)
        ident_b = p.sb("ident_b", [P, P], BF16)
        parts = p.sb("parts", [P, 2, ET, 4, EXPERTS], BF16)
        rest = p.sb("rest", [P, ET, EXPERTS])
        partsT = p.sb("partsT", [P, 2, HALF // 2 * TOK], BF16)
        prob = p.sb("prob", [P, ET, EXPERTS])
        stat = p.sb("stat", [P, ET])
        above = p.sb("above", [P, ET, EXPERTS, EXPERTS])
        tie = p.sb("tie", [P, ET, EXPERTS, EXPERTS])
        rank = p.sb("rank", [P, ET, EXPERTS])
        weight = p.sb("weight", [P, 2, ET, EXPERTS])
        wT = p.sb("wT", [P, TOK])
        hid = p.sb("hid", [P, 2, 2, HALF // 2 * TOK])
        scaled_hid = p.sb("scaled_hid", [P, 2, 2, HALF // 2 * TOK])
        oT = p.sb("oT", [P, HALF // 2, TOK])
        s = p.sems(LN_SEMS + "warm x_psum xT x_kept logit_psum max shifted exp total total_inv norm above "
                   "equal tie beaten rank sel sel_sum guarded sel_inv weight high after_high middle parts zeroed converted "
                   "partsT_psum partsT wT_psum wT hid_psum hid c_psum scaled "
                   "oT_psum oT o_psum res out")
        out_v = A.out.rearrange("n t d -> t n d")

        def run(eng, step):
            def turn(n, slot):
                for k in range(2 * EP):
                    step(n, slot, k)
            for n in range(-2, 2):
                turn(n, n % 2)
            with eng.Fori(1, TURNS_E // 2 - 1) as i:
                turn(2 * i, 0)
                turn(2 * i + 1, 1)
            for n in range(TURNS_E - 2, TURNS_E + 1):
                turn(n, n % 2)

        def there(n):
            return not isinstance(n, int) or 0 <= n < TURNS_E

        def half_ends(n, k):
            return there(n) if k >= EP else there(n - 1)

        with nc.Block() as block:
            @block.sync
            def _(sp):
                with sp.Fori(0, 2 * TURNS_E) as m:
                    sp.wait_ge(s.res, m + 1)
                    sp.dma_start(out_v[:, bass.ds(m * HALF, HALF), :], h[:, bass.ds(m * HALF, HALF), :])\
                        .then_inc(s.out, 16)
                sp.wait_ge(s.out, 16 * 2 * TURNS_E)

            @block.gpsimd
            def _(pool):
                nc.gpsimd.memset(parts[:], 0.0).then_inc(s.zeroed, 1)
                nc.gpsimd.memset(ln.minus_half[:], -0.5).then_inc(s.half_set, 1)
                pool.wait_ge(s.half_set, 1)
                with pool.Fori(0, TURNS_E) as n:
                    layer_norm_root(pool, nc, n, ln, s)
                    pool.wait_ge(s.ln_done, n + 1)
                    ht = h[:, bass.ds(n * ET, ET), :]
                    nc.gpsimd.tensor_tensor(ht, ht, ln.xn[:], ALU.add).then_inc(s.x_kept, 1)

            @block.vector
            def _(dve):
                dve.wait_ge(given.loaded, 16 * len(given.loads))
                dve.wait_ge(s.zeroed, 1)
                nc.vector.tensor_copy(select[:], select_f32[:]).then_inc(s.converted, 1)
                nc.vector.tensor_copy(ident_b[:], ident[:]).then_inc(s.converted, 1)

                def norm(f, k):
                    if k == 1:
                        nc.vector.tensor_reduce(ln.sum[:], h[:, bass.ds(f * ET, ET), :], AX.X, ALU.add).then_inc(s.ln_sum, 1)
                        dve.wait_ge(s.ln_sum, f + 1)
                        nc.vector.scalar_tensor_tensor(out=ln.xc[:], in0=spread(ln.sum[:], 2, D), scalar=-1.0 / D,
                                                       in1=h[:, bass.ds(f * ET, ET), :], op0=ALU.mult, op1=ALU.add)\
                            .then_inc(s.ln_centred, 1)
                    if k == 2:
                        dve.wait_ge(s.ln_centred, f + 1)
                        nc.vector.tensor_tensor(ln.sq[:], ln.xc[:], ln.xc[:], ALU.mult).then_inc(s.ln_squared, 1)
                        dve.wait_ge(s.ln_squared, f + 1)
                        nc.vector.tensor_reduce(ln.var[:], ln.sq[:], AX.X, ALU.add).then_inc(s.ln_sumsq, 1)
                        dve.wait_ge(s.ln_sumsq, f + 1)
                        nc.vector.tensor_scalar(ln.var[:], ln.var[:], 1.0 / D, EPS, ALU.mult, ALU.add)\
                            .then_inc(s.ln_var, 1)
                    if k == 7:
                        dve.wait_ge(s.x_psum, 2 * f)
                        dve.wait_ge(s.x_kept, f)
                        layer_norm_end(dve, nc, f, ln, s)

                def front(f, slot, k):
                    if k == 2:
                        dve.wait_ge(s.logit_psum, f + 1)
                        logits = PS[:, 7, 0:ET * EXPERTS].rearrange("p (n e) -> p n e", e=EXPERTS)
                        nc.vector.tensor_reduce(stat[:], logits, AX.X, ALU.max, negate=True).then_inc(s.max, 1)
                        dve.wait_ge(s.max, f + 1)
                        nc.vector.tensor_tensor(prob[:], logits, spread(stat[:], 2, EXPERTS), ALU.add)\
                            .then_inc(s.shifted, 1)
                    own, other = spread(prob[:], 3, EXPERTS), spread(prob[:], 2, EXPERTS)
                    if k == 3:
                        dve.wait_ge(s.exp, f + 1)
                        nc.vector.tensor_reduce(stat[:], prob[:], AX.X, ALU.add).then_inc(s.total, 1)
                        dve.wait_ge(s.total, f + 1)
                        nc.vector.reciprocal(stat[:], stat[:]).then_inc(s.total_inv, 1)
                        dve.wait_ge(s.total_inv, f + 1)
                        nc.vector.tensor_tensor(prob[:], prob[:], spread(stat[:], 2, EXPERTS), ALU.mult).then_inc(s.norm, 1)
                        dve.wait_ge(s.norm, f + 1)
                        nc.vector.tensor_tensor(tie[:], other, own, ALU.is_equal).then_inc(s.equal, 1)
                    if k == 4:
                        nc.vector.tensor_tensor(above[:], other, own, ALU.is_gt).then_inc(s.above, 1)
                        dve.wait_ge(s.equal, f + 1)
                        tv = tie[:].rearrange("p n a b -> p n (a b)")
                        nc.vector.tensor_tensor(tv, tv, spread(earlier[:], 1, ET), ALU.mult).then_inc(s.tie, 1)
                        dve.wait_ge(s.tie, f + 1)
                        dve.wait_ge(s.above, f + 1)
                        nc.vector.tensor_tensor(tie[:], tie[:], above[:], ALU.add).then_inc(s.beaten, 1)
                    if k == 5:
                        dve.wait_ge(s.beaten, f + 1)
                        nc.vector.tensor_reduce(rank[:], tie[:], AX.X, ALU.add).then_inc(s.rank, 1)
                        dve.wait_ge(s.rank, f + 1)
                        nc.vector.scalar_tensor_tensor(out=rank[:], in0=rank[:], scalar=2.0, in1=prob[:], op0=ALU.is_lt,
                                                       op1=ALU.mult).then_inc(s.sel, 1)
                        dve.wait_ge(s.sel, f + 1)
                        nc.vector.tensor_reduce(stat[:], rank[:], AX.X, ALU.add).then_inc(s.sel_sum, 1)
                        dve.wait_ge(s.sel_sum, f + 1)
                        nc.vector.tensor_scalar(stat[:], stat[:], 1e-12, None, ALU.max).then_inc(s.guarded, 1)
                        dve.wait_ge(s.guarded, f + 1)
                        nc.vector.reciprocal(stat[:], stat[:]).then_inc(s.sel_inv, 1)
                        dve.wait_ge(s.sel_inv, f + 1)
                        dve.wait_ge(s.wT_psum, count(f - 1))
                        w = weight[:, slot]
                        nc.vector.tensor_tensor(w, rank[:], spread(stat[:], 2, EXPERTS), ALU.mult).then_inc(s.weight, 1)
                    if k == 6:
                        w = weight[:, slot]
                        dve.wait_ge(s.weight, f + 1)
                        dve.wait_ge(s.partsT_psum, count(f - 1))
                        nc.vector.tensor_copy(parts[:, slot, :, 0, :], w).then_inc(s.high, 1)
                        dve.wait_ge(s.high, f + 1)
                        nc.vector.tensor_tensor(rest[:], w, parts[:, slot, :, 0, :], ALU.subtract).then_inc(s.after_high, 1)
                        dve.wait_ge(s.after_high, f + 1)
                        nc.vector.tensor_copy(parts[:, slot, :, 1, :], rest[:]).then_inc(s.middle, 1)
                        dve.wait_ge(s.middle, f + 1)
                        nc.vector.tensor_tensor(parts[:, slot, :, 2, :], rest[:], parts[:, slot, :, 1, :], ALU.subtract)\
                            .then_inc(s.parts, 1)

                def step(n, slot, k):
                    t = 2 * EP * n + k
                    if there(n):
                        for b in range(2):
                            dve.wait_ge(s.hid, 2 * t + b + 1)
                            dve.wait_ge(s.c_psum, 2 * t + b + 1)
                            dve.wait_ge(s.oT_psum, count(t - 1))
                            nc.vector.tensor_tensor(scaled_hid[:, k % 2, b], hid[:, k % 2, b], PS[:, 2 + b, :], ALU.mult)\
                                .then_inc(s.scaled, 1)
                    if half_ends(n, k) and k % EP == 1:
                        m = 2 * n + k // EP - 1
                        dve.wait_ge(s.o_psum, m + 1)
                        dve.wait_ge(s.x_kept, n + k // EP)
                        hm = h[:, bass.ds(m * HALF, HALF), :]
                        nc.vector.tensor_tensor(hm, hm, PS[:, 5, :].rearrange("p (n d) -> p n d", d=D), ALU.add)\
                            .then_inc(s.res, 1)
                    if there(n + 1):
                        front(n + 1, 1 - slot, k)
                    if there(n + 2):
                        norm(n + 2, k)

                run(dve, step)

            @block.scalar
            def _(act):
                act.wait_ge(given.loaded, 16 * len(given.loads))
                nc.scalar.activation(warm[:], b1[:, 0:1], ACT.Gelu).then_inc(s.warm, 1)

                def step(n, slot, k):
                    t = 2 * EP * n + k
                    if there(n) and k == 0:
                        act.wait_ge(s.partsT_psum, n + 1)
                        act.wait_ge(s.c_psum, count(16 * (n - 1)))
                        nc.scalar.activation(partsT[:, slot, :], PS[:, 7, :], ACT.Copy).then_inc(s.partsT, 1)
                    if there(n):
                        for b in range(2):
                            act.wait_ge(s.hid_psum, 2 * t + b + 1)
                            act.wait_ge(s.scaled, count(2 * t + b - 3))
                            nc.scalar.activation(hid[:, k % 2, b], PS[:, b, :], ACT.Gelu, bias=b1[:, k % EP:k % EP + 1])\
                                .then_inc(s.hid, 1)
                    if half_ends(n, k) and k % EP == 0:
                        m = 2 * n + k // EP - 1
                        act.wait_ge(s.oT_psum, t)
                        act.wait_ge(s.o_psum, m)
                        nc.scalar.activation(oT[:].rearrange("p a t -> p (a t)"), PS[:, 4, :], ACT.Copy).then_inc(s.oT, 1)
                    if there(n + 1) and k in (0, 1):
                        f, c = n + 1, k
                        act.wait_ge(s.x_psum, 2 * f + c + 1)
                        act.wait_ge(s.hid_psum, count(16 * (f - 1)))
                        nc.scalar.activation(xT[:, 1 - slot, 4 * c:4 * c + 4, :].rearrange("p a t -> p (a t)"), PS[:, 6, :],
                                             ACT.Copy).then_inc(s.xT, 1)
                    if there(n) and k == 1:
                        act.wait_ge(s.wT_psum, n + 1)
                        act.wait_ge(s.o_psum, 2 * n)
                        nc.scalar.activation(wT[:], PS[:, 7, 0:TOK], ACT.Copy).then_inc(s.wT, 1)
                    if there(n + 1) and k == 2:
                        act.wait_ge(s.shifted, n + 2)
                        nc.scalar.activation(prob[:], prob[:], ACT.Exp).then_inc(s.exp, 1)

                run(act, step)

            @block.tensor
            def _(pe):
                pe.wait_ge(given.loaded, 16 * len(given.loads))
                pe.wait_ge(s.converted, 2)

                def second(t, ep):
                    for b in range(2):
                        pe.wait_ge(s.scaled, 2 * t + b + 1)
                        mm = nc.tensor.matmul(PS[64 * b:64 * b + 64, 4, :], w2[:, ep, :], scaled_hid[:, ep % 2, b],
                                              start=(ep == 0), stop=(ep == EP - 1))
                    mm.then_inc(s.oT_psum, 1)

                def step(n, slot, k):
                    t = 2 * EP * n + k
                    hf, ep = k // EP, k % EP
                    if there(n) and k == 0:
                        pe.wait_ge(s.parts, n + 1)
                        for c in range(4):
                            for g in range(HALF // 2):
                                a = HALF * (c // 2) + 2 * g + c % 2
                                mm = nc.tensor.matmul(PS[32 * c:32 * c + 32, 7, g * TOK:(g + 1) * TOK],
                                                      parts[:, slot, a].rearrange("p m e -> p (m e)"), ident_b[:],
                                                      start=True, stop=True)
                        mm.then_inc(s.partsT_psum, 1)
                    if there(n):
                        if ep == 0:
                            pe.wait_ge(s.xT, 2 * n + hf + 1)
                        for b in range(2):
                            pe.wait_ge(s.hid, count(2 * t + b - 1))
                            nc.tensor.matmul(PS[:, b, :], w1[:, ep, b, :],
                                             xT[:, slot, 4 * hf:4 * hf + 4, :].rearrange("p a t -> p (a t)"),
                                             start=True, stop=True).then_inc(s.hid_psum, 1)
                        if k == 0:
                            pe.wait_ge(s.partsT, n + 1)
                        for b in range(2):
                            pe.wait_ge(s.scaled, count(2 * t + b - 1))
                            mm = nc.tensor.matmul(PS[:, 2 + b, :], select[:, 2 * hf + b, ep, :], partsT[:, slot, :],
                                                  start=True, stop=True)
                            mm.then_inc(s.c_psum, 1)
                    if (there(n) if k else there(n - 1)):
                        if ep == 1:
                            pe.wait_ge(s.oT, count(2 * n + hf))
                        second(t - 1, (ep - 1) % EP)
                    if half_ends(n, k) and ep == 1:
                        m = 2 * n + hf - 1
                        pe.wait_ge(s.oT, m + 1)
                        pe.wait_ge(s.wT, n + hf)
                        pe.wait_ge(s.res, m)
                        nc.tensor.matmul(PS[:, 5, :], wT[:], b2[:, 1 - hf, :], start=True, stop=False)
                        for g in range(HALF // 2):
                            mm = nc.tensor.matmul(PS[:, 5, g * P:(g + 1) * P], oT[:, g, :], ident[:], start=False,
                                                  stop=(g == HALF // 2 - 1))
                        mm.then_inc(s.o_psum, 1)
                    if there(n) and k == 1:
                        nc.tensor.transpose(PS[:, 7, 0:TOK], weight[:, slot].rearrange("p n e -> p (n e)"), ident[:])\
                            .then_inc(s.wT_psum, 1)
                    if there(n + 1) and k in (0, 1):
                        f, c = n + 1, k
                        pe.wait_ge(s.ln_done, f + 1)
                        pe.wait_ge(s.xT, 2 * f + c)
                        for g in range(4):
                            a = 8 * c + 2 * g
                            mm = nc.tensor.transpose(PS[:, 6, g * P:(g + 1) * P],
                                                     ln.xn[:, a:a + 2, :].rearrange("p b w -> p (b w)"), ident[:])
                        mm.then_inc(s.x_psum, 1)
                    if there(n + 1) and k == 2:
                        f = n + 1
                        pe.wait_ge(s.xT, 2 * f + 2)
                        pe.wait_ge(s.wT, count(n + 1))
                        for g in range(ET // 2):
                            mm = nc.tensor.matmul(PS[:, 7, g * 2 * EXPERTS:(g + 1) * 2 * EXPERTS], xT[:, 1 - slot, g, :],
                                                  rw[:], start=True, stop=True)
                        mm.then_inc(s.logit_psum, 1)

                run(pe, step)
        p.end()


def build(nc, A):
    with nc.sbuf_tensor("h", [P, SAMPLES, D], F32) as h, nc.psum_tensor("banks", [P, 8, 512], F32) as banks:
        with ExitStack() as ctx:
            routed = routed_weights(nc, ctx, A)
            with ExitStack() as ctx2:
                l1 = l1_weights(nc, ctx2, A)
                tokenise(nc, A, h, banks, [l1, routed])
                l1_attention(nc, A, h, banks, l1)
            causal = causal_weights(nc, ctx, A)
            expert = expert_weights(nc, ctx, A)
            routed_layers(nc, A, h, banks, routed, [causal, expert])
            causal_attention(nc, A, h, banks, causal)
            experts(nc, A, h, banks, expert)


def _columns(np, *vectors):
    return np.stack([np.tile(v, P // v.shape[0]) for v in vectors], axis=1)


def _layouts(np, I):
    f = np.float32
    out = {}
    out["x_rows"] = I["x"].reshape(2 * SAMPLES, LEN)
    w1 = I["L0_tok_w1"]
    c1 = np.zeros((8, 8, 2, 8, 16), f)
    for b in range(8):
        c1[0:3, b, :, b, :] = w1.transpose(2, 1, 0)
    out["c1_w"] = c1.reshape(P, P)
    w2 = I["L0_tok_w2"]
    c2 = np.zeros((3, 2, 16, 2, 64), f)
    for b in range(2):
        c2[:, b, :, b, :] = w2.transpose(2, 1, 0)
    out["c2_w"] = c2.reshape(96, P)
    c3 = np.zeros((2, D, 2, 4, P), f)
    for b in range(2):
        c3[b, :, b] = I["L0_tok_w3"].transpose(1, 2, 0)
    out["c3_w"] = c3.reshape(P, 2, 4, P)
    out["norm_cols"] = np.stack([_columns(np, *(I[f"L0_tok_{v}{m}"] for v in ("b", "g", "be", "m", "v")))
                                 for m in (1, 2, 3)], axis=2)

    def two_blocks(w, width, step):
        o = np.zeros((P, width), f)
        o[0:64, 0:w.shape[1]] = w
        o[64:128, step:step + w.shape[1]] = w
        return o

    out["tok_wq"] = two_blocks(I["L0_tok_wq"].T, P, 32)
    wk = np.zeros((2, D, 2, P), f)
    bqk = np.zeros((P, 3), f)
    for b in range(2):
        rows = slice(32 * b, 32 * b + 8)
        wk[b, :, b, rows] = I["L0_tok_wk"].T
        bqk[rows, 0] = I["L0_tok_bq"]
        bqk[rows, 1 + b] = I["L0_tok_bk"]
    out["tok_wk"] = wk.reshape(P, 2, P)
    out["tok_bqk"] = bqk
    out["tok_wv"] = two_blocks(I["L0_tok_wv"].T, P, 64)
    out["tok_bv"] = np.broadcast_to(np.tile(I["L0_tok_bv"], 2), (P, P))
    out["gamma"] = np.broadcast_to(np.reshape(I["L0_tok_gamma"], (1, 1)), (P, 1))
    out["ident"] = np.eye(P, dtype=f)

    wqv = I["L0_attn_wqv_w"]
    q = wqv[0:HEADS * D].reshape(HEADS, D, D).transpose(2, 0, 1)
    wq = np.zeros((2, D, HEADS, 2, D), f)
    fan = np.zeros((2, D, 2, D), f)
    for b in range(2):
        wq[b, :, :, b, :] = q
        fan[b, :, b, :] = I["L0_attn_fanin_w"].T
    out["l1_wq"] = wq.reshape(P, HEADS, P)
    out["l1_wv"] = np.tile(wqv[HEADS * D:].T, (2, 1))
    out["l1_bv"] = np.broadcast_to(I["L0_attn_wqv_b"][HEADS * D:], (P, 2 * HEADS * D))
    out["l1_bq"] = np.tile(I["L0_attn_wqv_b"][0:HEADS * D].reshape(HEADS, D).T, (2, 1))
    out["wk_rows"] = np.broadcast_to(I["L0_attn_wk"].reshape(HEADS * D), (P, HEADS * D))
    out["wk_cols"] = np.tile(I["L0_attn_wk"].T, (2, 1))
    out["fan_w"] = fan.reshape(P, P)
    out["fan_b"] = np.broadcast_to(np.tile(I["L0_attn_fanin_b"], 2), (P, P))
    out["own_key"] = (np.arange(P)[:, None] // ROWS == np.arange(KEYS)[None, :]).astype(f)

    wi = np.zeros((2, D, 2, HID), f)
    for b in range(2):
        wi[b, :, b] = I["L0_ffn_Wi"].T
    out["rt_wi"] = wi.reshape(P, 2, HID)
    out["rt_bi"] = I["L0_ffn_bi"][:, None]
    out["rt_wr"] = np.concatenate([I["L0_ffn_Wr"].transpose(3, 0, 1, 2), I["L0_ffn_br"].transpose(2, 0, 1)[..., None]], axis=3)
    out["rt_ws"] = np.concatenate([I["L0_ffn_Ws"][:, 0].transpose(2, 0, 1), I["L0_ffn_bs"][:, 0].T[..., None]], axis=2)
    out["rt_wo"] = I["L0_ffn_Wo"].T
    out["rt_bo"] = np.broadcast_to(I["L0_ffn_bo"], (P, D))
    out["route_id"] = I["L0_ffn_route_id"].reshape(1, PAIRS)
    out["ca_wqk"] = np.tile(np.stack([I["L1_attn_Wq"], I["L1_attn_Wk"]], axis=1), (2, 1, 1))
    out["ca_wv"] = np.tile(I["L1_attn_Wv"], (2, 1))
    out["ca_wu"] = I["L1_attn_Wu"].reshape(HEADS // 2, P, D).transpose(1, 0, 2)
    out["ca_bqk"] = np.stack([I["L1_attn_bq"], I["L1_attn_bk"]]).reshape(2, HEADS // 2, P).transpose(2, 0, 1)
    out["ca_bv"] = np.broadcast_to(I["L1_attn_bv"], (P, HEADS * D))
    out["ca_bu"] = np.concatenate([I["L1_attn_bu"], np.zeros(D, f)])[:, None]
    out["mask"] = np.triu(np.full((P, TOK), MASKED, f))
    out["later"] = (np.arange(P) > 0).astype(f)[:, None]
    w1 = I["L1_ffn_w1"].reshape(EXPERTS // 2, 2, D, D)
    out["ex_rw"] = two_blocks(I["L1_ffn_router_w"].T, 2 * EXPERTS, EXPERTS)
    ex1 = np.zeros((2, D, EP, 2, P), f)
    for b in range(2):
        ex1[b, :, :, b, :] = w1.transpose(2, 0, 1, 3).reshape(D, EP, P)
    out["ex_w1"] = ex1.reshape(P, EP, 2, P)
    out["ex_w2"] = I["L1_ffn_w2"].reshape(EXPERTS // 2, P, D).transpose(1, 0, 2)
    out["ex_b1"] = I["L1_ffn_b1"].reshape(EXPERTS // 2, P).T
    b2 = np.zeros((ET, EXPERTS, ET, D), f)
    for n in range(ET):
        b2[n, :, n, :] = I["L1_ffn_b2"]
    out["ex_b2"] = b2.reshape(P, 2, HALF * D)
    sel = np.zeros((4, 4, EXPERTS, 4, EP, 2, D), f)
    for c in range(4):
        for e in range(EXPERTS):
            sel[c, 0:3, e, c, e // 2, e % 2, :] = 1.0
    out["ex_select"] = sel.reshape(P, 4, EP, P)
    out["earlier"] = np.broadcast_to(np.tril(np.ones((EXPERTS, EXPERTS), f), -1).reshape(EXPERTS ** 2), (P, EXPERTS ** 2))
    return {n: np.ascontiguousarray(a) for n, a in out.items()}


def kernel(**inputs):
    import numpy as _np
    import concourse.bacc as _bacc
    from concourse import mybir as _mybir
    from concourse.bass_utils import run_bass_kernel_spmd as _run

    nc = _bacc.Bacc("TRN2", target_bir_lowering=False, num_devices=1)
    laid = _layouts(_np, {n: _np.asarray(a) for n, a in inputs.items()})
    arrays, aps = {}, {}
    for name, a in laid.items():
        arrays[f"in_{name}_dram"] = a
        aps[name] = nc.dram_tensor(f"in_{name}_dram", a.shape, _mybir.dt.from_np(a.dtype), kind="ExternalInput").ap()
    aps["out"] = nc.dram_tensor("out_dram", (SAMPLES, TOK, D), _mybir.dt.float32, kind="ExternalOutput").ap()
    build(nc, named(**aps))
    r = _run(nc, [arrays], core_ids=[0])
    return r.results[0]["out_dram"]
```
